# Optimizing a Trainium2 kernel written in Bass

```python
import numpy as np
import jax
import jax.numpy as jnp

def _softmax(x, axis=-1):
    return jax.nn.softmax(x, axis=axis)

def _gelu(x):
    return jax.nn.gelu(x, approximate=True)

def _silu(x):
    return jax.nn.silu(x)

def _sigmoid(x):
    return jax.nn.sigmoid(x)

def _layernorm(x, axis=-1, eps=1e-05):
    m = jnp.mean(x, axis=axis, keepdims=True)
    v = jnp.var(x, axis=axis, keepdims=True)
    return (x - m) / jnp.sqrt(v + eps)

def _scatter_add(tgt, idx, src, axis=0):
    return tgt.at[idx].add(src)

def _segment_sum(src, seg, n):
    return jax.ops.segment_sum(src, seg, n)
kernel_name = 'mk_flamingo_gated_d2_seqx_r4_38b509'

def setup_inputs(seed: int=0):
    np.random.seed(seed)
    _w = jnp.asarray

    def _rec_inputs():
        import jax
        import jax.numpy as jnp
        _rk = jax.random.key(seed)
        x = 7.22e-05 + 1 * jax.random.normal(jax.random.fold_in(_rk, 1), (4, 1024, 256), jnp.float32)
        _lenS = 1024 - jax.random.randint(jax.random.fold_in(_rk, 7), (4,), 0, max(1, 1024 // 4) + 1, jnp.int32)
        _lenS2 = 77 - jax.random.randint(jax.random.fold_in(_rk, 8), (4,), 0, max(1, 77 // 4) + 1, jnp.int32)
        _ctx_1024P = jax.random.normal(jax.random.fold_in(_rk, 11), (4, 16, 256), jnp.float32)
        _ctx_1024c = jax.random.dirichlet(jax.random.fold_in(_rk, 511), 0.3 * jnp.ones((16,), jnp.float32), (4, 77))
        _ctx_1024t = jnp.einsum('bsk,bkd->bsd', _ctx_1024c, _ctx_1024P)
        _ctx_1024t = _ctx_1024t * jax.lax.rsqrt(jnp.mean(jnp.square(_ctx_1024t)) + 1e-12) * 0.953939
        ctx_1024 = 4.13588e-05 + 0.999923 * (_ctx_1024t + 0.3 * jax.random.normal(jax.random.fold_in(_rk, 611), (4, 77, 256), jnp.float32))
        _g = jax.random.normal(jax.random.fold_in(_rk, 9001), (2, 2), jnp.float32)
        _g = jnp.sign(_g) * jnp.maximum(jnp.abs(_g), 1.0) + (_g == 0) * 1.0
        g_xattn = _g[0]
        g_ffn = _g[1]
        return (x, ctx_1024, g_xattn, g_ffn)
    x, ctx_1024, g_xattn, g_ffn = _rec_inputs()

    def _L0_xattn_setup():
        import jax, jax.numpy as jnp
        import numpy as np
        B, SQ, SKV = (4, 512, 512)
        INPUT_DIM, EMBED_DIM, NUM_HEADS = (256, 256, 16)
        HEAD_DIM = EMBED_DIM // NUM_HEADS
        key = jax.random.key(seed)
        kq, kc, kwkv, kwo = jax.random.split(key, 4)

        def xavier(k, shape):
            fan_in, fan_out = shape
            lim = jnp.sqrt(6.0 / (fan_in + fan_out))
            return jax.random.uniform(k, shape, jnp.float32, -lim, lim)
        return {'q': jax.random.normal(kq, (B, SQ, EMBED_DIM), jnp.float32), 'c': jax.random.normal(kc, (B, SKV, INPUT_DIM), jnp.float32), 'W_kv': xavier(kwkv, (INPUT_DIM, 2 * EMBED_DIM)), 'b_kv': jnp.zeros((2 * EMBED_DIM,), jnp.float32), 'W_o': xavier(kwo, (EMBED_DIM, EMBED_DIM)), 'b_o': jnp.zeros((EMBED_DIM,), jnp.float32)}
    _L0_xattn_all = _L0_xattn_setup()
    _L0_xattn_in = {k: v for k, v in _L0_xattn_all.items() if k in ('W_kv', 'b_kv', 'W_o', 'b_o')}
    del _L0_xattn_all

    def _L0_ffn_setup():
        import jax, jax.numpy as jnp
        import numpy as np
        D_MODEL = 256
        D_FF = 1024
        NUM_EXPERTS = 8
        TOP_K = 2
        key = jax.random.key(seed)
        ks = jax.random.split(key, 8)
        s_in = 1.0 / np.sqrt(D_MODEL)
        s_ff = 1.0 / np.sqrt(D_FF)
        x = jax.random.normal(ks[0], (2, 512, D_MODEL), dtype=jnp.float32)
        Wg = jax.random.uniform(ks[1], (D_MODEL, NUM_EXPERTS), minval=-s_in, maxval=s_in, dtype=jnp.float32)
        bg = jax.random.uniform(ks[2], (NUM_EXPERTS,), minval=-s_in, maxval=s_in, dtype=jnp.float32)
        W1 = jax.random.uniform(ks[3], (NUM_EXPERTS, D_MODEL, D_FF), minval=-s_in, maxval=s_in, dtype=jnp.float32)
        b1 = jax.random.uniform(ks[4], (NUM_EXPERTS, D_FF), minval=-s_in, maxval=s_in, dtype=jnp.float32)
        W2 = jax.random.uniform(ks[5], (NUM_EXPERTS, D_FF, D_MODEL), minval=-s_ff, maxval=s_ff, dtype=jnp.float32)
        b2 = jax.random.uniform(ks[6], (NUM_EXPERTS, D_MODEL), minval=-s_ff, maxval=s_ff, dtype=jnp.float32)
        return {'x': x, 'Wg': Wg, 'bg': bg, 'W1': W1, 'b1': b1, 'W2': W2, 'b2': b2}
    _L0_ffn_all = _L0_ffn_setup()
    _L0_ffn_in = {k: v for k, v in _L0_ffn_all.items() if k in ('Wg', 'bg', 'W1', 'b1', 'W2', 'b2')}
    del _L0_ffn_all

    def _L1_xattn_setup():
        import jax, jax.numpy as jnp
        import numpy as np
        DIM = 256
        NUM_HEADS = 16
        DIM_HEAD = 64
        INNER = NUM_HEADS * DIM_HEAD
        SCALE = DIM_HEAD ** (-0.5)

        def _layernorm(x, gamma, beta, eps=1e-05):
            mu = jnp.mean(x, axis=-1, keepdims=True)
            var = jnp.mean(jnp.square(x - mu), axis=-1, keepdims=True)
            return (x - mu) * jax.lax.rsqrt(var + eps) * gamma + beta
        key = jax.random.key(seed)
        ks = jax.random.split(key, 8)
        B, SQ, SK = (2, 512, 1024)
        x = jax.random.normal(ks[0], (B, SQ, DIM), dtype=jnp.float32)
        context = jax.random.normal(ks[1], (B, SK, DIM), dtype=jnp.float32)
        ln_gamma = jnp.ones((DIM,), jnp.float32)
        ln_beta = jnp.zeros((DIM,), jnp.float32)
        w_q = jax.random.normal(ks[2], (DIM, INNER), dtype=jnp.float32) / np.sqrt(DIM)
        w_kv = jax.random.normal(ks[3], (DIM, 2 * INNER), dtype=jnp.float32) / np.sqrt(DIM)
        w_out = jax.random.normal(ks[4], (INNER, DIM), dtype=jnp.float32) / np.sqrt(INNER)
        b_out = jnp.zeros((DIM,), jnp.float32)
        gate = jnp.array([0.5], jnp.float32)
        return {'x': x, 'context': context, 'ln_gamma': ln_gamma, 'ln_beta': ln_beta, 'w_q': w_q, 'w_kv': w_kv, 'w_out': w_out, 'b_out': b_out, 'gate': gate}
    _L1_xattn_all = _L1_xattn_setup()
    _L1_xattn_in = {k: v for k, v in _L1_xattn_all.items() if k in ('ln_gamma', 'ln_beta', 'w_q', 'w_kv', 'w_out', 'b_out', 'gate')}
    del _L1_xattn_all

    def _L1_ffn_setup():
        import jax, jax.numpy as jnp
        import numpy as np
        D_MODEL, D_FF, RANK = (256, 1024, 64)
        B, S = (4, 1024)
        key = jax.random.key(seed)
        ks = jax.random.split(key, 7)
        return {'x': jax.random.normal(ks[0], (B, S, D_MODEL), dtype=jnp.float32), 'U1': jax.random.normal(ks[1], (D_MODEL, RANK), dtype=jnp.float32) * 0.02, 'V1': jax.random.normal(ks[2], (RANK, D_FF), dtype=jnp.float32) * 0.02, 'b1': jnp.zeros((D_FF,), dtype=jnp.float32), 'U2': jax.random.normal(ks[3], (D_FF, RANK), dtype=jnp.float32) * 0.02, 'V2': jax.random.normal(ks[4], (RANK, D_MODEL), dtype=jnp.float32) * 0.02, 'b2': jnp.zeros((D_MODEL,), dtype=jnp.float32)}
    _L1_ffn_all = _L1_ffn_setup()
    _L1_ffn_in = {k: v for k, v in _L1_ffn_all.items() if k in ('U1', 'V1', 'b1', 'U2', 'V2', 'b2')}
    del _L1_ffn_all
    return {'x': x, 'ctx_1024': ctx_1024, 'g_xattn': g_xattn, 'g_ffn': g_ffn, 'L0_xattn_W_kv': _L0_xattn_in['W_kv'], 'L0_xattn_b_kv': _L0_xattn_in['b_kv'], 'L0_xattn_W_o': _L0_xattn_in['W_o'], 'L0_xattn_b_o': _L0_xattn_in['b_o'], 'L0_ffn_Wg': _L0_ffn_in['Wg'], 'L0_ffn_bg': _L0_ffn_in['bg'], 'L0_ffn_W1': _L0_ffn_in['W1'], 'L0_ffn_b1': _L0_ffn_in['b1'], 'L0_ffn_W2': _L0_ffn_in['W2'], 'L0_ffn_b2': _L0_ffn_in['b2'], 'L1_xattn_ln_gamma': _L1_xattn_in['ln_gamma'], 'L1_xattn_ln_beta': _L1_xattn_in['ln_beta'], 'L1_xattn_w_q': _L1_xattn_in['w_q'], 'L1_xattn_w_kv': _L1_xattn_in['w_kv'], 'L1_xattn_w_out': _L1_xattn_in['w_out'], 'L1_xattn_b_out': _L1_xattn_in['b_out'], 'L1_xattn_gate': _L1_xattn_in['gate'], 'L1_ffn_U1': _L1_ffn_in['U1'], 'L1_ffn_V1': _L1_ffn_in['V1'], 'L1_ffn_b1': _L1_ffn_in['b1'], 'L1_ffn_U2': _L1_ffn_in['U2'], 'L1_ffn_V2': _L1_ffn_in['V2'], 'L1_ffn_b2': _L1_ffn_in['b2']}

def reference(x, ctx_1024, g_xattn, g_ffn, L0_xattn_W_kv, L0_xattn_b_kv, L0_xattn_W_o, L0_xattn_b_o, L0_ffn_Wg, L0_ffn_bg, L0_ffn_W1, L0_ffn_b1, L0_ffn_W2, L0_ffn_b2, L1_xattn_ln_gamma, L1_xattn_ln_beta, L1_xattn_w_q, L1_xattn_w_kv, L1_xattn_w_out, L1_xattn_b_out, L1_xattn_gate, L1_ffn_U1, L1_ffn_V1, L1_ffn_b1, L1_ffn_U2, L1_ffn_V2, L1_ffn_b2):
    import jax
    import jax.numpy as jnp

    def _L0_xattn_ref(q, c, W_kv, b_kv, W_o, b_o):
        import jax, jax.numpy as jnp
        import numpy as np
        B, SQ, SKV = (4, 512, 512)
        INPUT_DIM, EMBED_DIM, NUM_HEADS = (256, 256, 16)
        HEAD_DIM = EMBED_DIM // NUM_HEADS
        Bc, Skv, _ = c.shape
        Bq, Sq, embed_dim = q.shape
        kv = c @ W_kv + b_kv
        kv = kv.reshape(Bc, Skv, NUM_HEADS, 2 * HEAD_DIM).transpose(0, 2, 1, 3)
        k, v = jnp.split(kv, 2, axis=-1)
        qh = q.reshape(Bq, Sq, NUM_HEADS, HEAD_DIM).transpose(0, 2, 1, 3)
        scale = 1.0 / jnp.sqrt(jnp.asarray(HEAD_DIM, q.dtype))
        logits = jnp.einsum('bhqd,bhkd->bhqk', qh, k) * scale
        attn = jax.nn.softmax(logits, axis=-1)
        values = jnp.einsum('bhqk,bhkd->bhqd', attn, v)
        values = values.transpose(0, 2, 1, 3).reshape(Bc, Sq, embed_dim)
        out = values @ W_o + b_o
        return out

    def _L0_ffn_ref(x, Wg, bg, W1, b1, W2, b2):
        import jax, jax.numpy as jnp
        import numpy as np
        D_MODEL = 256
        D_FF = 1024
        NUM_EXPERTS = 8
        TOP_K = 2
        gate_logits = jnp.einsum('bsd,de->bse', x, Wg) + bg
        gate_probs = jax.nn.softmax(gate_logits, axis=-1)
        topk_probs, topk_idx = jax.lax.top_k(gate_probs, TOP_K)
        topk_probs = topk_probs / jnp.sum(topk_probs, axis=-1, keepdims=True)
        onehot = jax.nn.one_hot(topk_idx, NUM_EXPERTS, dtype=x.dtype)
        weights = jnp.einsum('bske,bsk->bse', onehot, topk_probs)
        h = jnp.einsum('bsd,edf->bsef', x, W1) + b1
        h = jax.nn.gelu(h, approximate=False)
        y = jnp.einsum('bsef,efd->bsed', h, W2) + b2
        return jnp.einsum('bsed,bse->bsd', y, weights)

    def _L1_xattn_ref(x, context, ln_gamma, ln_beta, w_q, w_kv, w_out, b_out, gate):
        import jax, jax.numpy as jnp
        import numpy as np
        DIM = 256
        NUM_HEADS = 16
        DIM_HEAD = 64
        INNER = NUM_HEADS * DIM_HEAD
        SCALE = DIM_HEAD ** (-0.5)

        def _layernorm(x, gamma, beta, eps=1e-05):
            mu = jnp.mean(x, axis=-1, keepdims=True)
            var = jnp.mean(jnp.square(x - mu), axis=-1, keepdims=True)
            return (x - mu) * jax.lax.rsqrt(var + eps) * gamma + beta
        B, SQ, _ = x.shape
        SK = context.shape[1]
        xn = _layernorm(x, ln_gamma, ln_beta)
        q = (xn @ w_q).reshape(B, SQ, NUM_HEADS, DIM_HEAD)
        kv = context @ w_kv
        k, v = jnp.split(kv, 2, axis=-1)
        k = k.reshape(B, SK, NUM_HEADS, DIM_HEAD)
        v = v.reshape(B, SK, NUM_HEADS, DIM_HEAD)
        scores = jnp.einsum('bqhd,bkhd->bhqk', q * SCALE, k)
        attn = jax.nn.softmax(scores, axis=-1)
        out = jnp.einsum('bhqk,bkhd->bqhd', attn, v).reshape(B, SQ, INNER)
        out = out @ w_out + b_out
        return out * jnp.tanh(gate[0])

    def _L1_ffn_ref(x, U1, V1, b1, U2, V2, b2):
        import jax, jax.numpy as jnp
        import numpy as np
        D_MODEL, D_FF, RANK = (256, 1024, 64)
        B, S = (4, 1024)
        P = jnp.einsum('bsd,dr->bsr', x, U1)
        H = jax.nn.gelu(jnp.einsum('bsr,rf->bsf', P, V1) + b1)
        Q = jnp.einsum('bsf,fr->bsr', H, U2)
        return jnp.einsum('bsr,rd->bsd', Q, V2) + b2
    x = x + jnp.tanh(g_xattn[0]) * _L0_xattn_ref(_layernorm(x, axis=-1), ctx_1024, L0_xattn_W_kv, L0_xattn_b_kv, L0_xattn_W_o, L0_xattn_b_o)
    x = x + jnp.tanh(g_ffn[0]) * _L0_ffn_ref(_layernorm(x, axis=-1), L0_ffn_Wg, L0_ffn_bg, L0_ffn_W1, L0_ffn_b1, L0_ffn_W2, L0_ffn_b2)
    x = x + jnp.tanh(g_xattn[1]) * _L1_xattn_ref(_layernorm(x, axis=-1), ctx_1024, L1_xattn_ln_gamma, L1_xattn_ln_beta, L1_xattn_w_q, L1_xattn_w_kv, L1_xattn_w_out, L1_xattn_b_out, L1_xattn_gate)
    x = x + jnp.tanh(g_ffn[1]) * _L1_ffn_ref(_layernorm(x, axis=-1), L1_ffn_U1, L1_ffn_V1, L1_ffn_b1, L1_ffn_U2, L1_ffn_V2, L1_ffn_b2)
    return x

_drawn_inputs = setup_inputs


def setup_inputs(seed=0):
    import zlib

    import numpy as np

    out = dict(_drawn_inputs(seed))
    spreads = {'g_ffn': (-1.0, 0.6),
     'L0_xattn_b_kv': (0.0, 0.1),
     'L0_xattn_b_o': (0.0, 0.1),
     'L1_xattn_ln_gamma': (1.0, 0.6),
     'L1_xattn_ln_beta': (0.0, 0.8),
     'L1_xattn_b_out': (0.0, 0.1),
     'L1_ffn_b1': (0.0, 0.8),
     'L1_ffn_b2': (0.0, 0.8)}
    factors = {'L0_ffn_bg': 3.007,
     'L0_ffn_b1': 8.0,
     'L0_ffn_b2': 6.168,
     'L1_ffn_U1': 8.0,
     'L1_ffn_V1': 8.0,
     'L1_ffn_U2': 8.0,
     'L1_ffn_V2': 8.0}
    for name, (base, spread) in spreads.items():
        noise = np.random.default_rng([zlib.crc32(name.encode()), seed]).standard_normal(out[name].shape)
        drawn = base * np.exp(spread * noise) if base else spread * noise
        out[name] = jnp.asarray(drawn.astype(out[name].dtype))
    for name, factor in factors.items():
        out[name] = (out[name] * factor).astype(out[name].dtype)
    return out
```

```python
from contextlib import ExitStack

import concourse.bass as bass
from concourse import mybir

F32 = mybir.dt.float32
F16 = mybir.dt.float16
I32 = mybir.dt.int32
ALU = mybir.AluOpType
ACT = mybir.ActivationFunctionType
AX = mybir.AxisListType.X

P = 128
BANK = 512


def wait(eng, sem, value):
    if not (isinstance(value, int) and value <= 0):
        eng.wait_ge(sem, value)


def flamingo_kernel(nc, a, out, stop=99):
    B, SQ, D = a["x"].shape
    _, SK, _ = a["ctx_1024"].shape
    C = D // P
    TB = SQ // P
    T = B * TB
    H = 16
    HD0 = D // H
    INNER = a["L1_xattn_w_q"].shape[1]
    HD1 = INNER // H
    E, _, F = a["L0_ffn_W1"].shape
    FC = F // P
    HK = H * SK
    J = -(-HK // P)
    HKP = J * P
    KB = B * SK
    R = a["L1_ffn_U1"].shape[1]
    EPS = 1e-5
    NCOL = T * E
    TT = 2 * P
    NT = 2 * B * SQ // TT + E - 1
    NH = 2 * (NT + 2)
    HEADS_OF_BANK = [6, 6, 4]
    WS = 64.0
    AS = 16.0
    PS = 256.0

    ctx = ExitStack()
    with ctx:
        def sb(name, shape, dt=F32):
            return ctx.enter_context(nc.sbuf_tensor(name, shape, dt))

        def sem(name):
            return ctx.enter_context(nc.semaphore(name))

        def view(arena, word, shape, dt=F32):
            n = 1
            for s in shape:
                n *= s
            words = n if dt in (F32, I32) else n // 2
            v = arena[:, word:word + words]
            if dt != F32:
                v = v.bitcast(dt)
            if len(shape) == 2:
                v = v.rearrange("p (a b) -> p a b", a=shape[0])
            elif len(shape) == 3:
                v = v.rearrange("p (a b c) -> p a b c", a=shape[0], b=shape[1])
            elif len(shape) == 4:
                v = v.rearrange("p (a b c d) -> p a b c d", a=shape[0], b=shape[1], c=shape[2])
            return v

        x_res = sb("x_res", [P, T, D])
        region_a = sb("region_a", [P, 16384])
        region_b = sb("region_b", [P, 16384])
        work = sb("work", [P, 6750])
        ident = sb("ident", [P, P])
        ident16 = sb("ident16", [P, P], F16)
        b_row = sb("b_row", [P, D])
        gates = sb("gates", [P, 5])
        gtanh = sb("gtanh", [P, 5])
        gscale = sb("gscale", [P, 4])
        small = sb("small", [P, 48])
        mv = sb("mv", [P, 2, 2])
        bst = sb("bst", [P, 2, 6])
        rstd = sb("rstd", [P, 2, 2])
        smax = sb("smax", [P, 2, H])
        ssum = sb("ssum", [P, 2, H])
        srec = sb("srec", [P, 2, H])
        slot_token = sb("slot_token", [P, NH], I32)
        tile_expert = sb("tile_expert", [1, NT], I32)
        pos = sb("pos", [P, 2, T], I32)
        topw = sb("topw", [P, 2, T])
        idx_now = sb("idx_now", [P, 2], I32)
        idx_ring = sb("idx_ring", [P, 2, 2], I32)
        b1_cols = sb("b1_cols", [P, E, FC])
        half = small[:, 0:1]
        eps = small[:, 1:2]
        eps2 = small[:, 2:3]

        banks = ctx.enter_context(nc.psum_tensor("banks", [P, 8, BANK], F32))

        xs = nc.dram_tensor("xs", (B * SQ, 2 * D), F16, kind="Internal").ap()
        ys = nc.dram_tensor("ys", (NT * TT, D), F32, kind="Internal").ap()

        def hk_banks(ap):
            return [(12, ap[:, 0:2, 0:6 * SK].rearrange("p b (h k) -> p b h k", h=6), 0),
                    (4, ap[:, 2, 0:4 * SK].rearrange("p (h k) -> p h k", h=4), 12)]

        G0 = view(region_b, 0, [2, B, C, (H // C) * SK], F16)
        vw_word = B * C * (H // C) * SK
        VW = view(region_b, vw_word, [2, B, J, D], F16)
        ctx_sb = view(region_a, 0, [B, D])
        wkv0 = view(region_a, 1024, [C, 2 * D])
        wo0 = view(region_a, 2048, [C, D])
        ctxT = view(region_a, 2560, [C, KB])
        kT0 = view(region_a, 3200, [2, C, KB], F16)
        vT0 = view(region_a, 4500, [C, KB])
        W0 = (H // C) * SK
        VB0 = view(region_a, 5200, [P + 2 * (W0 + P)])
        bkv = view(region_a, 7000, [2 * D])
        ones = view(region_a, 7600, [KB])
        wkv0s = view(region_a, 8100, [C, 2, D])
        bkvs = view(region_a, 9200, [2, D])
        mask = view(region_a, 8000, [H // C])
        mask16 = view(region_a, 8010, [H // C], F16)
        S = view(work, 0, [2, HKP])
        PT = view(work, 2 * HKP, [2, 2, J, P], F16)
        xnb = view(work, 4 * HKP, [2, D])
        xT = view(work, 4 * HKP + 2 * D, [2, 2, C, P], F16)

        s_c = sem("consts")
        s_x = sem("x_loaded")
        s_w = sem("setup_weights_loaded")
        s_ws = sem("kv_weights_sorted")
        s_ct = sem("ctx_transposed")
        s_ctc = sem("ctx_transpose_copied")
        s_kv = sem("kv_projected")
        s_kh = sem("k_hi")
        s_kl = sem("kv_copied")
        s_vb = sem("v_spread")
        s_g0 = sem("k_spread_hi")
        s_g0l = sem("k_spread_lo")
        s_vw = sem("vw_done")
        s_vh = sem("vw_hi")
        s_vl = sem("vw_lo")
        s_gt = sem("gates_tanh")
        s_gs = sem("gates_scaled")
        VGROUPS = [(0, 4), (4, 8), (8, J)]

        def vw_chunks(width, n, j):
            return [(k, P + k * (width + P) + P * j - k * width) for k in range(n)
                    if P * j + P > k * width and P * j < (k + 1) * width]

        def vw_product(pe, b, vb, width, n, w_out, before):
            for g, (j0, j1) in enumerate(VGROUPS):
                at = len(VGROUPS) * b + g
                wait(pe, s_vl if before else s_vl, vw_base[0] + at - 1)
                wait(pe, s_vh, vw_base[0] + at - 1)
                for j in range(j0, j1):
                    parts = vw_chunks(width, n, j)
                    o = banks[:, 4 + 2 * (at % 2) + (j - j0) // 2, (j - j0) % 2 * D:(j - j0) % 2 * D + D]
                    for i, (k, start) in enumerate(parts):
                        last = nc.tensor.matmul(o, vb[:, start:start + P], w_out[:, k, :],
                                                start=(i == 0), stop=(i == len(parts) - 1))
                last.then_inc(s_vw, 1)

        def vw_hi(act, b):
            for g, (j0, j1) in enumerate(VGROUPS):
                at = len(VGROUPS) * b + g
                act.wait_ge(s_vw, vw_base[0] + at + 1)
                src = banks[:, 4 + 2 * (at % 2):4 + 2 * (at % 2) + (j1 - j0) // 2, :]
                nc.scalar.activation(VW[:, 0, b, j0:j1, :].rearrange("p (a b) n -> p a (b n)", b=2), src,
                                     ACT.Copy, scale=AS).then_inc(s_vh, 1)

        def vw_lo(dve, b):
            for g, (j0, j1) in enumerate(VGROUPS):
                at = len(VGROUPS) * b + g
                dve.wait_ge(s_vh, vw_base[0] + at + 1)
                src = banks[:, 4 + 2 * (at % 2):4 + 2 * (at % 2) + (j1 - j0) // 2, :]
                nc.vector.scalar_tensor_tensor(
                    out=VW[:, 1, b, j0:j1, :].rearrange("p (a b) n -> p a (b n)", b=2), in0=src, scalar=AS,
                    in1=VW[:, 0, b, j0:j1, :].rearrange("p (a b) n -> p a (b n)", b=2),
                    op0=ALU.mult, op1=ALU.subtract).then_inc(s_vl, 1)

        vw_base = [0]

        with nc.Block() as block:
            @block.sync
            def _(sp):
                sp.dma_start(ctx_sb[0:SK], a["ctx_1024"].rearrange("b k d -> k b d")).then_inc(s_w, 16)
                sp.dma_start(wkv0, a["L0_xattn_W_kv"].rearrange("(c p) n -> p c n", p=P)).then_inc(s_w, 16)
                sp.dma_start(wo0, a["L0_xattn_W_o"].rearrange("(c p) n -> p c n", p=P)).then_inc(s_w, 16)
                sp.dma_start(bkv[0:1], a["L0_xattn_b_kv"].rearrange("(a n) -> a n", a=1)).then_inc(s_w, 16)
                sp.dma_start(b_row[:], a["L0_xattn_b_o"].rearrange("(a n) -> a n", a=1).to_broadcast([P, D])).then_inc(s_w, 16)
                for lo, name in ((0, "g_xattn"), (2, "g_ffn"), (4, "L1_xattn_gate")):
                    n = a[name].shape[0]
                    sp.dma_start(gates[:, lo:lo + n], a[name].rearrange("(a n) -> a n", a=1).to_broadcast([P, n])).then_inc(s_w, 16)
                for b in range(B):
                    sp.dma_start(x_res[:, b * TB:(b + 1) * TB, :],
                                 a["x"][b].rearrange("(t p) d -> p t d", p=P)).then_inc(s_x, 16)

            @block.gpsimd
            def _(pool):
                nc.gpsimd.memset(ident[:], 0.0).then_inc(s_c, 1)
                nc.gpsimd.memset(mask, 1.0).then_inc(s_c, 1)
                nc.gpsimd.memset(ones, 1.0).then_inc(s_c, 1)
                nc.gpsimd.memset(VB0, 0.0).then_inc(s_c, 1)
                nc.gpsimd.memset(S[:, :, HK:HKP], 0.0).then_inc(s_c, 1)
                nc.gpsimd.memset(half, -0.5).then_inc(s_c, 1)
                nc.gpsimd.memset(eps, EPS).then_inc(s_c, 1)
                nc.gpsimd.memset(eps2, EPS * EPS / (1.0 + EPS)).then_inc(s_c, 1)
                pool.wait_ge(s_c, 8)
                nc.gpsimd.affine_select(out=ident[:], in_=ident[:], compare_op=ALU.not_equal, fill=1.0, base=0,
                                        pattern=[[-1, P]], channel_multiplier=1).then_inc(s_c, 1)
                nc.gpsimd.affine_select(out=mask, in_=mask, compare_op=ALU.is_ge, fill=0.0, base=0,
                                        pattern=[[-HD0, H // C]], channel_multiplier=1).then_inc(s_c, 1)
                pool.wait_ge(s_c, 10)
                nc.gpsimd.affine_select(out=mask, in_=mask, compare_op=ALU.is_ge, fill=0.0, base=HD0 - 1,
                                        pattern=[[HD0, H // C]], channel_multiplier=-1).then_inc(s_c, 1)
                nc.gpsimd.tensor_copy(ident16[:], ident[:]).then_inc(s_c, 1)
                pool.wait_ge(s_c, 12)
                nc.gpsimd.tensor_copy(mask16, mask).then_inc(s_c, 1)
                pool.wait_ge(s_c, 13)
                pool.wait_ge(s_kh, 1)
                for b in range(B):
                    for c in range(C):
                        nc.gpsimd.tensor_tensor(
                            G0[:, 0, b, c, :].rearrange("p (h k) -> p h k", k=SK),
                            kT0[:, 0, c, b * SK:(b + 1) * SK].unsqueeze(1).to_broadcast([P, H // C, SK]),
                            mask16.unsqueeze(2).to_broadcast([P, H // C, SK]), ALU.mult).then_inc(s_g0, 1)

            @block.scalar
            def _(act):
                act.wait_ge(s_w, 8 * 16)
                nc.scalar.activation(gtanh[:], gates[:], ACT.Tanh).then_inc(s_gt, 1)
                act.wait_ge(s_ct, 1)
                nc.scalar.copy(ctxT, banks[:, 0:2, 0:KB]).then_inc(s_ctc, 1)
                act.wait_ge(s_kv, 1)
                nc.scalar.activation(kT0[:, 0], banks[:, 0:2, 0:KB], ACT.Copy, scale=AS).then_inc(s_kh, 1)
                nc.scalar.copy(vT0, banks[:, 2:4, 0:KB]).then_inc(s_kl, 1)
                for b in range(B):
                    vw_hi(act, b)

            @block.tensor
            def _(pe):
                pe.wait_ge(s_w, 8 * 16)
                pe.wait_ge(s_c, 9)
                for c in range(C):
                    for b in range(B):
                        last = nc.tensor.transpose(banks[:, c, b * SK:(b + 1) * SK],
                                                   ctx_sb[0:SK, b, c * P:(c + 1) * P], ident[0:SK, 0:SK])
                last.then_inc(s_ct, 1)
                pe.wait_ge(s_ctc, 1)
                pe.wait_ge(s_ws, C + 1)
                for s in range(2):
                    for g in range(C):
                        o = banks[:, 2 * s + g, 0:KB]
                        for c in range(C):
                            nc.tensor.matmul(o, wkv0s[:, c, s, g * P:(g + 1) * P], ctxT[:, c, :], start=(c == 0), stop=False)
                        last = nc.tensor.matmul(o, bkvs[0:1, s, g * P:(g + 1) * P], ones[0:1, :], start=False, stop=True)
                last.then_inc(s_kv, 1)
                for b in range(B):
                    pe.wait_ge(s_vb, C * (b + 1))
                    vw_product(pe, b, VB0, W0, C, wo0, None)

            @block.vector
            def _(dve):
                dve.wait_ge(s_w, 8 * 16)
                for c in range(C):
                    nc.vector.tensor_copy(wkv0s[:, c].rearrange("p s (h d) -> p s h d", d=HD0),
                                          wkv0[:, c].rearrange("p (h s d) -> p s h d", s=2, d=HD0)).then_inc(s_ws, 1)
                nc.vector.tensor_copy(bkvs[0:1].rearrange("p s (h d) -> p s h d", d=HD0),
                                      bkv[0:1].rearrange("p (h s d) -> p s h d", s=2, d=HD0)).then_inc(s_ws, 1)
                dve.wait_ge(s_gt, 1)
                nc.vector.tensor_scalar(gscale[:, 0:1], gtanh[:, 0:1], 1.0 / (AS * PS), None, ALU.mult).then_inc(s_gs, 1)
                nc.vector.tensor_copy(gscale[:, 1:2], gtanh[:, 2:3]).then_inc(s_gs, 1)
                nc.vector.tensor_scalar(gscale[:, 2:3], gtanh[:, 1:2], gtanh[:, 4:5], 1.0 / (AS * PS), ALU.mult, ALU.mult).then_inc(s_gs, 1)
                nc.vector.tensor_scalar(gscale[:, 3:4], gtanh[:, 3:4], 1.0 / (AS * AS), None, ALU.mult).then_inc(s_gs, 1)
                nc.vector.tensor_scalar(b_row[:], b_row[:], gtanh[:, 0:1], None, ALU.mult).then_inc(s_gs, 1)
                dve.wait_ge(s_kh, 1)
                dve.wait_ge(s_kl, 1)
                nc.vector.scalar_tensor_tensor(out=kT0[:, 1], in0=banks[:, 0:2, 0:KB], scalar=AS, in1=kT0[:, 0],
                                               op0=ALU.mult, op1=ALU.subtract).then_inc(s_kl, 1)
                dve.wait_ge(s_kl, 2)
                dve.wait_ge(s_c, 13)
                for b in range(B):
                    wait(dve, s_vw, len(VGROUPS) * b)
                    for c in range(C):
                        o = P + c * (W0 + P)
                        nc.vector.tensor_tensor(
                            VB0[:, o:o + W0].rearrange("p (h k) -> p h k", k=SK),
                            vT0[:, c, b * SK:(b + 1) * SK].unsqueeze(1).to_broadcast([P, H // C, SK]),
                            mask.unsqueeze(2).to_broadcast([P, H // C, SK]), ALU.mult).then_inc(s_vb, 1)
                    for c in range(C):
                        nc.vector.tensor_tensor(
                            G0[:, 1, b, c, :].rearrange("p (h k) -> p h k", k=SK),
                            kT0[:, 1, c, b * SK:(b + 1) * SK].unsqueeze(1).to_broadcast([P, H // C, SK]),
                            mask16.unsqueeze(2).to_broadcast([P, H // C, SK]), ALU.mult).then_inc(s_g0l, 1)
                    vw_lo(dve, b)

        def attention(name, pieces, Gof, layer, softmax_scale, ln_eps, affine, combine):
            stats_done = sem(name + "_stats")
            rstd_done = sem(name + "_rstd")
            xn_done = sem(name + "_xn")
            xin_done = sem(name + "_xn_ready")
            bias_done = sem(name + "_bias_added")
            tx_done = sem(name + "_x_transposed")
            xhi_done = sem(name + "_x_hi")
            xlo_done = sem(name + "_x_lo")
            sc_done = sem(name + "_scores")
            max_done = sem(name + "_max")
            sub_done = sem(name + "_sub")
            exp_done = sem(name + "_exp")
            sum_done = sem(name + "_sum")
            rec_done = sem(name + "_recip")
            nrm_done = sem(name + "_normalised")
            tp_done = sem(name + "_p_transposed")
            phi_done = sem(name + "_p_hi")
            plo_done = sem(name + "_p_lo")
            pv_done = sem(name + "_pv")
            epi_done = sem(name + "_residual")
            bn_done = sem(name + "_bn")
            eps_done = sem(name + "_eps")
            if combine:
                idx_done = sem(name + "_idx")
                got = [sem(name + "_rows_0"), sem(name + "_rows_1")]
                comb_a = sem(name + "_first_expert_added")
                comb_done = sem(name + "_experts_added")
            pX = banks[:, 0, 0:C * P].rearrange("p (c n) -> p c n", c=C)
            pS = banks[:, 1:4, :]
            pT = banks[:, 4:7, :].rearrange("p a b -> p (a b)")[:, 0:HKP]
            pO = banks[:, 7, 0:D]
            per = 2 if affine else 1

            def tile(t):
                return x_res[:, bass.ds(t, 1), :].rearrange("p a d -> p (a d)")

            FIRST, LAST = -4, T + 1
            LO, HI = 2, T - 4

            def ok(t):
                return not isinstance(t, int) or 0 <= t < T

            def drive(eng, step):
                for s in range(FIRST, LO):
                    step(s, s % 2)
                with eng.Fori(0, (HI - LO) // 2) as i:
                    for k in range(2):
                        step(2 * i + (LO + k), (LO + k) % 2)
                for s in range(HI, LAST + 1):
                    step(s, s % 2)

            with nc.Block() as block:
                @block.sync
                def _(sp):
                    if layer == 0:
                        expert_loads(sp, 0, range(E - 1))

                @block.vector
                def _(dve):
                    def step(s, par):
                        if ok(s + 3):
                            dve.wait_ge(bn_done, s + 4)
                        if ok(s):
                            m, z = smax[:, par, :], S[:, par, :]
                            dve.wait_ge(sc_done, s + 1)
                            wait(dve, sub_done, 2 * s)
                            for n, src, h0 in hk_banks(pS):
                                nc.vector.tensor_reduce(
                                    m[:, h0:h0 + n] if n == 4 else m[:, 0:12].rearrange("p (b h) -> p b h", b=2),
                                    src, AX, ALU.max).then_inc(max_done, 1)
                            dve.wait_ge(max_done, 2 * (s + 1))
                            wait(dve, tp_done, s - 1)
                            for n, src, h0 in hk_banks(pS):
                                dst = z[:, h0 * SK:(h0 + n) * SK]
                                mm = m[:, h0:h0 + n]
                                if n == 12:
                                    dst = dst.rearrange("p (b h k) -> p b h k", b=2, k=SK)
                                    mm = mm.rearrange("p (b h) -> p b h", b=2).unsqueeze(3).to_broadcast([P, 2, 6, SK])
                                else:
                                    dst = dst.rearrange("p (h k) -> p h k", k=SK)
                                    mm = mm.unsqueeze(2).to_broadcast([P, 4, SK])
                                nc.vector.tensor_tensor(dst, src, mm, ALU.subtract).then_inc(sub_done, 1)
                        if ok(s + 3):
                            q = 1 - par
                            nc.vector.bn_aggr(mv[:, q, :], bst[:, q, :]).then_inc(stats_done, 1)
                        if ok(s - 2):
                            t = s - 2
                            dve.wait_ge(pv_done, t + 1)
                            dve.wait_ge(bias_done, t + 1)
                            nc.vector.scalar_tensor_tensor(out=tile(t), in0=pO, scalar=gscale[:, layer:layer + 1],
                                                           in1=tile(t), op0=ALU.mult, op1=ALU.add).then_inc(epi_done, 1)
                        if ok(s - 1):
                            t, q = s - 1, 1 - par
                            dve.wait_ge(phi_done, t + 1)
                            wait(dve, pv_done, t - 1)
                            nc.vector.scalar_tensor_tensor(
                                out=PT[:, q, 1].rearrange("p j n -> p (j n)"), in0=pT, scalar=PS,
                                in1=PT[:, q, 0].rearrange("p j n -> p (j n)"),
                                op0=ALU.mult, op1=ALU.subtract).then_inc(plo_done, 1)
                        if ok(s):
                            dve.wait_ge(exp_done, s + 1)
                            wait(dve, rec_done, s - 1)
                            nc.vector.tensor_reduce(ssum[:, par, :], S[:, par, 0:HK].rearrange("p (h k) -> p h k", k=SK),
                                                    AX, ALU.add).then_inc(sum_done, 1)
                            dve.wait_ge(sum_done, s + 1)
                            wait(dve, nrm_done, s - 1)
                            nc.vector.reciprocal(srec[:, par, :], ssum[:, par, :]).then_inc(rec_done, 1)
                        if ok(s + 2):
                            t = s + 2
                            dve.wait_ge(xhi_done, t + 1)
                            wait(dve, sc_done, t - 1)
                            nc.vector.tensor_tensor(xT[:, par, 1], pX, xT[:, par, 0], ALU.subtract).then_inc(xlo_done, 1)
                        if ok(s + 4):
                            t = s + 4
                            if combine:
                                for k in range(2):
                                    dve.wait_ge(got[k], 16 * (t + 1))
                                    if k:
                                        dve.wait_ge(comb_a, t + 1)
                                    nc.vector.scalar_tensor_tensor(
                                        out=tile(t), in0=yrows[:, k, :], scalar=topw[:, k, bass.ds(t, 1)],
                                        in1=tile(t), op0=ALU.mult, op1=ALU.add).then_inc(comb_done if k else comb_a, 1)
                                dve.wait_ge(comb_done, t + 1)
                            wait(dve, stats_done, t - 1)
                        if ok(s + 3):
                            t, q = s + 3, 1 - par
                            dve.wait_ge(rstd_done, t + 1)
                            wait(dve, tx_done, t - 1)
                            nc.vector.tensor_scalar(xnb[:, q, :], tile(t), mv[:, q, 0:1], rstd[:, q, 0:1],
                                                    ALU.subtract, ALU.mult).then_inc(xn_done, 1)
                        if ok(s + 4):
                            nc.vector.bn_stats(bst[:, par, :], tile(s + 4)).then_inc(bn_done, 1)
                    if layer == 0:
                        dve.wait_ge(s_x, 16 * B)
                    drive(dve, step)

                @block.scalar
                def _(act):
                    def step(s, par):
                        if ok(s - 1):
                            t, q = s - 1, 1 - par
                            act.wait_ge(tp_done, t + 1)
                            wait(act, pv_done, t - 1)
                            nc.scalar.activation(PT[:, q, 0].rearrange("p j n -> p (j n)"), pT, ACT.Copy,
                                                 scale=PS).then_inc(phi_done, 1)
                        if ok(s):
                            act.wait_ge(sub_done, 2 * (s + 1))
                            nc.scalar.activation(S[:, par, 0:HK], S[:, par, 0:HK], ACT.Exp,
                                                 scale=softmax_scale).then_inc(exp_done, 1)
                        if ok(s + 2):
                            t = s + 2
                            act.wait_ge(tx_done, t + 1)
                            wait(act, sc_done, t - 1)
                            nc.scalar.copy(xT[:, par, 0], pX).then_inc(xhi_done, 1)
                    drive(act, step)

                @block.gpsimd
                def _(pool):
                    def index(t):
                        wait(pool, comb_done, t)
                        nc.gpsimd.tensor_copy(idx_now[:], pos[:, :, bass.ds(t, 1)].rearrange("p a b -> p (a b)")).then_inc(idx_done, 1)

                    def gather(t):
                        for k in range(2):
                            nc.gpsimd.indirect_dma_start(yrows[:, k, :], None, ys, bass.IndirectOffsetOnAxis(
                                ap=idx_now[:, k:k + 1], axis=0)).then_inc(got[k], 16)

                    def step(s, par):
                        if combine and ok(s + 4):
                            index(s + 4)
                            pool.wait_ge(idx_done, s + 5)
                        if ok(s + 3):
                            t, q = s + 3, 1 - par
                            pool.wait_ge(stats_done, t + 1)
                            wait(pool, xn_done, t - 1)
                            nc.gpsimd.tensor_tensor(rstd[:, q, 1:2], mv[:, q, 1:2], ln_eps, ALU.add).then_inc(eps_done, 1)
                            pool.wait_ge(eps_done, t + 1)
                            nc.gpsimd.tensor_tensor(rstd[:, q, 0:1], rstd[:, q, 1:2], half, ALU.pow).then_inc(rstd_done, 1)
                        if combine and ok(s + 4):
                            gather(s + 4)
                        if ok(s):
                            pool.wait_ge(rec_done, s + 1)
                            z = S[:, par, 0:HK].rearrange("p (h k) -> p h k", k=SK)
                            nc.gpsimd.tensor_tensor(z, z, srec[:, par, :].unsqueeze(2).to_broadcast([P, H, SK]),
                                                    ALU.mult).then_inc(nrm_done, 1)
                        if ok(s + 3):
                            t, q = s + 3, 1 - par
                            pool.wait_ge(xn_done, t + 1)
                            if affine:
                                nc.gpsimd.tensor_tensor(xnb[:, q, :], xnb[:, q, :], ln_gamma, ALU.mult).then_inc(xin_done, 1)
                            nc.gpsimd.tensor_tensor(tile(t), tile(t), b_row[:], ALU.add).then_inc(bias_done, 1)
                            if affine:
                                pool.wait_ge(xin_done, 2 * t + 1)
                                nc.gpsimd.tensor_tensor(xnb[:, q, :], xnb[:, q, :], ln_beta, ALU.add).then_inc(xin_done, 1)
                    drive(pool, step)

                @block.tensor
                def _(pe):
                    def step(s, par, b1, b2):
                        if ok(s + 1):
                            t, q = s + 1, 1 - par
                            pe.wait_ge(xlo_done, t + 1)
                            wait(pe, sub_done, 2 * t)
                            for bank, o0, o1, c, g0 in pieces:
                                w = o1 - o0
                                cs = c if isinstance(c, tuple) else (c,)
                                n = 0
                                for cc in cs:
                                    for px, pg in ((0, 0), (1, 0), (0, 1)):
                                        last = nc.tensor.matmul(
                                            banks[:, 1 + bank, o0:o1], xT[:, q, px, cc, :], Gof(pg, b1, cc)[:, g0:g0 + w],
                                            start=(n == 0), stop=(n == 3 * len(cs) - 1))
                                        n += 1
                            last.then_inc(sc_done, 1)
                        if ok(s + 2):
                            t = s + 2
                            pe.wait_ge(xin_done if affine else xn_done, per * (t + 1))
                            wait(pe, xlo_done, t)
                            for c in range(C):
                                last = nc.tensor.transpose(pX[:, c, :], xnb[:, par, c * P:(c + 1) * P], ident[:])
                            last.then_inc(tx_done, 1)
                        if ok(s - 1):
                            t, q = s - 1, 1 - par
                            pe.wait_ge(plo_done, t + 1)
                            wait(pe, epi_done, t)
                            n = 0
                            for pp, pv in ((0, 0), (1, 0), (0, 1)):
                                for j in range(J):
                                    last = nc.tensor.matmul(pO, PT[:, q, pp, j, :], VW[:, pv, b2, j, :],
                                                            start=(n == 0), stop=(n == 3 * J - 1))
                                    n += 1
                            last.then_inc(pv_done, 1)
                        if ok(s):
                            pe.wait_ge(nrm_done, s + 1)
                            wait(pe, plo_done, s)
                            for j in range(J):
                                last = nc.tensor.transpose(pT[:, j * P:(j + 1) * P], S[:, par, j * P:(j + 1) * P], ident[:])
                            last.then_inc(tp_done, 1)

                    def batches(s):
                        return min(max(s + 1, 0), T - 1) // TB, min(max(s - 1, 0), T - 1) // TB

                    s = FIRST
                    while s <= LAST:
                        n = 0
                        while 2 <= s and s + n + 1 <= T - 3 and batches(s) == batches(s + n + 1):
                            n += 1
                        if n >= 3:
                            n = (n + 1) // 2
                            with pe.Fori(0, n) as i:
                                for k in range(2):
                                    step(2 * i + (s + k), (s + k) % 2, *batches(s))
                            s += 2 * n
                        else:
                            step(s, s % 2, *batches(s))
                            s += 1

        pieces0 = []
        for bank, (h0, n) in enumerate(((0, 6), (6, 6), (12, 4))):
            for c in range(C):
                lo, hi = max(h0, c * H // C), min(h0 + n, (c + 1) * H // C)
                if lo < hi:
                    pieces0.append((bank, (lo - h0) * SK, (hi - h0) * SK, c, (lo - c * H // C) * SK))
        TE = [P, T, E]
        wA = view(region_a, 0, [E, 2 * C * F], F16)
        wB = view(region_b, 0, [E, 2 * FC * D], F16)
        WW = C * F
        raw = [view(region_a, 0, [E, WW]), view(region_b, 0, [E, WW])]
        raw_last = view(work, 0, [WW])
        w_o = WW
        xnb2 = view(work, w_o, [2, D])
        xsb = view(work, w_o + 512, [2, 2, D], F16)
        xT32 = view(work, w_o + 1024, [2, C, P])
        stats = view(work, w_o + 1536, [T, 6])
        mv_all = view(work, w_o + 1728, [T, 2])
        rs_all = view(work, w_o + 1792, [2, T])
        r_o = w_o + 1856
        wg = view(work, r_o, [C, E])
        bg = view(work, r_o + 16, [E])
        iota_e = view(work, r_o + 24, [E])
        b1_rows = view(work, r_o + 32, [P])
        tri = view(work, r_o + 160, [P], F16)
        ones16 = view(work, r_o + 224, [P], F16)
        logits = view(work, r_o + 288, [T, E])
        q_o = r_o + 288 + NCOL
        oh = [view(work, q_o, [T, E]), view(work, q_o + NCOL, [T, E])]
        tmp = view(work, q_o + 2 * NCOL, [T, E])
        sel16 = view(work, q_o + 3 * NCOL, [T, E], F16)
        i_o = q_o + 3 * NCOL + NCOL // 2
        incl = view(work, i_o, [E, T])
        top_v = view(work, i_o + NCOL, [6, T])
        iota_lo = view(work, w_o, [P])
        iota_hi = view(work, w_o + 128, [NH])
        token = view(work, w_o + 216, [T])
        oh_lo = view(work, w_o + 248, [2, P])
        oh_hi = view(work, w_o + 504, [2, NH])
        pos_f = view(work, w_o + 668, [2, T])
        lohi_i = view(work, w_o + 732, [2, 2 * T], I32)
        lohi = view(work, w_o + 860, [2, 2 * T])
        tiles_i = view(work, w_o + 988, [2, E], I32)
        tiles_f = view(work, w_o + 1004, [3, E])
        iota_tile = view(work, w_o + 1028, [NT])
        tile_cmp = view(work, w_o + 1070, [NT, E])
        ones_t = view(work, w_o + 1070 + NT * E, [T])
        te_f = view(work, w_o + 1070 + NT * E + T, [NT])
        assert w_o + 1070 + NT * E + T + NT <= w_o + 1536 and i_o + NCOL + 6 * T <= 6750

        s_wl = [[sem(f"expert_matrices_{m}_loaded"), sem(f"last_expert_matrix_{m}_loaded")] for m in range(2)]
        s_whi = sem("expert_weights_hi")
        s_wlo = sem("expert_weights_lo")
        s_gl = sem("gate_inputs_loaded")
        s_gc = sem("gate_consts")
        s_b1t = sem("b1_transposed")
        s_b1 = sem("b1_columns")
        s_bn = sem("gate_bn")
        s_ag = sem("gate_bn_aggr")
        s_rs = sem("gate_rstd")
        s_xn = sem("gate_xn")
        s_xh = sem("gate_x_hi")
        s_xl = sem("gate_x_lo")
        s_tx = sem("gate_x_transposed")
        s_tc = sem("gate_x_transpose_copied")
        s_lg = sem("gate_logits")
        s_st = [sem("xs_written_0"), sem("xs_written_1")]
        s_r = sem("routing_step")
        s_se = sem("selected")
        s_ex = sem("gate_exp")
        s_pf = sem("prefix_counts")
        s_hot = sem("one_hots")
        s_hm = sem("one_hots_used")
        s_slot = sem("slot_table")

        def expert_loads(sp, m, experts):
            src = a["L0_ffn_W1"] if m == 0 else a["L0_ffn_W2"]
            for e in experts:
                dst = raw[m][:, e + 1, :] if e < E - 1 else raw_last
                n = src.shape[2]
                sp.dma_start(dst.rearrange("p (c n) -> p c n", n=n),
                             src[e].rearrange("(c p) n -> p c n", p=P)).then_inc(s_wl[m][e == E - 1], 16)

        def weights_of(m):
            return wA if m == 0 else wB

        def split_hi(act, m, e):
            act.wait_ge(s_wl[m][e == E - 1], 16 if e == E - 1 else 16 * (E - 1))
            wait(act, s_wlo, E * m + e)
            src = raw[m][:, e + 1, :] if e < E - 1 else raw_last
            nc.scalar.activation(weights_of(m)[:, e, 0:WW], src, ACT.Copy, scale=WS).then_inc(s_whi, 1)

        def split_lo(dve, m, e):
            dve.wait_ge(s_whi, E * m + e + 1)
            src = raw[m][:, e + 1, :] if e < E - 1 else raw_last
            nc.vector.scalar_tensor_tensor(out=weights_of(m)[:, e, WW:2 * WW], in0=src, scalar=WS,
                                           in1=weights_of(m)[:, e, 0:WW], op0=ALU.mult,
                                           op1=ALU.subtract).then_inc(s_wlo, 1)

        pGX = banks[:, 0:2, 0:C * P].rearrange("p a (c n) -> p a c n", c=C)
        pG = banks[:, 2, 0:NCOL]
        pPre = banks[:, 3, 0:NCOL].rearrange("p (t e) -> p t e", e=E)
        pTot = banks[:, 4, 0:NCOL].rearrange("p (t e) -> p t e", e=E)
        pB1 = banks[:, 5, 0:E * FC]
        pSlot = banks[:, 6, 0:NH]
        xs_t = xs.rearrange("(t p) d -> p t d", p=P)

        def pairs(eng, n, step):
            for t in range(2):
                step(t, t, 0)
            with eng.Fori(1, n // 2) as i:
                for k in range(2):
                    step(2 * i + k, k, i)

        def gating():
            with nc.Block() as block:
                @block.sync
                def _(sp):
                    sp.dma_start(wg, a["L0_ffn_Wg"].rearrange("(c p) e -> p c e", p=P)).then_inc(s_gl, 16)
                    sp.dma_start(bg, a["L0_ffn_bg"].rearrange("(a e) -> a e", a=1).to_broadcast([P, E])).then_inc(s_gl, 16)
                    sp.dma_start(b1_rows[0:E * FC], a["L0_ffn_b1"].rearrange("e (f p) -> (e f) p", p=P)).then_inc(s_gl, 16)
                    expert_loads(sp, 0, [E - 1])
                    expert_loads(sp, 1, range(E - 1))

                    def step(t, par, h):
                        sp.wait_ge(s_xl, t + 1)
                        sp.wait_ge(s_xh, t + 1)
                        sp.dma_start(xs_t[:, bass.ds(t, 1), :].rearrange("p a d -> p (a d)"),
                                     xsb[:, par].rearrange("p s d -> p (s d)")).then_inc(s_st[par], 16)
                    pairs(sp, T, step)
                    sp.wait_ge(s_wlo, E)
                    expert_loads(sp, 1, [E - 1])
                    for par in range(2):
                        sp.wait_ge(s_st[par], 16 * T // 2)

                @block.gpsimd
                def _(pool):
                    nc.gpsimd.iota(iota_e, pattern=[[1, E]], base=-E, channel_multiplier=0,
                                   allow_small_or_imprecise_dtypes=True).then_inc(s_gc, 1)
                    nc.gpsimd.memset(tri, 1.0).then_inc(s_gc, 1)
                    nc.gpsimd.memset(ones16, 1.0).then_inc(s_gc, 1)
                    pool.wait_ge(s_gc, 3)
                    nc.gpsimd.affine_select(out=tri, in_=tri, compare_op=ALU.is_gt, fill=0.0, base=0,
                                            pattern=[[1, P]], channel_multiplier=-1).then_inc(s_gc, 1)
                    pool.wait_ge(s_ag, T)
                    nc.gpsimd.tensor_tensor(rs_all[:, 1, :], mv_all[:, :, 1], eps.to_broadcast([P, T]), ALU.add).then_inc(s_rs, 1)
                    pool.wait_ge(s_rs, 1)
                    nc.gpsimd.tensor_tensor(rs_all[:, 0, :], rs_all[:, 1, :], half.to_broadcast([P, T]), ALU.pow).then_inc(s_rs, 1)

                    def step(t, par, h):
                        pool.wait_ge(s_xh, t + 1)
                        wait(pool, s_st[par], 16 * h)
                        nc.gpsimd.tensor_tensor(xsb[:, par, 1, :], xnb2[:, par, :], xsb[:, par, 0, :],
                                                ALU.subtract).then_inc(s_xl, 1)
                    pairs(pool, T, step)
                    pool.wait_ge(s_st[0], 16 * T // 2)
                    pool.wait_ge(s_st[1], 16 * T // 2)
                    pool.wait_ge(s_lg, T)
                    nc.gpsimd.iota(iota_lo, pattern=[[1, P]], base=0, channel_multiplier=0,
                                   allow_small_or_imprecise_dtypes=True).then_inc(s_gc, 1)
                    nc.gpsimd.iota(iota_hi, pattern=[[1, NH]], base=0, channel_multiplier=0,
                                   allow_small_or_imprecise_dtypes=True).then_inc(s_gc, 1)
                    nc.gpsimd.iota(token, pattern=[[P, T]], base=0, channel_multiplier=1,
                                   allow_small_or_imprecise_dtypes=True).then_inc(s_gc, 1)
                    nc.gpsimd.iota(iota_tile, pattern=[[1, NT]], base=0, channel_multiplier=0,
                                   allow_small_or_imprecise_dtypes=True).then_inc(s_gc, 1)
                    nc.gpsimd.memset(ones_t, 1.0).then_inc(s_gc, 1)

                @block.scalar
                def _(act):
                    act.wait_ge(s_b1t, 1)
                    nc.scalar.copy(b1_cols[:].rearrange("p e f -> p (e f)"), pB1).then_inc(s_b1, 1)

                    def step(t, par, h):
                        act.wait_ge(s_xn, t + 1)
                        wait(act, s_st[par], 16 * h)
                        nc.scalar.copy(xsb[:, par, 0, :], xnb2[:, par, :]).then_inc(s_xh, 1)
                        act.wait_ge(s_tx, t + 1)
                        wait(act, s_lg, t - 1)
                        nc.scalar.copy(xT32[:, par], pGX[:, par]).then_inc(s_tc, 1)
                    pairs(act, T, step)
                    for e in range(E):
                        split_hi(act, 0, e)
                    act.wait_ge(s_se, 1)
                    nc.scalar.activation(top_v[:, 3, :], top_v[:, 3, :], ACT.Exp).then_inc(s_ex, 1)
                    for e in range(E):
                        split_hi(act, 1, e)

                @block.tensor
                def _(pe):
                    pe.wait_ge(s_gl, 48)
                    nc.tensor.transpose(pB1, b1_rows[0:E * FC, :], ident[0:E * FC, 0:E * FC]).then_inc(s_b1t, 1)

                    def step(t, par, h):
                        pe.wait_ge(s_xn, t + 1)
                        wait(pe, s_tc, t - 1)
                        for c in range(C):
                            last = nc.tensor.transpose(pGX[:, par, c, :], xnb2[:, par, c * P:(c + 1) * P], ident[:])
                        last.then_inc(s_tx, 1)
                        pe.wait_ge(s_tc, t + 1)
                        o = banks[:, 2, bass.ds(t * E, E)]
                        for c in range(C):
                            last = nc.tensor.matmul(o, xT32[:, par, c, :], wg[:, c, :], start=(c == 0), stop=(c == C - 1))
                        last.then_inc(s_lg, 1)
                    pairs(pe, T, step)
                    pe.wait_ge(s_se, 2)
                    pe.wait_ge(s_gc, 4)
                    sel = sel16.rearrange("p t e -> p (t e)")
                    nc.tensor.matmul(banks[:, 3, 0:NCOL], tri, sel, start=True, stop=True).then_inc(s_pf, 1)
                    nc.tensor.matmul(banks[:, 4, 0:NCOL], ones16, sel, start=True, stop=True).then_inc(s_pf, 1)

                    def hot(t, first, last_one):
                        for k in range(2):
                            pe.wait_ge(s_hot, 4 * t + 2 * k + 2)
                            nc.tensor.matmul(pSlot, oh_lo[:, k, :], oh_hi[:, k, :], start=first and k == 0,
                                             stop=last_one and k == 1).then_inc(s_hm, 1)
                    hot(0, True, False)
                    with pe.Fori(1, T - 1) as t:
                        hot(t, False, False)
                    hot(T - 1, False, True)

                @block.vector
                def _(dve):
                    with dve.Fori(0, T) as t:
                        nc.vector.bn_stats(stats[:, bass.ds(t, 1), :].rearrange("p a b -> p (a b)"),
                                           x_res[:, bass.ds(t, 1), :].rearrange("p a b -> p (a b)")).then_inc(s_bn, 1)
                    dve.wait_ge(s_bn, T)
                    for t in range(T):
                        nc.vector.bn_aggr(mv_all[:, t, :], stats[:, t, :]).then_inc(s_ag, 1)
                    dve.wait_ge(s_rs, 2)

                    def step(t, par, h):
                        wait(dve, s_xl, t - 1)
                        wait(dve, s_tx, t - 1)
                        wait(dve, s_xh, t - 1)
                        nc.vector.tensor_scalar(xnb2[:, par, :], x_res[:, bass.ds(t, 1), :].rearrange("p a b -> p (a b)"),
                                                mv_all[:, bass.ds(t, 1), 0], rs_all[:, 0, bass.ds(t, 1)],
                                                ALU.subtract, ALU.mult).then_inc(s_xn, 1)
                    pairs(dve, T, step)
                    for e in range(E):
                        split_lo(dve, 0, e)

                    count = [0]

                    def link(instruction):
                        count[0] += 1
                        instruction.then_inc(s_r, 1)
                        dve.wait_ge(s_r, count[0])

                    def bt(v):
                        return v.unsqueeze(2).to_broadcast(TE)

                    def be(v):
                        return v.unsqueeze(1).to_broadcast(TE)

                    dve.wait_ge(s_lg, T)
                    dve.wait_ge(s_gc, 4)
                    link(nc.vector.tensor_tensor(logits, pG.rearrange("p (t e) -> p t e", e=E), be(bg), ALU.add))
                    src = logits
                    for k in range(2):
                        link(nc.vector.tensor_reduce(top_v[:, k, :], src, AX, ALU.max))
                        link(nc.vector.tensor_tensor(tmp, src, bt(top_v[:, k, :]), ALU.is_equal))
                        link(nc.vector.tensor_tensor(tmp, tmp, be(iota_e), ALU.mult))
                        link(nc.vector.tensor_reduce(top_v[:, 2, :], tmp, AX, ALU.min))
                        link(nc.vector.tensor_tensor(oh[k], be(iota_e), bt(top_v[:, 2, :]), ALU.is_equal))
                        if k == 0:
                            link(nc.vector.scalar_tensor_tensor(out=logits, in0=oh[0], scalar=-1e30, in1=logits,
                                                                op0=ALU.mult, op1=ALU.add))
                    nc.vector.tensor_tensor(top_v[:, 3, :], top_v[:, 1, :], top_v[:, 0, :], ALU.subtract).then_inc(s_se, 1)
                    nc.vector.tensor_tensor(sel16, oh[0], oh[1], ALU.add).then_inc(s_se, 1)
                    dve.wait_ge(s_ex, 1)
                    link(nc.vector.tensor_scalar(top_v[:, 4, :], top_v[:, 3, :], 1.0, None, ALU.add))
                    link(nc.vector.reciprocal(top_v[:, 5, :], top_v[:, 4, :]))
                    link(nc.vector.tensor_scalar(topw[:, 0, :], top_v[:, 5, :], gscale[:, 1:2], None, ALU.mult))
                    link(nc.vector.tensor_tensor(topw[:, 1, :], topw[:, 0, :], top_v[:, 3, :], ALU.mult))
                    dve.wait_ge(s_pf, 2)
                    dve.wait_ge(s_gc, 9)
                    for e in range(E):
                        link(nc.vector.tensor_tensor_scan(incl[:, e, :], ones_t, pTot[:, :, e], 0.0, ALU.mult, ALU.add))
                    link(nc.vector.tensor_scalar(tiles_i[:, 0, :], incl[:, :, T - 1], float(TT - 1), None, ALU.add))
                    link(nc.vector.tensor_scalar(tiles_i[:, 1, :], tiles_i[:, 0, :], TT.bit_length() - 1, None, ALU.arith_shift_right))
                    link(nc.vector.tensor_copy(tiles_f[:, 0, :], tiles_i[:, 1, :]))
                    link(nc.vector.tensor_tensor_scan(tiles_f[:, 1, :], ones_t[:, 0:E], tiles_f[:, 0, :], 0.0, ALU.mult, ALU.add))
                    link(nc.vector.tensor_tensor(tiles_f[:, 2, :], tiles_f[:, 1, :], tiles_f[:, 0, :], ALU.subtract))
                    link(nc.vector.tensor_scalar(tiles_f[:, 2, :], tiles_f[:, 2, :], float(TT), None, ALU.mult))
                    link(nc.vector.tensor_tensor(tmp, incl.rearrange("p e t -> p t e"), pTot, ALU.subtract))
                    link(nc.vector.tensor_tensor(tmp, tmp, pPre, ALU.add))
                    link(nc.vector.tensor_tensor(tmp, tmp, be(tiles_f[:, 2, :]), ALU.add))
                    for k in range(2):
                        link(nc.vector.tensor_tensor(oh[k], oh[k], tmp, ALU.mult))
                        link(nc.vector.tensor_reduce(pos_f[:, k, :], oh[k], AX, ALU.add))
                    link(nc.vector.tensor_copy(pos[:], pos_f))
                    flat = pos[:].rearrange("p a b -> p (a b)")
                    link(nc.vector.tensor_scalar(lohi_i[:, 0, :], flat, P - 1, None, ALU.bitwise_and))
                    link(nc.vector.tensor_scalar(lohi_i[:, 1, :], flat, P.bit_length() - 1, None, ALU.arith_shift_right))
                    link(nc.vector.tensor_copy(lohi, lohi_i))

                    def hot(t):
                        for k in range(2):
                            wait(dve, s_hm, 2 * t + k - 1)
                            at = k * T + t
                            nc.vector.tensor_scalar(oh_lo[:, k, :], iota_lo, lohi[:, 0, bass.ds(at, 1)], None,
                                                    ALU.is_equal).then_inc(s_hot, 1)
                            nc.vector.tensor_scalar(oh_hi[:, k, :], iota_hi, lohi[:, 1, bass.ds(at, 1)],
                                                    token[:, bass.ds(t, 1)], ALU.is_equal, ALU.mult).then_inc(s_hot, 1)
                    hot(0)
                    with dve.Fori(1, T) as t:
                        hot(t)
                    row = [1, NT, E]
                    link(nc.vector.tensor_tensor(tile_cmp[0:1], iota_tile[0:1].unsqueeze(2).to_broadcast(row),
                                                 tiles_f[0:1, 1, :].unsqueeze(1).to_broadcast(row), ALU.is_ge))
                    link(nc.vector.tensor_reduce(te_f[0:1], tile_cmp[0:1], AX, ALU.add))
                    link(nc.vector.tensor_scalar(te_f[0:1], te_f[0:1], float(E - 1), None, ALU.min))
                    link(nc.vector.tensor_copy(tile_expert[:], te_f[0:1]))
                    dve.wait_ge(s_hm, 2 * T)
                    nc.vector.tensor_copy(slot_token[:], pSlot).then_inc(s_slot, 1)
                    for e in range(E):
                        split_lo(dve, 1, e)

        b2_all = view(work, 0, [E, D])
        m_o = E * D
        xg = view(work, m_o, [2, 2 * D], F16)
        xgT = view(work, m_o + 512, [2, C, TT], F16)
        hf = view(work, m_o + 1024, [2, 2 * TT])
        hh = view(work, m_o + 2048, [4, 2, 2, TT], F16)
        ysb = view(work, m_o + 4096, [2, D])
        s_b2 = sem("b2_loaded")
        s_gi = sem("moe_index")
        s_xg = [sem("moe_rows_0"), sem("moe_rows_1")]
        s_gt2 = sem("moe_transposed")
        s_gx = sem("moe_transpose_copied")
        s_up = sem("moe_up")
        s_ge = sem("moe_gelu")
        s_hi = sem("moe_hi")
        s_lo = sem("moe_lo")
        s_dn = sem("moe_down")
        s_ye = sem("moe_out_copied")
        s_yw = sem("moe_out_written")
        pXg = banks[:, 5, :].bitcast(F16).rearrange("p (s c n) -> p s c n", s=2, c=C)
        pY = banks[:, 4, :].rearrange("p (s d) -> p s d", s=2)
        ys_t = ys.rearrange("(i s p) d -> p i s d", s=2, p=P)

        def experts():
            with nc.Block() as block:
                @block.sync
                def _(sp):
                    sp.dma_start(b2_all, a["L0_ffn_b2"].rearrange("(a e) d -> a e d", a=1).to_broadcast([P, E, D])).then_inc(s_b2, 16)
                    with sp.Fori(0, NT) as i:
                        sp.wait_ge(s_ye, i + 1)
                        sp.dma_start(ys_t[:, bass.ds(i, 1), :, :].rearrange("p a s d -> p (a s) d"), ysb).then_inc(s_yw, 16)
                    sp.wait_ge(s_yw, 16 * NT)

                @block.gpsimd
                def _(pool):
                    def index(i, par):
                        nc.gpsimd.tensor_copy(idx_ring[:, par, :], slot_token[:, bass.ds(2 * i, 2)]).then_inc(s_gi, 1)

                    def step(i, par, h):
                        wait(pool, s_gt2, i)
                        pool.wait_ge(s_gi, i + 1)
                        index(i + 1, 1 - par)
                        for s in range(2):
                            nc.gpsimd.indirect_dma_start(xg[:, s, :], None, xs, bass.IndirectOffsetOnAxis(
                                ap=idx_ring[:, par, s:s + 1], axis=0)).then_inc(s_xg[s], 16)
                    index(0, 0)
                    pairs(pool, NT + 1, step)
                    for s in range(2):
                        pool.wait_ge(s_xg[s], 16 * (NT + 1))

                @block.tensor
                def _(pe):
                    def transposes(i):
                        wait(pe, s_gx, i)
                        for s in range(2):
                            pe.wait_ge(s_xg[s], 16 * (i + 1))
                            for part in range(2):
                                for c in range(C):
                                    last = nc.tensor.transpose(pXg[:, part, c, s * P:(s + 1) * P],
                                                               xg[:, s, part * D + c * P:part * D + (c + 1) * P], ident16[:])
                        last.then_inc(s_gt2, 1)

                    def up(i, e, b):
                        wait(pe, s_ge, 8 * (i - 1) + 2 * b + 2)
                        for f in (2 * b, 2 * b + 1):
                            n = 0
                            for pw, px in ((0, 0), (0, 1), (1, 0)):
                                for c in range(C):
                                    o = pw * WW + c * F + f * P
                                    last = nc.tensor.matmul(
                                        banks[:, b, (f % 2) * TT:(f % 2) * TT + TT],
                                        wA[:, bass.ds(e, 1), o:o + P].rearrange("p a m -> p (a m)"),
                                        xgT[:, px, c, :], start=(n == 0), stop=(n == 3 * C - 1))
                                    n += 1
                        last.then_inc(s_up, 1)

                    def down(i, e, b):
                        pe.wait_ge(s_lo, 4 * i + b + 1)
                        if b == 0:
                            wait(pe, s_ye, i)
                        for s in range(2):
                            for ph, pw in ((0, 0), (1, 0), (0, 1)):
                                for k in range(2):
                                    o = pw * WW + (2 * b + k) * D
                                    last = nc.tensor.matmul(
                                        pY[:, s, :], hh[:, b, ph, k, s * P:(s + 1) * P],
                                        wB[:, bass.ds(e, 1), o:o + D].rearrange("p a m -> p (a m)"),
                                        start=(b == 0 and s == 0 and ph == 0 and pw == 0 and k == 0),
                                        stop=(b == 3 and s == 1 and pw == 1 and k == 1),
                                        skip_group_check=True)
                        last.then_inc(s_dn, 1)

                    def tile(i):
                        e = pe.value_load(tile_expert[0:1, bass.ds(i, 1)], min_val=0, max_val=E - 1)
                        pe.wait_ge(s_gx, i + 1)
                        up(i, e, 0)
                        up(i, e, 1)
                        down(i, e, 0)
                        up(i, e, 2)
                        down(i, e, 1)
                        up(i, e, 3)
                        transposes(i + 1)
                        down(i, e, 2)
                        down(i, e, 3)
                    transposes(0)
                    tile(0)
                    with pe.Fori(1, NT) as i:
                        tile(i)

                @block.scalar
                def _(act):
                    b1f = b1_cols[:].rearrange("p e f -> p (e f)")

                    def tile(i):
                        e = act.value_load(tile_expert[0:1, bass.ds(i, 1)], min_val=0, max_val=E - 1)
                        for b in range(4):
                            act.wait_ge(s_up, 4 * i + b + 1)
                            wait(act, s_lo, 4 * i + b - 1)
                            for k in range(2):
                                nc.scalar.activation(hf[:, b % 2, k * TT:(k + 1) * TT], banks[:, b, k * TT:(k + 1) * TT],
                                                     ACT.Gelu, bias=b1f[:, bass.ds(e * FC + (2 * b + k), 1)],
                                                     scale=1.0 / WS).then_inc(s_ge, 1)
                    tile(0)
                    with act.Fori(1, NT) as i:
                        tile(i)

                @block.vector
                def _(dve):
                    def rows(i):
                        dve.wait_ge(s_gt2, i + 1)
                        nc.vector.tensor_copy(xgT.rearrange("p s c n -> p (s c n)"),
                                              pXg.rearrange("p s c n -> p (s c n)")).then_inc(s_gx, 1)

                    def tile(i):
                        e = dve.value_load(tile_expert[0:1, bass.ds(i, 1)], min_val=0, max_val=E - 1)
                        for b in range(4):
                            dve.wait_ge(s_ge, 8 * i + 2 * b + 2)
                            wait(dve, s_dn, 4 * (i - 1) + b + 1)
                            h_hi, h_lo = (hh[:, b, s].rearrange("p k n -> p (k n)") for s in range(2))
                            nc.vector.tensor_copy(h_hi, hf[:, b % 2, :]).then_inc(s_hi, 1)
                            dve.wait_ge(s_hi, 4 * i + b + 1)
                            nc.vector.tensor_tensor(h_lo, hf[:, b % 2, :], h_hi, ALU.subtract).then_inc(s_lo, 1)
                        rows(i + 1)
                        dve.wait_ge(s_dn, 4 * i + 4)
                        wait(dve, s_yw, 16 * i)
                        nc.vector.scalar_tensor_tensor(
                            out=ysb, in0=pY, scalar=1.0 / WS,
                            in1=b2_all[:, bass.ds(e, 1), :].to_broadcast([P, 2, D]),
                            op0=ALU.mult, op1=ALU.add).then_inc(s_ye, 1)
                    dve.wait_ge(s_b2, 16)
                    rows(0)
                    tile(0)
                    with dve.Fori(1, NT) as i:
                        tile(i)

        NP_ = INNER // P
        W1_ = 2 * SK
        G1 = view(region_a, 0, [2, B, C, HK], F16)
        kv1 = view(region_a, B * C * HK, [2, NP_, KB])
        ctxT1 = view(region_a, B * C * HK + 2 * NP_ * KB, [C, KB])
        w_out = view(region_b, 0, [NP_, D])
        wqT = view(region_b, NP_ * D, [NP_, D])
        ln_gamma = view(region_b, 2 * NP_ * D, [D])
        ln_beta = view(region_b, 2 * NP_ * D + D, [D])
        wkv1 = view(region_b, vw_word, [C, 2 * INNER])
        wq = view(region_b, vw_word + C * 2 * INNER, [C, INNER])
        ctx1 = view(region_b, vw_word + 3 * C * INNER, [B, D])
        VB1 = view(work, 2 * HKP, [P + NP_ * (W1_ + P)])
        kTB = view(work, 2 * HKP + P + NP_ * (W1_ + P), [NP_, W1_])
        yrows = view(work, 4 * HKP + 2 * D + 4 * C * P // 2, [2, D])
        assert 3 * C * INNER + B * D <= 2 * B * J * D // 2
        assert 2 * NP_ * D + 2 * D <= vw_word
        s_l1 = sem("l1_weights_loaded")
        s_l1c = sem("l1_consts")
        s_l1b = sem("l1_bias_scaled")
        s_ct1 = sem("l1_ctx_transposed")
        s_cc1 = sem("l1_ctx_copied")
        s_wt = sem("wq_transposed")
        s_wtc = sem("wq_copied")
        s_kv1 = sem("l1_kv")
        s_kvc = sem("l1_kv_copied")
        s_kb = sem("l1_k_spread")
        s_vb1 = sem("l1_v_spread")
        s_g1 = sem("l1_g")
        s_g1h = sem("l1_g_hi")
        s_g1l = sem("l1_g_lo")

        def fold_layer1():
            vw_base[0] = len(VGROUPS) * B
            with nc.Block() as block:
                @block.sync
                def _(sp):
                    sp.dma_start(ctx1[0:SK], a["ctx_1024"].rearrange("b k d -> k b d")).then_inc(s_l1, 16)
                    sp.dma_start(wq, a["L1_xattn_w_q"].rearrange("(c p) n -> p c n", p=P)).then_inc(s_l1, 16)
                    sp.dma_start(wkv1, a["L1_xattn_w_kv"].rearrange("(c p) n -> p c n", p=P)).then_inc(s_l1, 16)
                    sp.dma_start(w_out, a["L1_xattn_w_out"].rearrange("(c p) n -> p c n", p=P)).then_inc(s_l1, 16)
                    for dst, name in ((b_row[:], "L1_xattn_b_out"), (ln_gamma, "L1_xattn_ln_gamma"), (ln_beta, "L1_xattn_ln_beta")):
                        sp.dma_start(dst, a[name].rearrange("(a n) -> a n", a=1).to_broadcast([P, D])).then_inc(s_l1, 16)

                @block.gpsimd
                def _(pool):
                    nc.gpsimd.memset(VB1, 0.0).then_inc(s_l1c, 1)
                    nc.gpsimd.memset(kTB, 0.0).then_inc(s_l1c, 1)
                    nc.gpsimd.memset(S[:, :, HK:HKP], 0.0).then_inc(s_l1c, 1)
                    pool.wait_ge(s_l1c, 3)
                    pool.wait_ge(s_kvc, 2 * NP_)
                    for b in range(B):
                        wait(pool, s_vw, vw_base[0] + len(VGROUPS) * b)
                        for h in range(2):
                            rows = slice(64 * h, 64 * h + 64)
                            dst = VB1[rows, P:P + NP_ * (W1_ + P)].rearrange("p (n w) -> p n w", n=NP_)[:, :, h * SK:(h + 1) * SK]
                            nc.gpsimd.tensor_copy(dst, kv1[rows, 1, :, b * SK:(b + 1) * SK]).then_inc(s_vb1, 1)

                @block.scalar
                def _(act):
                    act.wait_ge(s_ct1, 1)
                    nc.scalar.copy(ctxT1, banks[:, 0:2, 0:KB]).then_inc(s_cc1, 1)
                    for n in range(NP_):
                        act.wait_ge(s_kv1, 2 * (n + 1))
                        o = 6 * (n % 2)
                        nc.scalar.copy(kv1[:, :, n, :], banks[:, o:o + 2, 0:KB]).then_inc(s_kvc, 2)
                    for b in range(B):
                        for c in range(C):
                            if c == 1:
                                vw_hi(act, b)
                            act.wait_ge(s_g1, 2 * b + c + 1)
                            nc.scalar.activation(G1[:, 0, b, c, 0:924].rearrange("p (a n) -> p a n", a=2), banks[:, 0:2, 0:462],
                                                 ACT.Copy, scale=AS).then_inc(s_g1h, 1)
                            nc.scalar.activation(G1[:, 0, b, c, 924:HK], banks[:, 2, 0:308],
                                                 ACT.Copy, scale=AS).then_inc(s_g1h, 1)

                @block.vector
                def _(dve):
                    dve.wait_ge(s_l1, 7 * 16)
                    nc.vector.tensor_scalar(b_row[:], b_row[:], gtanh[:, 1:2], gtanh[:, 4:5], ALU.mult, ALU.mult).then_inc(s_l1b, 1)
                    nc.vector.tensor_scalar(ln_gamma, ln_gamma, (1.0 + EPS) ** -0.5, None, ALU.mult).then_inc(s_l1b, 1)
                    dve.wait_ge(s_wt, 1)
                    nc.vector.tensor_copy(wqT.rearrange("p n d -> p (n d)"),
                                          banks[:, 2:6, :].rearrange("p a b -> p (a b)")).then_inc(s_wtc, 1)
                    dve.wait_ge(s_kvc, 2 * NP_)
                    dve.wait_ge(s_l1c, 3)
                    for b in range(B):
                        for c in range(C):
                            if c == 0:
                                wait(dve, s_g1, 2 * b)
                                for h in range(2):
                                    rows = slice(64 * h, 64 * h + 64)
                                    nc.vector.tensor_copy(kTB[rows, :, h * SK:(h + 1) * SK],
                                                          kv1[rows, 0, :, b * SK:(b + 1) * SK]).then_inc(s_kb, 1)
                            else:
                                vw_lo(dve, b)
                            dve.wait_ge(s_g1h, 2 * (2 * b + c + 1))
                            nc.vector.scalar_tensor_tensor(
                                out=G1[:, 1, b, c, 0:924].rearrange("p (a n) -> p a n", a=2), in0=banks[:, 0:2, 0:462],
                                scalar=AS, in1=G1[:, 0, b, c, 0:924].rearrange("p (a n) -> p a n", a=2),
                                op0=ALU.mult, op1=ALU.subtract).then_inc(s_g1l, 1)
                            nc.vector.scalar_tensor_tensor(
                                out=G1[:, 1, b, c, 924:HK], in0=banks[:, 2, 0:308], scalar=AS,
                                in1=G1[:, 0, b, c, 924:HK], op0=ALU.mult, op1=ALU.subtract).then_inc(s_g1l, 1)

                @block.tensor
                def _(pe):
                    pe.wait_ge(s_l1, 7 * 16)
                    for c in range(C):
                        for b in range(B):
                            last = nc.tensor.transpose(banks[:, c, b * SK:(b + 1) * SK],
                                                       ctx1[0:SK, b, c * P:(c + 1) * P], ident[0:SK, 0:SK])
                    last.then_inc(s_ct1, 1)
                    for n in range(NP_):
                        for c in range(C):
                            last = nc.tensor.transpose(banks[:, 2 + n // 2, (n % 2) * D + c * P:(n % 2) * D + (c + 1) * P],
                                                       wq[:, c, n * P:(n + 1) * P], ident[:])
                    last.then_inc(s_wt, 1)
                    pe.wait_ge(s_cc1, 1)
                    for n in range(NP_):
                        wait(pe, s_kvc, 2 * (n - 1))
                        for s in range(2):
                            for c in range(C):
                                o = s * INNER + n * P
                                last = nc.tensor.matmul(banks[:, 6 * (n % 2) + s, 0:KB], wkv1[:, c, o:o + P], ctxT1[:, c, :],
                                                        start=(c == 0), stop=(c == C - 1))
                            last.then_inc(s_kv1, 1)
                    pe.wait_ge(s_wtc, 1)
                    pe.wait_ge(s_kvc, 2 * NP_)
                    for b in range(B):
                        pe.wait_ge(s_kb, 2 * (b + 1))
                        for c in range(C):
                            if c == 1:
                                pe.wait_ge(s_vb1, 2 * (b + 1))
                                vw_product(pe, b, VB1, W1_, NP_, w_out, None)
                            wait(pe, s_g1l, 2 * (2 * b + c))
                            for n in range(NP_):
                                last = nc.tensor.matmul(banks[:, n // 3, (n % 3) * W1_:(n % 3) * W1_ + W1_],
                                                        wqT[:, n, c * P:(c + 1) * P], kTB[:, n, :], start=True, stop=True)
                            last.then_inc(s_g1, 1)

        GT = 4
        GN = GT * P
        NG = T // GT
        R2 = 2 * R
        U1r = view(region_a, 0, [C, R2])
        V1r = view(region_a, 256, [F])
        U2r = view(region_a, 1280, [FC, R])
        V2r = view(region_a, 1792, [D])
        U1s = view(region_a, 2048, [2, C, R2], F16)
        V1s = view(region_a, 2304, [2, F], F16)
        U2s = view(region_a, 3328, [FC, R2], F16)
        V2s = view(region_a, 3840, [2, D], F16)
        fb1_rows = view(region_a, 4096, [P])
        fb1 = view(region_a, 4224, [FC])
        fstats = view(region_a, 4300, [T, 6])
        fmv = view(region_a, 4500, [T, 2])
        frs = view(region_a, 4600, [2, T])
        fxn = view(region_b, 0, [2, D])
        fxT = view(region_b, 512, [2, C, GN], F16)
        rank_s = view(region_b, 1536, [GN], F16)
        fh = view(region_b, 1792, [2, GN])
        fhh = view(region_b, 2816, [4, 2, GN], F16)
        fq = view(region_b, 4864, [2, GN], F16)
        s_fl = sem("ffn_loaded")
        s_fw = sem("ffn_weights_hi")
        s_fwl = sem("ffn_weights_lo")
        s_fbt = sem("ffn_bias_transposed")
        s_fb = sem("ffn_bias_columns")
        s_fbn = sem("ffn_bn")
        s_fag = sem("ffn_bn_aggr")
        s_frs = sem("ffn_rstd")
        s_fxn = sem("ffn_xn")
        s_fba = sem("ffn_out_bias_added")
        s_ftx = sem("ffn_x_transposed")
        s_fxh = sem("ffn_x_hi")
        s_fxl = sem("ffn_x_lo")
        s_fu1 = sem("ffn_u1")
        s_fsh = sem("ffn_rank_hi")
        s_fsl = sem("ffn_rank_lo")
        s_fv1 = sem("ffn_v1")
        s_fge = sem("ffn_gelu")
        s_fhi = sem("ffn_h_hi")
        s_flo = sem("ffn_h_lo")
        s_fu2 = sem("ffn_u2")
        s_fqh = sem("ffn_q_hi")
        s_fql = sem("ffn_q_lo")
        s_fv2 = sem("ffn_v2")
        s_fep = sem("ffn_residual")
        s_out = sem("out_written")
        pFX = banks[:, 0:2, 0:C * P].rearrange("p a (c n) -> p a c n", c=C)
        out_t = out.rearrange("b (t p) d -> p (b t) d", p=P)

        def group_loop(eng, body):
            body(0, False, True)
            body(1, True, True)
            with eng.Fori(2, NG - 1) as g:
                body(g, True, True)
            body(NG - 1, True, False)

        def xtile(g, j):
            return x_res[:, bass.ds(g * GT + j, 1), :].rearrange("p a b -> p (a b)")

        def low_rank_ffn():
            with nc.Block() as block:
                @block.sync
                def _(sp):
                    for k in range(2):
                        rows = slice(k * R, (k + 1) * R)
                        sp.dma_start(U1r[:, :, rows], a["L1_ffn_U1"].rearrange("(c p) r -> p c r", p=P)).then_inc(s_fl, 16)
                        sp.dma_start(V1r[rows], a["L1_ffn_V1"]).then_inc(s_fl, 16)
                        sp.dma_start(V2r[rows], a["L1_ffn_V2"]).then_inc(s_fl, 16)
                    sp.dma_start(U2r, a["L1_ffn_U2"].rearrange("(f p) r -> p f r", p=P)).then_inc(s_fl, 16)
                    sp.dma_start(fb1_rows[0:FC], a["L1_ffn_b1"].rearrange("(f p) -> f p", p=P)).then_inc(s_fl, 16)
                    sp.dma_start(b_row[:], a["L1_ffn_b2"].rearrange("(a n) -> a n", a=1).to_broadcast([P, D])).then_inc(s_fl, 16)

                    def body(g):
                        sp.wait_ge(s_fep, GT * (g + 1))
                        sp.dma_start(out_t[:, bass.ds(g * GT, GT), :], x_res[:, bass.ds(g * GT, GT), :]).then_inc(s_out, 16)
                    with sp.Fori(0, NG) as g:
                        body(g)
                    sp.wait_ge(s_out, 16 * NG)

                @block.gpsimd
                def _(pool):
                    pool.wait_ge(s_fag, T)
                    nc.gpsimd.tensor_tensor(frs[:, 1, :], fmv[:, :, 1], eps.to_broadcast([P, T]), ALU.add).then_inc(s_frs, 1)
                    pool.wait_ge(s_frs, 1)
                    nc.gpsimd.tensor_tensor(frs[:, 0, :], frs[:, 1, :], half.to_broadcast([P, T]), ALU.pow).then_inc(s_frs, 1)
                    pool.wait_ge(s_fwl, 5)

                    def bias(g, j):
                        pool.wait_ge(s_fxn, GT * g + j + 1)
                        nc.gpsimd.tensor_tensor(xtile(g, j), xtile(g, j), b_row[:], ALU.add).then_inc(s_fba, 1)

                    def body(g, prev, nxt):
                        if nxt:
                            for j in range(GT):
                                bias(g + 1, j)
                    for j in range(GT):
                        bias(0, j)
                    group_loop(pool, body)

                @block.scalar
                def _(act):
                    act.wait_ge(s_fl, 9 * 16)
                    nc.scalar.activation(U1s[:, 0], U1r, ACT.Copy, scale=AS).then_inc(s_fw, 1)
                    nc.scalar.activation(V1s[:, 0], V1r, ACT.Copy, scale=AS).then_inc(s_fw, 1)
                    nc.scalar.activation(V2s[:, 0], V2r, ACT.Copy, scale=AS).then_inc(s_fw, 1)
                    nc.scalar.activation(U2s[:, :, 0:R], U2r, ACT.Copy, scale=AS).then_inc(s_fw, 1)
                    act.wait_ge(s_fbt, 1)
                    nc.scalar.copy(fb1, banks[:, 2, 0:FC]).then_inc(s_fb, 1)
                    act.wait_ge(s_fb, 1)

                    def xhi(g, j):
                        act.wait_ge(s_ftx, GT * g + j + 1)
                        wait(act, s_fu1, g)
                        nc.scalar.copy(fxT[:, 0, :, j * P:(j + 1) * P], pFX[:, j % 2]).then_inc(s_fxh, 1)

                    def body(g, prev, nxt):
                        act.wait_ge(s_fu1, g + 1)
                        wait(act, s_fv1, FC * g)
                        nc.scalar.copy(rank_s, banks[:, 2, :]).then_inc(s_fsh, 1)
                        for f in range(FC):
                            act.wait_ge(s_fv1, FC * g + f + 1)
                            wait(act, s_flo, FC * g + f - 1)
                            nc.scalar.activation(fh[:, f % 2, :], banks[:, 3 + f % 2, :], ACT.Gelu_apprx_tanh,
                                                 bias=fb1[:, f:f + 1], scale=1.0 / (AS * AS)).then_inc(s_fge, 1)
                            if nxt and f >= GT:
                                xhi(g + 1, f - GT)
                        act.wait_ge(s_fu2, FC * (g + 1))
                        wait(act, s_fv2, GT * g)
                        nc.scalar.copy(fq[:, 0, :], banks[:, 7, :]).then_inc(s_fqh, 1)
                    for j in range(GT):
                        xhi(0, j)
                    group_loop(act, body)

                @block.vector
                def _(dve):
                    with dve.Fori(0, T) as t:
                        nc.vector.bn_stats(fstats[:, bass.ds(t, 1), :].rearrange("p a b -> p (a b)"),
                                           x_res[:, bass.ds(t, 1), :].rearrange("p a b -> p (a b)")).then_inc(s_fbn, 1)
                    dve.wait_ge(s_fbn, T)
                    for t in range(T):
                        nc.vector.bn_aggr(fmv[:, t, :], fstats[:, t, :]).then_inc(s_fag, 1)
                    dve.wait_ge(s_fw, 4)
                    for n, (lo, r, hi) in enumerate(((U1s[:, 1], U1r, U1s[:, 0]), (V1s[:, 1], V1r, V1s[:, 0]),
                                                     (V2s[:, 1], V2r, V2s[:, 0]), (U2s[:, :, R:R2], U2r, U2s[:, :, 0:R]))):
                        nc.vector.scalar_tensor_tensor(out=lo, in0=r, scalar=AS, in1=hi, op0=ALU.mult,
                                                       op1=ALU.subtract).then_inc(s_fwl, 1)
                    nc.vector.tensor_scalar(b_row[:], b_row[:], gtanh[:, 3:4], None, ALU.mult).then_inc(s_fwl, 1)
                    dve.wait_ge(s_frs, 2)

                    def xn(g, j):
                        wait(dve, s_ftx, GT * g + j - 1)
                        nc.vector.tensor_scalar(fxn[:, j % 2, :], xtile(g, j), fmv[:, bass.ds(g * GT + j, 1), 0],
                                                frs[:, 0, bass.ds(g * GT + j, 1)], ALU.subtract, ALU.mult).then_inc(s_fxn, 1)

                    def xlo(g, j):
                        dve.wait_ge(s_fxh, GT * g + j + 1)
                        nc.vector.tensor_tensor(fxT[:, 1, :, j * P:(j + 1) * P], pFX[:, j % 2],
                                                fxT[:, 0, :, j * P:(j + 1) * P], ALU.subtract).then_inc(s_fxl, 1)

                    def residual(g, j):
                        dve.wait_ge(s_fv2, GT * g + j + 1)
                        dve.wait_ge(s_fba, GT * g + j + 1)
                        nc.vector.scalar_tensor_tensor(out=xtile(g, j), in0=banks[:, 5 + j % 2, 0:D],
                                                       scalar=gscale[:, 3:4], in1=xtile(g, j),
                                                       op0=ALU.mult, op1=ALU.add).then_inc(s_fep, 1)

                    def body(g, prev, nxt):
                        dve.wait_ge(s_fsh, g + 1)
                        nc.vector.tensor_tensor(rank_s[R:R2], banks[R:R2, 2, :], rank_s[R:R2], ALU.subtract).then_inc(s_fsl, 1)
                        if prev:
                            for j in range(GT):
                                residual(g - 1, j)
                        for f in range(FC):
                            if nxt and f >= GT - 1 and f - GT + 1 < GT:
                                xn(g + 1, f - GT + 1)
                            dve.wait_ge(s_fge, FC * g + f + 1)
                            wait(dve, s_fu2, FC * g + f - 3)
                            nc.vector.tensor_copy(fhh[:, f % 4, 0, :], fh[:, f % 2, :]).then_inc(s_fhi, 1)
                            dve.wait_ge(s_fhi, FC * g + f + 1)
                            nc.vector.tensor_tensor(fhh[:, f % 4, 1, :], fh[:, f % 2, :], fhh[:, f % 4, 0, :],
                                                    ALU.subtract).then_inc(s_flo, 1)
                            if nxt and f > GT:
                                xlo(g + 1, f - GT - 1)
                        if nxt:
                            xlo(g + 1, GT - 1)
                        dve.wait_ge(s_fqh, g + 1)
                        nc.vector.tensor_tensor(fq[:, 1, :], banks[:, 7, :], fq[:, 0, :], ALU.subtract).then_inc(s_fql, 1)
                    for j in range(GT):
                        xn(0, j)
                        if j:
                            xlo(0, j - 1)
                    xlo(0, GT - 1)
                    group_loop(dve, body)
                    for j in range(GT):
                        residual(NG - 1, j)

                @block.tensor
                def _(pe):
                    pe.wait_ge(s_fl, 9 * 16)
                    nc.tensor.transpose(banks[:, 2, 0:FC], fb1_rows[0:FC, :], ident[0:FC, 0:FC]).then_inc(s_fbt, 1)

                    def tx(g, j):
                        pe.wait_ge(s_fxn, GT * g + j + 1)
                        wait(pe, s_fxl, GT * g + j - 1)
                        for c in range(C):
                            last = nc.tensor.transpose(pFX[:, j % 2, c, :], fxn[:, j % 2, c * P:(c + 1) * P], ident[:])
                        last.then_inc(s_ftx, 1)

                    def up(g):
                        pe.wait_ge(s_fxl, GT * (g + 1))
                        wait(pe, s_fsl, g)
                        n = 0
                        for pw, px in ((0, 0), (0, 1), (1, 0)):
                            for c in range(C):
                                last = nc.tensor.matmul(banks[:, 2, :], U1s[:, pw, c, :], fxT[:, px, c, :],
                                                        start=(n == 0), stop=(n == 3 * C - 1))
                                n += 1
                        last.then_inc(s_fu1, 1)

                    def v1(g, f):
                        wait(pe, s_fge, FC * g + f - 1)
                        for part in range(2):
                            last = nc.tensor.matmul(banks[:, 3 + f % 2, :], V1s[:, part, f * P:(f + 1) * P], rank_s,
                                                    start=(part == 0), stop=(part == 1))
                        last.then_inc(s_fv1, 1)

                    def u2(g, f):
                        pe.wait_ge(s_flo, FC * g + f + 1)
                        if f == 0:
                            wait(pe, s_fql, g)
                        for part in range(2):
                            last = nc.tensor.matmul(banks[:, 7, :], U2s[:, f, :], fhh[:, f % 4, part, :],
                                                    start=(f == 0 and part == 0), stop=(f == FC - 1 and part == 1))
                        last.then_inc(s_fu2, 1)

                    def v2(g):
                        pe.wait_ge(s_fql, g + 1)
                        for j in range(GT):
                            wait(pe, s_fep, GT * g + j - 1)
                            for n, (pq, pw) in enumerate(((0, 0), (1, 0), (0, 1))):
                                last = nc.tensor.matmul(banks[:, 5 + j % 2, 0:D], fq[:, pq, j * P:(j + 1) * P],
                                                        V2s[:, pw, :], start=(n == 0), stop=(n == 2))
                            last.then_inc(s_fv2, 1)

                    def body(g, prev, nxt):
                        up(g)
                        if prev:
                            v2(g - 1)
                        pe.wait_ge(s_fsl, g + 1)
                        v1(g, 0)
                        for f in range(FC):
                            if f + 1 < FC:
                                v1(g, f + 1)
                            u2(g, f)
                            if nxt and f >= GT:
                                tx(g + 1, f - GT)
                    pe.wait_ge(s_fb, 1)
                    pe.wait_ge(s_fwl, 4)
                    for j in range(GT):
                        tx(0, j)
                    group_loop(pe, body)
                    v2(NG - 1)

        if stop >= 1:
            attention("xattn0", pieces0, lambda part, b, c: G0[:, part, b, c, :], 0,
                      1.0 / (HD0 ** 0.5 * AS), eps, False, False)

        if stop >= 2:
            gating()
            experts()
            fold_layer1()
            pieces1 = [(bank, 0, n * SK, tuple(range(C)), h0 * SK) for bank, (h0, n) in enumerate(((0, 6), (6, 6), (12, 4)))]
            attention("xattn1", pieces1, lambda part, b, c: G1[:, part, b, c, :], 2,
                      1.0 / (HD1 ** 0.5 * AS), eps2, True, True)

        if stop >= 4:
            low_rank_ffn()
            return
        with nc.Block() as block:
            @block.sync
            def _(sp):
                sp.wait_ge(s_x, 64)
                for b in range(B):
                    sp.dma_start(out[b].rearrange("(t p) d -> p t d", p=P), x_res[:, b * TB:(b + 1) * TB, :]).then_inc(s_out, 16)
                sp.wait_ge(s_out, 16 * B)


_NAMES = ["x", "ctx_1024", "g_xattn", "g_ffn", "L0_xattn_W_kv", "L0_xattn_b_kv", "L0_xattn_W_o", "L0_xattn_b_o",
          "L0_ffn_Wg", "L0_ffn_bg", "L0_ffn_W1", "L0_ffn_b1", "L0_ffn_W2", "L0_ffn_b2", "L1_xattn_ln_gamma",
          "L1_xattn_ln_beta", "L1_xattn_w_q", "L1_xattn_w_kv", "L1_xattn_w_out", "L1_xattn_b_out", "L1_xattn_gate",
          "L1_ffn_U1", "L1_ffn_V1", "L1_ffn_b1", "L1_ffn_U2", "L1_ffn_V2", "L1_ffn_b2"]


def kernel(**inputs):
    import numpy as _np
    import concourse.bacc as _bacc
    from concourse import mybir as _mybir
    from concourse.bass_utils import run_bass_kernel_spmd as _run

    nc = _bacc.Bacc("TRN2", target_bir_lowering=False, num_devices=1)
    arrays, aps = {}, {}
    for name in _NAMES:
        v = _np.ascontiguousarray(inputs[name])
        arrays[f"in_{name}"] = v
        aps[name] = nc.dram_tensor(f"in_{name}", v.shape, _mybir.dt.from_np(v.dtype), kind="ExternalInput").ap()
    out = nc.dram_tensor("out", inputs["x"].shape, _mybir.dt.float32, kind="ExternalOutput").ap()
    flamingo_kernel(nc, aps, out)
    r = _run(nc, [arrays], core_ids=[0])
    return r.results[0]["out"]
```

```python
from contextlib import ExitStack

import concourse.bass as bass
from concourse import mybir

F32 = mybir.dt.float32
F16 = mybir.dt.float16
I32 = mybir.dt.int32
ALU = mybir.AluOpType
ACT = mybir.ActivationFunctionType
AX = mybir.AxisListType.X

P = 128
BANK = 512


def wait(eng, sem, value):
    if not (isinstance(value, int) and value <= 0):
        eng.wait_ge(sem, value)


def flamingo_kernel(nc, a, out, stop=99):
    B, SQ, D = a["x"].shape
    _, SK, _ = a["ctx_1024"].shape
    C = D // P
    TB = SQ // P
    T = B * TB
    H = 16
    HD0 = D // H
    INNER = a["L1_xattn_w_q"].shape[1]
    HD1 = INNER // H
    E, _, F = a["L0_ffn_W1"].shape
    FC = F // P
    HK = H * SK
    J = -(-HK // P)
    HKP = J * P
    KB = B * SK
    R = a["L1_ffn_U1"].shape[1]
    EPS = 1e-5
    NCOL = T * E
    TT = 2 * P
    NT = 2 * B * SQ // TT + E - 1
    NH = 2 * (NT + 2)
    HEADS_OF_BANK = [6, 6, 4]
    WS = 64.0
    AS = 16.0
    PS = 256.0

    ctx = ExitStack()
    with ctx:
        def sb(name, shape, dt=F32):
            return ctx.enter_context(nc.sbuf_tensor(name, shape, dt))

        def sem(name):
            return ctx.enter_context(nc.semaphore(name))

        def view(arena, word, shape, dt=F32):
            n = 1
            for s in shape:
                n *= s
            words = n if dt in (F32, I32) else n // 2
            v = arena[:, word:word + words]
            if dt != F32:
                v = v.bitcast(dt)
            if len(shape) == 2:
                v = v.rearrange("p (a b) -> p a b", a=shape[0])
            elif len(shape) == 3:
                v = v.rearrange("p (a b c) -> p a b c", a=shape[0], b=shape[1])
            elif len(shape) == 4:
                v = v.rearrange("p (a b c d) -> p a b c d", a=shape[0], b=shape[1], c=shape[2])
            return v

        x_res = sb("x_res", [P, T, D])
        region_a = sb("region_a", [P, 16384])
        region_b = sb("region_b", [P, 16384])
        work = sb("work", [P, 6750])
        ident = sb("ident", [P, P])
        ident16 = sb("ident16", [P, P], F16)
        b_row = sb("b_row", [P, D])
        gates = sb("gates", [P, 5])
        gtanh = sb("gtanh", [P, 5])
        gscale = sb("gscale", [P, 4])
        small = sb("small", [P, 48])
        mv = sb("mv", [P, 2, 2])
        bst = sb("bst", [P, 2, 6])
        rstd = sb("rstd", [P, 2, 2])
        smax = sb("smax", [P, 2, H])
        ssum = sb("ssum", [P, 2, H])
        srec = sb("srec", [P, 2, H])
        nmax = sb("nmax", [P, 2, H])
        slot_token = sb("slot_token", [P, NH], I32)
        tile_expert = sb("tile_expert", [1, NT], I32)
        pos = sb("pos", [P, 2, T], I32)
        topw = sb("topw", [P, 2, T])
        idx_now = sb("idx_now", [P, 2], I32)
        idx_ring = sb("idx_ring", [P, 2, 2], I32)
        b1_cols = sb("b1_cols", [P, E, FC])
        half = small[:, 0:1]
        eps = small[:, 1:2]
        eps2 = small[:, 2:3]

        banks = ctx.enter_context(nc.psum_tensor("banks", [P, 8, BANK], F32))

        xs = nc.dram_tensor("xs", (B * SQ, 2 * D), F16, kind="Internal").ap()
        ys = nc.dram_tensor("ys", (NT * TT, D), F32, kind="Internal").ap()

        def hk_banks(ap):
            return [(12, ap[:, 0:2, 0:6 * SK].rearrange("p b (h k) -> p b h k", h=6), 0),
                    (4, ap[:, 2, 0:4 * SK].rearrange("p (h k) -> p h k", h=4), 12)]

        G0 = view(region_b, 0, [2, B, C, (H // C) * SK], F16)
        vw_word = B * C * (H // C) * SK
        VW = view(region_b, vw_word, [2, B, J, D], F16)
        ctx_sb = view(region_a, 0, [B, D])
        wkv0 = view(region_a, 1024, [C, 2 * D])
        wo0 = view(region_a, 2048, [C, D])
        ctxT = view(region_a, 2560, [C, KB])
        kT0 = view(region_a, 3200, [2, C, KB], F16)
        vT0 = view(region_a, 4500, [C, KB])
        W0 = (H // C) * SK
        VB0 = view(region_a, 5200, [P + 2 * (W0 + P)])
        bkv = view(region_a, 7000, [2 * D])
        ones = view(region_a, 7600, [KB])
        wkv0s = view(region_a, 8100, [C, 2, D])
        bkvs = view(region_a, 9200, [2, D])
        mask = view(region_a, 8000, [H // C])
        mask16 = view(region_a, 8010, [H // C], F16)
        S = view(work, 0, [2, HKP])
        PT = view(work, 2 * HKP, [2, 2, J, P], F16)
        xnb = view(work, 4 * HKP, [2, D])
        xT = view(work, 4 * HKP + 2 * D, [2, 2, C, P], F16)

        s_c = sem("consts")
        s_x = sem("x_loaded")
        s_w = sem("setup_weights_loaded")
        s_ws = sem("kv_weights_sorted")
        s_ct = sem("ctx_transposed")
        s_ctc = sem("ctx_transpose_copied")
        s_kv = sem("kv_projected")
        s_kh = sem("k_hi")
        s_kl = sem("kv_copied")
        s_vb = sem("v_spread")
        s_g0 = sem("k_spread_hi")
        s_g0l = sem("k_spread_lo")
        s_vw = sem("vw_done")
        s_vh = sem("vw_hi")
        s_vl = sem("vw_lo")
        s_gt = sem("gates_tanh")
        s_gs = sem("gates_scaled")
        VGROUPS = [(0, 4), (4, 8), (8, J)]

        def vw_chunks(width, n, j):
            return [(k, P + k * (width + P) + P * j - k * width) for k in range(n)
                    if P * j + P > k * width and P * j < (k + 1) * width]

        def vw_product(pe, b, vb, width, n, w_out, before):
            for g, (j0, j1) in enumerate(VGROUPS):
                at = len(VGROUPS) * b + g
                wait(pe, s_vl if before else s_vl, vw_base[0] + at - 1)
                wait(pe, s_vh, vw_base[0] + at - 1)
                for j in range(j0, j1):
                    parts = vw_chunks(width, n, j)
                    o = banks[:, 4 + 2 * (at % 2) + (j - j0) // 2, (j - j0) % 2 * D:(j - j0) % 2 * D + D]
                    for i, (k, start) in enumerate(parts):
                        last = nc.tensor.matmul(o, vb[:, start:start + P], w_out[:, k, :],
                                                start=(i == 0), stop=(i == len(parts) - 1))
                last.then_inc(s_vw, 1)

        def vw_hi(act, b):
            for g, (j0, j1) in enumerate(VGROUPS):
                at = len(VGROUPS) * b + g
                act.wait_ge(s_vw, vw_base[0] + at + 1)
                src = banks[:, 4 + 2 * (at % 2):4 + 2 * (at % 2) + (j1 - j0) // 2, :]
                nc.scalar.activation(VW[:, 0, b, j0:j1, :].rearrange("p (a b) n -> p a (b n)", b=2), src,
                                     ACT.Copy, scale=AS).then_inc(s_vh, 1)

        def vw_lo(dve, b):
            for g, (j0, j1) in enumerate(VGROUPS):
                at = len(VGROUPS) * b + g
                dve.wait_ge(s_vh, vw_base[0] + at + 1)
                src = banks[:, 4 + 2 * (at % 2):4 + 2 * (at % 2) + (j1 - j0) // 2, :]
                nc.vector.scalar_tensor_tensor(
                    out=VW[:, 1, b, j0:j1, :].rearrange("p (a b) n -> p a (b n)", b=2), in0=src, scalar=AS,
                    in1=VW[:, 0, b, j0:j1, :].rearrange("p (a b) n -> p a (b n)", b=2),
                    op0=ALU.mult, op1=ALU.subtract).then_inc(s_vl, 1)

        vw_base = [0]

        with nc.Block() as block:
            @block.sync
            def _(sp):
                sp.dma_start(ctx_sb[0:SK], a["ctx_1024"].rearrange("b k d -> k b d")).then_inc(s_w, 16)
                sp.dma_start(wkv0, a["L0_xattn_W_kv"].rearrange("(c p) n -> p c n", p=P)).then_inc(s_w, 16)
                sp.dma_start(wo0, a["L0_xattn_W_o"].rearrange("(c p) n -> p c n", p=P)).then_inc(s_w, 16)
                sp.dma_start(bkv[0:1], a["L0_xattn_b_kv"].rearrange("(a n) -> a n", a=1)).then_inc(s_w, 16)
                sp.dma_start(b_row[:], a["L0_xattn_b_o"].rearrange("(a n) -> a n", a=1).to_broadcast([P, D])).then_inc(s_w, 16)
                for lo, name in ((0, "g_xattn"), (2, "g_ffn"), (4, "L1_xattn_gate")):
                    n = a[name].shape[0]
                    sp.dma_start(gates[:, lo:lo + n], a[name].rearrange("(a n) -> a n", a=1).to_broadcast([P, n])).then_inc(s_w, 16)
                for b in range(B):
                    sp.dma_start(x_res[:, b * TB:(b + 1) * TB, :],
                                 a["x"][b].rearrange("(t p) d -> p t d", p=P)).then_inc(s_x, 16)

            @block.gpsimd
            def _(pool):
                nc.gpsimd.memset(ident[:], 0.0).then_inc(s_c, 1)
                nc.gpsimd.memset(mask, 1.0).then_inc(s_c, 1)
                nc.gpsimd.memset(ones, 1.0).then_inc(s_c, 1)
                nc.gpsimd.memset(VB0, 0.0).then_inc(s_c, 1)
                nc.gpsimd.memset(S[:, :, HK:HKP], 0.0).then_inc(s_c, 1)
                nc.gpsimd.memset(half, -0.5).then_inc(s_c, 1)
                nc.gpsimd.memset(eps, EPS).then_inc(s_c, 1)
                nc.gpsimd.memset(eps2, EPS * EPS / (1.0 + EPS)).then_inc(s_c, 1)
                pool.wait_ge(s_c, 8)
                nc.gpsimd.affine_select(out=ident[:], in_=ident[:], compare_op=ALU.not_equal, fill=1.0, base=0,
                                        pattern=[[-1, P]], channel_multiplier=1).then_inc(s_c, 1)
                nc.gpsimd.affine_select(out=mask, in_=mask, compare_op=ALU.is_ge, fill=0.0, base=0,
                                        pattern=[[-HD0, H // C]], channel_multiplier=1).then_inc(s_c, 1)
                pool.wait_ge(s_c, 10)
                nc.gpsimd.affine_select(out=mask, in_=mask, compare_op=ALU.is_ge, fill=0.0, base=HD0 - 1,
                                        pattern=[[HD0, H // C]], channel_multiplier=-1).then_inc(s_c, 1)
                nc.gpsimd.tensor_copy(ident16[:], ident[:]).then_inc(s_c, 1)
                pool.wait_ge(s_c, 12)
                nc.gpsimd.tensor_copy(mask16, mask).then_inc(s_c, 1)
                pool.wait_ge(s_c, 13)
                pool.wait_ge(s_kh, 1)
                for b in range(B):
                    for c in range(C):
                        nc.gpsimd.tensor_tensor(
                            G0[:, 0, b, c, :].rearrange("p (h k) -> p h k", k=SK),
                            kT0[:, 0, c, b * SK:(b + 1) * SK].unsqueeze(1).to_broadcast([P, H // C, SK]),
                            mask16.unsqueeze(2).to_broadcast([P, H // C, SK]), ALU.mult).then_inc(s_g0, 1)

            @block.scalar
            def _(act):
                act.wait_ge(s_w, 8 * 16)
                nc.scalar.activation(gtanh[:], gates[:], ACT.Tanh).then_inc(s_gt, 1)
                act.wait_ge(s_ct, 1)
                nc.scalar.copy(ctxT, banks[:, 0:2, 0:KB]).then_inc(s_ctc, 1)
                act.wait_ge(s_kv, 1)
                nc.scalar.activation(kT0[:, 0], banks[:, 0:2, 0:KB], ACT.Copy, scale=AS).then_inc(s_kh, 1)
                nc.scalar.copy(vT0, banks[:, 2:4, 0:KB]).then_inc(s_kl, 1)
                for b in range(B):
                    vw_hi(act, b)

            @block.tensor
            def _(pe):
                pe.wait_ge(s_w, 8 * 16)
                pe.wait_ge(s_c, 9)
                for c in range(C):
                    for b in range(B):
                        last = nc.tensor.transpose(banks[:, c, b * SK:(b + 1) * SK],
                                                   ctx_sb[0:SK, b, c * P:(c + 1) * P], ident[0:SK, 0:SK])
                last.then_inc(s_ct, 1)
                pe.wait_ge(s_ctc, 1)
                pe.wait_ge(s_ws, C + 1)
                for s in range(2):
                    for g in range(C):
                        o = banks[:, 2 * s + g, 0:KB]
                        for c in range(C):
                            nc.tensor.matmul(o, wkv0s[:, c, s, g * P:(g + 1) * P], ctxT[:, c, :], start=(c == 0), stop=False)
                        last = nc.tensor.matmul(o, bkvs[0:1, s, g * P:(g + 1) * P], ones[0:1, :], start=False, stop=True)
                last.then_inc(s_kv, 1)
                for b in range(B):
                    pe.wait_ge(s_vb, C * (b + 1))
                    vw_product(pe, b, VB0, W0, C, wo0, None)

            @block.vector
            def _(dve):
                dve.wait_ge(s_w, 8 * 16)
                for c in range(C):
                    nc.vector.tensor_copy(wkv0s[:, c].rearrange("p s (h d) -> p s h d", d=HD0),
                                          wkv0[:, c].rearrange("p (h s d) -> p s h d", s=2, d=HD0)).then_inc(s_ws, 1)
                nc.vector.tensor_copy(bkvs[0:1].rearrange("p s (h d) -> p s h d", d=HD0),
                                      bkv[0:1].rearrange("p (h s d) -> p s h d", s=2, d=HD0)).then_inc(s_ws, 1)
                dve.wait_ge(s_gt, 1)
                nc.vector.tensor_scalar(gscale[:, 0:1], gtanh[:, 0:1], 1.0 / (AS * PS), None, ALU.mult).then_inc(s_gs, 1)
                nc.vector.tensor_copy(gscale[:, 1:2], gtanh[:, 2:3]).then_inc(s_gs, 1)
                nc.vector.tensor_scalar(gscale[:, 2:3], gtanh[:, 1:2], gtanh[:, 4:5], 1.0 / (AS * PS), ALU.mult, ALU.mult).then_inc(s_gs, 1)
                nc.vector.tensor_scalar(gscale[:, 3:4], gtanh[:, 3:4], 1.0 / (AS * AS), None, ALU.mult).then_inc(s_gs, 1)
                nc.vector.tensor_scalar(b_row[:], b_row[:], gtanh[:, 0:1], None, ALU.mult).then_inc(s_gs, 1)
                dve.wait_ge(s_kh, 1)
                dve.wait_ge(s_kl, 1)
                nc.vector.scalar_tensor_tensor(out=kT0[:, 1], in0=banks[:, 0:2, 0:KB], scalar=AS, in1=kT0[:, 0],
                                               op0=ALU.mult, op1=ALU.subtract).then_inc(s_kl, 1)
                dve.wait_ge(s_kl, 2)
                dve.wait_ge(s_c, 13)
                for b in range(B):
                    wait(dve, s_vw, len(VGROUPS) * b)
                    for c in range(C):
                        o = P + c * (W0 + P)
                        nc.vector.tensor_tensor(
                            VB0[:, o:o + W0].rearrange("p (h k) -> p h k", k=SK),
                            vT0[:, c, b * SK:(b + 1) * SK].unsqueeze(1).to_broadcast([P, H // C, SK]),
                            mask.unsqueeze(2).to_broadcast([P, H // C, SK]), ALU.mult).then_inc(s_vb, 1)
                    for c in range(C):
                        nc.vector.tensor_tensor(
                            G0[:, 1, b, c, :].rearrange("p (h k) -> p h k", k=SK),
                            kT0[:, 1, c, b * SK:(b + 1) * SK].unsqueeze(1).to_broadcast([P, H // C, SK]),
                            mask16.unsqueeze(2).to_broadcast([P, H // C, SK]), ALU.mult).then_inc(s_g0l, 1)
                    vw_lo(dve, b)

        def attention(name, pieces, Gof, layer, softmax_scale, ln_eps, affine, combine):
            stats_done = sem(name + "_stats")
            rstd_done = sem(name + "_rstd")
            xn_done = sem(name + "_xn")
            xin_done = sem(name + "_xn_ready")
            bias_done = sem(name + "_bias_added")
            tx_done = sem(name + "_x_transposed")
            xhi_done = sem(name + "_x_hi")
            xlo_done = sem(name + "_x_lo")
            sc_done = sem(name + "_scores")
            max_done = sem(name + "_max")
            nmax_done = sem(name + "_scaled_max")
            exp_done = sem(name + "_exp")
            sum_done = sem(name + "_sum")
            rec_done = sem(name + "_recip")
            nrm_done = sem(name + "_normalised")
            tp_done = sem(name + "_p_transposed")
            phi_done = sem(name + "_p_hi")
            plo_done = sem(name + "_p_lo")
            pv_done = sem(name + "_pv")
            epi_done = sem(name + "_residual")
            bn_done = sem(name + "_bn")
            eps_done = sem(name + "_eps")
            if combine:
                idx_done = sem(name + "_idx")
                got = [sem(name + "_rows_0"), sem(name + "_rows_1")]
                comb_a = sem(name + "_first_expert_added")
                comb_done = sem(name + "_experts_added")
            pX = banks[:, 0, 0:C * P].rearrange("p (c n) -> p c n", c=C)
            pS = banks[:, 1:4, :]
            pT = banks[:, 4:7, :].rearrange("p a b -> p (a b)")[:, 0:HKP]
            pO = banks[:, 7, 0:D]
            per = 2 if affine else 1

            def tile(t):
                return x_res[:, bass.ds(t, 1), :].rearrange("p a d -> p (a d)")

            HEADS = (6, 6, 4)
            BEHIND = (6, 12, 16)
            FIRST, LAST = -5 if combine else -4, T + 2
            LO, HI = 4, T - 6 if combine else T - 4

            def ok(t):
                return not isinstance(t, int) or 0 <= t < T

            def drive(eng, step):
                for s in range(FIRST, LO):
                    step(s, s % 2, s // 2)
                with eng.Fori(0, (HI - LO) // 2) as i:
                    for k in range(2):
                        step(2 * i + (LO + k), k, i + LO // 2)
                for s in range(HI, LAST + 1):
                    step(s, s % 2, s // 2)

            with nc.Block() as block:
                @block.sync
                def _(sp):
                    if layer == 0:
                        w1_loads(sp)
                    else:
                        ffn_loads(sp)

                @block.vector
                def _(dve):
                    def maximum(t, par, b):
                        h0, n = BEHIND[b] - HEADS[b], HEADS[b]
                        dve.wait_ge(sc_done, 3 * t + (b + 1))
                        nc.vector.tensor_reduce(smax[:, par, h0:h0 + n],
                                                pS[:, b, 0:n * SK].rearrange("p (h k) -> p h k", h=n),
                                                AX, ALU.max).then_inc(max_done, 1)

                    def scaled_maximum(t, par, b):
                        heads = slice(BEHIND[b] - HEADS[b], BEHIND[b])
                        dve.wait_ge(max_done, 3 * t + (b + 1))
                        nc.vector.tensor_scalar(nmax[:, par, heads], smax[:, par, heads], -softmax_scale, None,
                                                ALU.mult).then_inc(nmax_done, 1)

                    def add_expert(t, k):
                        dve.wait_ge(got[k], 16 * (t + 1))
                        if k:
                            dve.wait_ge(comb_a, t + 1)
                        nc.vector.scalar_tensor_tensor(
                            out=tile(t), in0=yrows[:, k, :], scalar=topw[:, k, bass.ds(t, 1)],
                            in1=tile(t), op0=ALU.mult, op1=ALU.add).then_inc(comb_done if k else comb_a, 1)

                    def step(s, par, half_s):
                        odd = 1 - par
                        if combine and ok(s + 4):
                            add_expert(s + 4, 0)
                        if ok(s + 3):
                            t = s + 3
                            dve.wait_ge(rstd_done, t + 1)
                            wait(dve, tx_done, t - 1)
                            nc.vector.tensor_scalar(xnb[:, odd, :], tile(t), mv[:, odd, 0:1], rstd[:, odd, 0:1],
                                                    ALU.subtract, ALU.mult).then_inc(xn_done, 1)
                        if combine and ok(s + 4):
                            add_expert(s + 4, 1)
                            dve.wait_ge(comb_done, s + 5)
                        if ok(s - 2):
                            t = s - 2
                            dve.wait_ge(phi_done, t + 1)
                            nc.vector.scalar_tensor_tensor(
                                out=PT[:, par, 1].rearrange("p j n -> p (j n)"), in0=pT, scalar=PS,
                                in1=PT[:, par, 0].rearrange("p j n -> p (j n)"),
                                op0=ALU.mult, op1=ALU.subtract).then_inc(plo_done, 1)
                        if ok(s + 4):
                            wait(dve, stats_done, s + 3)
                        if ok(s - 3):
                            t = s - 3
                            dve.wait_ge(pv_done, t + 1)
                            dve.wait_ge(bias_done, t + 1)
                            nc.vector.scalar_tensor_tensor(out=tile(t), in0=pO, scalar=gscale[:, layer:layer + 1],
                                                           in1=tile(t), op0=ALU.mult, op1=ALU.add).then_inc(epi_done, 1)
                        if ok(s + 4):
                            nc.vector.bn_stats(bst[:, par, :], tile(s + 4)).then_inc(bn_done, 1)
                            dve.wait_ge(bn_done, s + 5)
                        if ok(s + 1):
                            maximum(s + 1, odd, 0)
                        if ok(s + 4):
                            nc.vector.bn_aggr(mv[:, par, :], bst[:, par, :]).then_inc(stats_done, 1)
                        if ok(s + 1):
                            maximum(s + 1, odd, 1)
                            for b in range(2):
                                scaled_maximum(s + 1, odd, b)
                        if ok(s):
                            dve.wait_ge(exp_done, H * (s + 1))
                            nc.vector.tensor_reduce(ssum[:, par, :], S[:, par, 0:HK].rearrange("p (h k) -> p h k", k=SK),
                                                    AX, ALU.add).then_inc(sum_done, 1)
                            dve.wait_ge(sum_done, s + 1)
                            wait(dve, nrm_done, s - 1)
                            nc.vector.reciprocal(srec[:, par, :], ssum[:, par, :]).then_inc(rec_done, 1)
                        if ok(s + 1):
                            maximum(s + 1, odd, 2)
                            scaled_maximum(s + 1, odd, 2)
                        if ok(s + 2):
                            t = s + 2
                            dve.wait_ge(xhi_done, t + 1)
                            nc.vector.tensor_tensor(xT[:, par, 1], pX, xT[:, par, 0], ALU.subtract).then_inc(xlo_done, 1)
                    if layer == 0:
                        dve.wait_ge(s_x, 16 * B)
                    drive(dve, step)

                @block.scalar
                def _(act):
                    def step(s, par, half_s):
                        if ok(s):
                            wait(act, tp_done, s - 1)
                            for h in range(H):
                                b, at = h // 6, h % 6 * SK
                                if at == 0:
                                    act.wait_ge(nmax_done, 3 * s + (b + 1))
                                nc.scalar.activation(S[:, par, h * SK:(h + 1) * SK], pS[:, b, at:at + SK], ACT.Exp,
                                                     bias=nmax[:, par, h:h + 1], scale=softmax_scale).then_inc(exp_done, 1)
                            if layer == 0:
                                w1_hi(act, s, par, half_s)
                        if ok(s - 1):
                            t, q = s - 1, 1 - par
                            act.wait_ge(tp_done, t + 1)
                            wait(act, pv_done, t - 1)
                            nc.scalar.activation(PT[:, q, 0].rearrange("p j n -> p (j n)"), pT, ACT.Copy,
                                                 scale=PS).then_inc(phi_done, 1)
                        if ok(s + 2):
                            t = s + 2
                            act.wait_ge(tx_done, t + 1)
                            wait(act, sc_done, 3 * (t - 1))
                            nc.scalar.copy(xT[:, par, 0], pX).then_inc(xhi_done, 1)
                    drive(act, step)

                @block.gpsimd
                def _(pool):
                    def index(t):
                        wait(pool, comb_done, t)
                        nc.gpsimd.tensor_copy(idx_now[:], pos[:, :, bass.ds(t, 1)].rearrange("p a b -> p (a b)")).then_inc(idx_done, 1)

                    def gather(t):
                        for k in range(2):
                            nc.gpsimd.indirect_dma_start(yrows[:, k, :], None, ys, bass.IndirectOffsetOnAxis(
                                ap=idx_now[:, k:k + 1], axis=0)).then_inc(got[k], 16)

                    def step(s, par, half_s):
                        odd = 1 - par
                        if combine and ok(s + 5):
                            index(s + 5)
                            pool.wait_ge(idx_done, s + 6)
                        if ok(s + 3):
                            t = s + 3
                            pool.wait_ge(xn_done, t + 1)
                            if affine:
                                nc.gpsimd.tensor_tensor(xnb[:, odd, :], xnb[:, odd, :], ln_gamma, ALU.mult).then_inc(xin_done, 1)
                            nc.gpsimd.tensor_tensor(tile(t), tile(t), b_row[:], ALU.add).then_inc(bias_done, 1)
                        if combine and ok(s + 5):
                            gather(s + 5)
                        if affine and ok(s + 3):
                            pool.wait_ge(xin_done, 2 * (s + 3) + 1)
                            nc.gpsimd.tensor_tensor(xnb[:, odd, :], xnb[:, odd, :], ln_beta, ALU.add).then_inc(xin_done, 1)
                        if ok(s + 4):
                            t = s + 4
                            pool.wait_ge(stats_done, t + 1)
                            wait(pool, xn_done, t - 1)
                            nc.gpsimd.tensor_tensor(rstd[:, par, 1:2], mv[:, par, 1:2], ln_eps, ALU.add).then_inc(eps_done, 1)
                            pool.wait_ge(eps_done, t + 1)
                            nc.gpsimd.tensor_tensor(rstd[:, par, 0:1], rstd[:, par, 1:2], half, ALU.pow).then_inc(rstd_done, 1)
                        if layer == 0 and ok(s):
                            w1_lo(pool, s)
                        if ok(s):
                            pool.wait_ge(rec_done, s + 1)
                            z = S[:, par, 0:HK].rearrange("p (h k) -> p h k", k=SK)
                            nc.gpsimd.tensor_tensor(z, z, srec[:, par, :].unsqueeze(2).to_broadcast([P, H, SK]),
                                                    ALU.mult).then_inc(nrm_done, 1)
                    drive(pool, step)

                @block.tensor
                def _(pe):
                    def scores(t, par, b, batch):
                        wait(pe, exp_done, H * (t - 1) + BEHIND[b])
                        for bank, o0, o1, c, g0 in pieces:
                            if bank != b:
                                continue
                            cs = c if isinstance(c, tuple) else (c,)
                            n = 0
                            for cc in cs:
                                for px, pg in ((0, 0), (1, 0), (0, 1)):
                                    last = nc.tensor.matmul(
                                        banks[:, 1 + bank, o0:o1], xT[:, par, px, cc, :], Gof(pg, batch, cc)[:, g0:g0 + o1 - o0],
                                        start=(n == 0), stop=(n == 3 * len(cs) - 1))
                                    n += 1
                        last.then_inc(sc_done, 1)

                    def step(s, par, b1, b2):
                        odd = 1 - par
                        if ok(s + 1):
                            pe.wait_ge(xlo_done, s + 2)
                            scores(s + 1, odd, 0, b1)
                            scores(s + 1, odd, 1, b1)
                        if ok(s - 1):
                            t = s - 1
                            pe.wait_ge(nrm_done, t + 1)
                            wait(pe, plo_done, t)
                            for j in range(J):
                                last = nc.tensor.transpose(pT[:, j * P:(j + 1) * P], S[:, odd, j * P:(j + 1) * P], ident[:])
                            last.then_inc(tp_done, 1)
                        if ok(s + 1):
                            scores(s + 1, odd, 2, b1)
                        if ok(s + 2):
                            t = s + 2
                            pe.wait_ge(xin_done if affine else xn_done, per * (t + 1))
                            wait(pe, xlo_done, t)
                            for c in range(C):
                                last = nc.tensor.transpose(pX[:, c, :], xnb[:, par, c * P:(c + 1) * P], ident[:])
                            last.then_inc(tx_done, 1)
                        if ok(s - 2):
                            t = s - 2
                            pe.wait_ge(plo_done, t + 1)
                            wait(pe, epi_done, t)
                            n = 0
                            for pp, pv in ((0, 0), (1, 0), (0, 1)):
                                for j in range(J):
                                    last = nc.tensor.matmul(pO, PT[:, par, pp, j, :], VW[:, pv, b2, j, :],
                                                            start=(n == 0), stop=(n == 3 * J - 1))
                                    n += 1
                            last.then_inc(pv_done, 1)

                    def batches(s):
                        return min(max(s + 1, 0), T - 1) // TB, min(max(s - 2, 0), T - 1) // TB

                    s = FIRST
                    while s <= LAST:
                        n = 0
                        while LO <= s and s + n + 1 <= T - 3 and batches(s) == batches(s + n + 1):
                            n += 1
                        if n >= 3:
                            n = (n + 1) // 2
                            with pe.Fori(0, n) as i:
                                for k in range(2):
                                    step(2 * i + (s + k), (s + k) % 2, *batches(s))
                            s += 2 * n
                        else:
                            step(s, s % 2, *batches(s))
                            s += 1

        pieces0 = []
        for bank, (h0, n) in enumerate(((0, 6), (6, 6), (12, 4))):
            for c in range(C):
                lo, hi = max(h0, c * H // C), min(h0 + n, (c + 1) * H // C)
                if lo < hi:
                    pieces0.append((bank, (lo - h0) * SK, (hi - h0) * SK, c, (lo - c * H // C) * SK))
        TE = [P, T, E]
        WW = C * F
        Q1, Q2 = F // 2, WW // 2
        N1, N2 = E * WW // Q1, E * WW // Q2
        wA = view(region_a, 0, [E, 2 * WW], F16)
        wB = view(region_b, 0, [E, 2 * WW], F16)
        piece_a32, piece_a16 = view(region_a, 0, [N1, Q1]), view(region_a, 0, [N1, 2, Q1], F16)
        piece_b32, piece_b16 = view(region_b, 0, [N2, Q2]), view(region_b, 0, [N2, 2, Q2], F16)
        raw_last1 = view(work, 4 * HKP + 2 * D + 2 * C * P, [Q1])
        raw_last2 = view(work, 0, [2, Q2])
        GT = 4
        NG = T // GT
        g_o = 5 * WW
        xn_g = view(region_b, g_o, [2, GT, D])
        xs_g = view(region_b, g_o + 2 * GT * D, [2, GT, 2, D], F16)
        xT_g = view(region_b, g_o + 4 * GT * D, [2, 2, C, 2 * P])
        w_o = WW
        stats = view(work, w_o, [T, 6])
        mv_all = view(work, w_o + 192, [T, 2])
        rs_all = view(work, w_o + 256, [2, T])
        r_o = w_o + 320
        wg = view(work, r_o, [C, E])
        bg = view(work, r_o + 16, [E])
        iota_e = view(work, r_o + 24, [E])
        b1_rows = view(work, r_o + 32, [P])
        tri = view(work, r_o + 160, [P], F16)
        ones16 = view(work, r_o + 224, [P], F16)
        logits = view(work, r_o + 288, [T, E])
        q_o = r_o + 288 + NCOL
        oh = [view(work, q_o, [T, E]), view(work, q_o + NCOL, [T, E])]
        tmp = view(work, q_o + 2 * NCOL, [T, E])
        sel16 = view(work, q_o + 3 * NCOL, [T, E], F16)
        i_o = q_o + 3 * NCOL + NCOL // 2
        incl = view(work, i_o, [E, T])
        top_v = view(work, i_o + NCOL, [6, T])
        c_o = i_o + NCOL + 6 * T
        iota_lo = view(work, c_o, [P], F16)
        iota_hi = view(work, c_o + 64, [NH], F16)
        token = view(work, c_o + 64 + NH // 2, [T])
        HOTS = 8
        h_o = c_o + 64 + NH // 2 + T
        oh_lo = view(work, h_o, [HOTS, P], F16)
        oh_hi = view(work, h_o + HOTS * P // 2, [HOTS, NH], F16)
        p_o = h_o + HOTS * (P + NH) // 2
        pos_f = view(work, p_o, [2, T])
        lohi_i = view(work, p_o + 2 * T, [2, 2 * T], I32)
        lohi = view(work, p_o + 6 * T, [2, 2 * T])
        t_o = p_o + 10 * T
        tiles_i = view(work, t_o, [2, E], I32)
        tiles_f = view(work, t_o + 2 * E, [3, E])
        iota_tile = view(work, t_o + 5 * E, [NT])
        tile_cmp = view(work, t_o + 5 * E + NT, [NT, E])
        ones_t = view(work, t_o + 5 * E + NT * (E + 1), [T])
        te_f = view(work, t_o + 5 * E + NT * (E + 1) + T, [NT])
        slot_f = view(work, t_o + 5 * E + NT * (E + 2) + T, [NH])
        assert T * P <= 4096 and NH % 2 == 0 and HOTS == 2 * GT
        assert t_o + 5 * E + NT * (E + 2) + T + NH <= 6750

        s_w1 = [sem("w1_pieces_loaded_0"), sem("w1_pieces_loaded_1")]
        s_w2 = [sem("w2_first_loaded"), sem("w2_rest_loaded")]
        s_w1h = sem("w1_hi")
        s_w1l = sem("w1_lo")
        s_whi = sem("w2_hi")
        s_wlo = sem("w2_lo")
        s_wld = sem("w2_lo_last")
        s_gl = sem("gate_inputs_loaded")
        s_gc = sem("gate_consts")
        s_b1t = sem("b1_transposed")
        s_b1 = sem("b1_columns")
        s_bn = sem("gate_bn")
        s_ag = sem("gate_bn_aggr")
        s_rs = sem("gate_rstd")
        s_xn = sem("gate_xn")
        s_xh = sem("gate_x_hi")
        s_xl = sem("gate_x_lo")
        s_tx = sem("gate_x_transposed")
        s_tc = sem("gate_x_transpose_copied")
        s_lg = sem("gate_logits")
        s_st = [sem("xs_written_0"), sem("xs_written_1")]
        s_r = sem("routing_step")
        s_se = sem("selected")
        s_ex = sem("gate_exp")
        s_pf = sem("prefix_counts")
        s_hot = sem("one_hots")
        s_hm = sem("one_hots_used")
        s_slot = sem("slot_table")

        def w1_loads(sp):
            rows = a["L0_ffn_W1"].rearrange("e (c p) (h n) -> p (e c) h n", p=P, h=2)

            def load(i, par, dst):
                wait(sp, s_w1[par], 16 * i)
                sp.dma_start(dst, rows[:, bass.ds(i, 1), par, :].rearrange("p a n -> p (a n)")).then_inc(s_w1[par], 16)

            def place(i, par):
                return piece_a32[:, bass.ds(2 * i + (par + 1), 1), :].rearrange("p a n -> p (a n)")
            for par in range(2):
                load(0, par, place(0, par))
            with sp.Fori(1, N1 // 2 - 1) as i:
                for par in range(2):
                    load(i, par, place(i, par))
            load(N1 // 2 - 1, 0, place(N1 // 2 - 1, 0))
            load(N1 // 2 - 1, 1, raw_last1)

        def w1_piece(q):
            raw = (raw_last1 if isinstance(q, int) and q == N1 - 1 else
                   piece_a32[:, bass.ds(q + 1, 1), :].rearrange("p a n -> p (a n)"))
            return [raw] + [piece_a16[:, bass.ds(q, 1), part, :].rearrange("p a n -> p (a n)") for part in range(2)]

        def w1_hi(act, q, par, half_q):
            raw, hi, _ = w1_piece(q)
            act.wait_ge(s_w1[par], 16 * half_q + 16)
            wait(act, s_w1l, q)
            nc.scalar.activation(hi, raw, ACT.Copy, scale=WS).then_inc(s_w1h, 1)
            nc.scalar.activation(raw, raw, ACT.Copy, scale=WS).then_inc(s_w1h, 1)

        def w1_lo(pool, q):
            raw, hi, lo = w1_piece(q)
            pool.wait_ge(s_w1h, 2 * q + 2)
            nc.gpsimd.tensor_tensor(lo, raw, hi, ALU.subtract).then_inc(s_w1l, 1)

        def w2_loads(sp, experts, last, s_loaded):
            for e in experts:
                sp.dma_start(piece_b32[:, 2 * e + 2:2 * e + 4, :].rearrange("p a (f n) -> p (a f) n", n=D),
                             a["L0_ffn_W2"][e].rearrange("(f p) n -> p f n", p=P)).then_inc(s_loaded, 16)
            if last:
                sp.dma_start(raw_last2.rearrange("p a (f n) -> p (a f) n", n=D),
                             a["L0_ffn_W2"][E - 1].rearrange("(f p) n -> p f n", p=P)).then_inc(s_loaded, 16)

        W2_POOL = 13

        def w2_raw(q):
            return piece_b32[:, q + 2, :] if q + 2 < N2 else raw_last2[:, q + 2 - N2, :]

        def w2_hi(act, q):
            act.wait_ge(s_w2[0], 16 * 5)
            if q >= 8:
                act.wait_ge(s_w2[1], 16 * 3)
            if q - 2 < W2_POOL:
                wait(act, s_wlo, q - 1)
            else:
                act.wait_ge(s_wld, q - 1 - W2_POOL)
            nc.scalar.activation(piece_b16[:, q, 0, :], w2_raw(q), ACT.Copy, scale=WS).then_inc(s_whi, 1)
            if q < W2_POOL:
                nc.scalar.activation(w2_raw(q), w2_raw(q), ACT.Copy, scale=WS).then_inc(s_whi, 1)

        def w2_lo_pool(pool, q):
            pool.wait_ge(s_whi, 2 * q + 2)
            nc.gpsimd.tensor_tensor(piece_b16[:, q, 1, :], w2_raw(q), piece_b16[:, q, 0, :],
                                    ALU.subtract).then_inc(s_wlo, 1)

        def w2_lo_dve(dve, q):
            dve.wait_ge(s_whi, W2_POOL + q + 1)
            nc.vector.scalar_tensor_tensor(out=piece_b16[:, q, 1, :], in0=w2_raw(q), scalar=WS,
                                           in1=piece_b16[:, q, 0, :], op0=ALU.mult,
                                           op1=ALU.subtract).then_inc(s_wld, 1)

        pGX = banks[:, 0:2, :].rearrange("p a (c n) -> p a c n", c=C)
        pG = banks[:, 2, 0:NCOL]
        pPre = banks[:, 3, 0:NCOL].rearrange("p (t e) -> p t e", e=E)
        pTot = banks[:, 4, 0:NCOL].rearrange("p (t e) -> p t e", e=E)
        pB1 = banks[:, 5, 0:E * FC]
        pSlot = banks[:, 6, 0:NH]
        xs_t = xs.rearrange("(t p) d -> p t d", p=P)

        def pairs(eng, n, step):
            for t in range(2):
                step(t, t, 0)
            with eng.Fori(1, n // 2) as i:
                for k in range(2):
                    step(2 * i + k, k, i)

        def gating():
            with nc.Block() as block:
                @block.sync
                def _(sp):
                    sp.dma_start(wg, a["L0_ffn_Wg"].rearrange("(c p) e -> p c e", p=P)).then_inc(s_gl, 16)
                    sp.dma_start(bg, a["L0_ffn_bg"].rearrange("(a e) -> a e", a=1).to_broadcast([P, E])).then_inc(s_gl, 16)
                    sp.dma_start(b1_rows[0:E * FC], a["L0_ffn_b1"].rearrange("e (f p) -> (e f) p", p=P)).then_inc(s_gl, 16)
                    w2_loads(sp, range(4), True, s_w2[0])

                    def step(g, par, h):
                        sp.wait_ge(s_xl, g + 1)
                        sp.wait_ge(s_xh, g + 1)
                        sp.dma_start(xs_t[:, bass.ds(GT * g, GT), :], xs_g[:, par].rearrange("p t s d -> p t (s d)")).then_inc(s_st[par], 16)
                    pairs(sp, NG, step)
                    for par in range(2):
                        sp.wait_ge(s_st[par], 16 * NG // 2)
                    sp.wait_ge(s_lg, NG)
                    w2_loads(sp, range(4, E - 1), False, s_w2[1])

                @block.gpsimd
                def _(pool):
                    nc.gpsimd.iota(iota_e, pattern=[[1, E]], base=-E, channel_multiplier=0,
                                   allow_small_or_imprecise_dtypes=True).then_inc(s_gc, 1)
                    nc.gpsimd.memset(tri, 1.0).then_inc(s_gc, 1)
                    nc.gpsimd.memset(ones16, 1.0).then_inc(s_gc, 1)
                    pool.wait_ge(s_gc, 3)
                    nc.gpsimd.affine_select(out=tri, in_=tri, compare_op=ALU.is_gt, fill=0.0, base=0,
                                            pattern=[[1, P]], channel_multiplier=-1).then_inc(s_gc, 1)
                    nc.gpsimd.iota(iota_lo, pattern=[[1, P]], base=0, channel_multiplier=0,
                                   allow_small_or_imprecise_dtypes=True).then_inc(s_gc, 1)
                    nc.gpsimd.iota(iota_hi, pattern=[[1, NH]], base=0, channel_multiplier=0,
                                   allow_small_or_imprecise_dtypes=True).then_inc(s_gc, 1)
                    nc.gpsimd.iota(token, pattern=[[P, T]], base=-T * P // 2, channel_multiplier=1,
                                   allow_small_or_imprecise_dtypes=True).then_inc(s_gc, 1)
                    nc.gpsimd.iota(iota_tile, pattern=[[1, NT]], base=0, channel_multiplier=0,
                                   allow_small_or_imprecise_dtypes=True).then_inc(s_gc, 1)
                    nc.gpsimd.memset(ones_t, 1.0).then_inc(s_gc, 1)

                    def reciprocal_roots(k, g0, g1):
                        cols = slice(GT * g0, GT * g1)
                        n = GT * (g1 - g0)
                        pool.wait_ge(s_ag, GT * g1)
                        nc.gpsimd.tensor_tensor(rs_all[:, 1, cols], mv_all[:, cols, 1], eps.to_broadcast([P, n]), ALU.add).then_inc(s_rs, 1)
                        pool.wait_ge(s_rs, 2 * k + 1)
                        nc.gpsimd.tensor_tensor(rs_all[:, 0, cols], rs_all[:, 1, cols], half.to_broadcast([P, n]), ALU.pow).then_inc(s_rs, 1)

                    def x_lo(g):
                        pool.wait_ge(s_xh, g + 1)
                        wait(pool, s_st[g % 2], 16 * (g // 2))
                        nc.gpsimd.tensor_tensor(xs_g[:, g % 2, :, 1, :], xn_g[:, g % 2], xs_g[:, g % 2, :, 0, :],
                                                ALU.subtract).then_inc(s_xl, 1)
                    reciprocal_roots(0, 0, 1)
                    for g in range(NG):
                        if g + 1 < NG:
                            reciprocal_roots(g + 1, g + 1, g + 2)
                        x_lo(g)
                    for q in range(W2_POOL):
                        w2_lo_pool(pool, q)

                @block.scalar
                def _(act):
                    act.wait_ge(s_b1t, 1)
                    nc.scalar.copy(b1_cols[:].rearrange("p e f -> p (e f)"), pB1).then_inc(s_b1, 1)

                    def step(g, par, h):
                        act.wait_ge(s_xn, GT * g + GT)
                        wait(act, s_st[par], 16 * h)
                        nc.scalar.copy(xs_g[:, par, :, 0, :], xn_g[:, par]).then_inc(s_xh, 1)
                        for pair in range(2):
                            act.wait_ge(s_tx, 2 * g + (pair + 1))
                            wait(act, s_lg, g - 1)
                            nc.scalar.copy(xT_g[:, par, pair], pGX[:, pair]).then_inc(s_tc, 1)
                    pairs(act, NG, step)
                    for q in range(N2):
                        w2_hi(act, q)
                        if q == N2 // 2:
                            act.wait_ge(s_se, 1)
                            nc.scalar.activation(top_v[:, 3, :], top_v[:, 3, :], ACT.Exp).then_inc(s_ex, 1)

                @block.tensor
                def _(pe):
                    pe.wait_ge(s_gl, 48)
                    nc.tensor.transpose(pB1, b1_rows[0:E * FC, :], ident[0:E * FC, 0:E * FC]).then_inc(s_b1t, 1)

                    def step(g, par, h):
                        pe.wait_ge(s_xn, GT * g + GT)
                        for pair in range(2):
                            wait(pe, s_tc, 2 * g + (pair - 1))
                            for j in range(2):
                                for c in range(C):
                                    last = nc.tensor.transpose(pGX[:, pair, c, j * P:(j + 1) * P],
                                                               xn_g[:, par, 2 * pair + j, c * P:(c + 1) * P], ident[:])
                            last.then_inc(s_tx, 1)
                        for pair in range(2):
                            pe.wait_ge(s_tc, 2 * g + (pair + 1))
                            for j in range(2):
                                o = banks[:, 2, bass.ds(g * (GT * E) + (2 * pair + j) * E, E)]
                                for c in range(C):
                                    last = nc.tensor.matmul(o, xT_g[:, par, pair, c, j * P:(j + 1) * P], wg[:, c, :],
                                                            start=(c == 0), stop=(c == C - 1))
                        last.then_inc(s_lg, 1)
                    pairs(pe, NG, step)
                    pe.wait_ge(s_se, 2)
                    pe.wait_ge(s_gc, 4)
                    sel = sel16.rearrange("p t e -> p (t e)")
                    nc.tensor.matmul(banks[:, 3, 0:NCOL], tri, sel, start=True, stop=True).then_inc(s_pf, 1)
                    nc.tensor.matmul(banks[:, 4, 0:NCOL], ones16, sel, start=True, stop=True).then_inc(s_pf, 1)

                    def hot(g, first=False, last_one=False):
                        for n in range(HOTS):
                            pe.wait_ge(s_hot, 2 * HOTS * g + (2 * n + 2))
                            nc.tensor.matmul(pSlot, oh_lo[:, n, :], oh_hi[:, n, :], start=first and n == 0,
                                             stop=last_one and n == HOTS - 1).then_inc(s_hm, 1)
                    hot(0, first=True)
                    with pe.Fori(1, NG - 1) as g:
                        hot(g)
                    hot(NG - 1, last_one=True)

                @block.vector
                def _(dve):
                    def group_stats(g):
                        for t in range(GT * g, GT * (g + 1)):
                            nc.vector.bn_stats(stats[:, t, :], x_res[:, t, :]).then_inc(s_bn, 1)
                        dve.wait_ge(s_bn, GT * (g + 1))
                        for t in range(GT * g, GT * (g + 1)):
                            nc.vector.bn_aggr(mv_all[:, t, :], stats[:, t, :]).then_inc(s_ag, 1)

                    def group_xn(g):
                        wait(dve, s_xl, g - 1)
                        wait(dve, s_tx, 2 * (g - 1))
                        wait(dve, s_xh, g - 1)
                        dve.wait_ge(s_rs, 2 * g + 2)
                        for j in range(GT):
                            t = GT * g + j
                            nc.vector.tensor_scalar(xn_g[:, g % 2, j, :], x_res[:, t, :], mv_all[:, t, 0:1],
                                                    rs_all[:, 0, t:t + 1], ALU.subtract, ALU.mult).then_inc(s_xn, 1)
                    group_stats(0)
                    group_stats(1)
                    for g in range(NG):
                        if g + 2 < NG:
                            group_stats(g + 2)
                        group_xn(g)

                    count = [0]

                    def link(instruction):
                        count[0] += 1
                        instruction.then_inc(s_r, 1)
                        dve.wait_ge(s_r, count[0])

                    def bt(v):
                        return v.unsqueeze(2).to_broadcast(TE)

                    def be(v):
                        return v.unsqueeze(1).to_broadcast(TE)

                    dve.wait_ge(s_lg, NG)
                    dve.wait_ge(s_gc, 4)
                    link(nc.vector.tensor_tensor(logits, pG.rearrange("p (t e) -> p t e", e=E), be(bg), ALU.add))
                    src = logits
                    for k in range(2):
                        link(nc.vector.tensor_reduce(top_v[:, k, :], src, AX, ALU.max))
                        link(nc.vector.tensor_tensor(tmp, src, bt(top_v[:, k, :]), ALU.is_equal))
                        link(nc.vector.tensor_tensor(tmp, tmp, be(iota_e), ALU.mult))
                        link(nc.vector.tensor_reduce(top_v[:, 2, :], tmp, AX, ALU.min))
                        link(nc.vector.tensor_tensor(oh[k], be(iota_e), bt(top_v[:, 2, :]), ALU.is_equal))
                        if k == 0:
                            link(nc.vector.scalar_tensor_tensor(out=logits, in0=oh[0], scalar=-1e30, in1=logits,
                                                                op0=ALU.mult, op1=ALU.add))
                    nc.vector.tensor_tensor(top_v[:, 3, :], top_v[:, 1, :], top_v[:, 0, :], ALU.subtract).then_inc(s_se, 1)
                    nc.vector.tensor_tensor(sel16, oh[0], oh[1], ALU.add).then_inc(s_se, 1)
                    dve.wait_ge(s_pf, 2)
                    dve.wait_ge(s_gc, 9)
                    for e in range(E):
                        link(nc.vector.tensor_tensor_scan(incl[:, e, :], ones_t, pTot[:, :, e], 0.0, ALU.mult, ALU.add))
                    link(nc.vector.tensor_scalar(tiles_i[:, 0, :], incl[:, :, T - 1], float(TT - 1), None, ALU.add))
                    link(nc.vector.tensor_scalar(tiles_i[:, 1, :], tiles_i[:, 0, :], TT.bit_length() - 1, None, ALU.arith_shift_right))
                    link(nc.vector.tensor_copy(tiles_f[:, 0, :], tiles_i[:, 1, :]))
                    link(nc.vector.tensor_tensor_scan(tiles_f[:, 1, :], ones_t[:, 0:E], tiles_f[:, 0, :], 0.0, ALU.mult, ALU.add))
                    link(nc.vector.tensor_tensor(tiles_f[:, 2, :], tiles_f[:, 1, :], tiles_f[:, 0, :], ALU.subtract))
                    link(nc.vector.tensor_scalar(tiles_f[:, 2, :], tiles_f[:, 2, :], float(TT), None, ALU.mult))
                    link(nc.vector.tensor_tensor(tmp, incl.rearrange("p e t -> p t e"), pTot, ALU.subtract))
                    link(nc.vector.tensor_tensor(tmp, tmp, pPre, ALU.add))
                    link(nc.vector.tensor_tensor(tmp, tmp, be(tiles_f[:, 2, :]), ALU.add))
                    for k in range(2):
                        link(nc.vector.tensor_tensor(oh[k], oh[k], tmp, ALU.mult))
                        link(nc.vector.tensor_reduce(pos_f[:, k, :], oh[k], AX, ALU.add))
                    link(nc.vector.tensor_copy(pos[:], pos_f))
                    flat = pos[:].rearrange("p a b -> p (a b)")
                    link(nc.vector.tensor_scalar(lohi_i[:, 0, :], flat, P - 1, None, ALU.bitwise_and))
                    link(nc.vector.tensor_scalar(lohi_i[:, 1, :], flat, P.bit_length() - 1, None, ALU.arith_shift_right))
                    link(nc.vector.tensor_copy(lohi, lohi_i))

                    def hot(g):
                        for n in range(HOTS):
                            k, j = n % 2, n // 2
                            wait(dve, s_hm, HOTS * (g - 1) + (n + 1))
                            at = g * GT + (k * T + j)
                            nc.vector.tensor_scalar(oh_lo[:, n, :], iota_lo, lohi[:, 0, bass.ds(at, 1)], None,
                                                    ALU.is_equal).then_inc(s_hot, 1)
                            nc.vector.tensor_scalar(oh_hi[:, n, :], iota_hi, lohi[:, 1, bass.ds(at, 1)],
                                                    token[:, bass.ds(g * GT + j, 1)], ALU.is_equal, ALU.mult).then_inc(s_hot, 1)
                    hot(0)
                    with dve.Fori(1, NG) as g:
                        hot(g)
                    row = [1, NT, E]
                    link(nc.vector.tensor_tensor(tile_cmp[0:1], iota_tile[0:1].unsqueeze(2).to_broadcast(row),
                                                 tiles_f[0:1, 1, :].unsqueeze(1).to_broadcast(row), ALU.is_ge))
                    link(nc.vector.tensor_reduce(te_f[0:1], tile_cmp[0:1], AX, ALU.add))
                    link(nc.vector.tensor_scalar(te_f[0:1], te_f[0:1], float(E - 1), None, ALU.min))
                    link(nc.vector.tensor_copy(tile_expert[:], te_f[0:1]))
                    dve.wait_ge(s_hm, 2 * T)
                    link(nc.vector.tensor_scalar(slot_f, pSlot, float(T * P // 2), None, ALU.add))
                    nc.vector.tensor_copy(slot_token[:], slot_f).then_inc(s_slot, 1)
                    dve.wait_ge(s_ex, 1)
                    link(nc.vector.tensor_scalar(top_v[:, 4, :], top_v[:, 3, :], 1.0, None, ALU.add))
                    link(nc.vector.reciprocal(top_v[:, 5, :], top_v[:, 4, :]))
                    link(nc.vector.tensor_scalar(topw[:, 0, :], top_v[:, 5, :], gscale[:, 1:2], None, ALU.mult))
                    link(nc.vector.tensor_tensor(topw[:, 1, :], topw[:, 0, :], top_v[:, 3, :], ALU.mult))
                    for q in range(W2_POOL, N2):
                        w2_lo_dve(dve, q)

        b2_all = view(work, 0, [E, D])
        m_o = E * D
        xg = view(work, m_o, [2, 2 * D], F16)
        xgT = view(work, m_o + 512, [2, C, TT], F16)
        hf = view(work, m_o + 1024, [2, 2 * TT])
        hh = view(work, m_o + 2048, [4, 2, 2, TT], F16)
        ysb = view(work, m_o + 4096, [2, D])
        s_b2 = sem("b2_loaded")
        s_gi = sem("moe_index")
        s_xg = [sem("moe_rows_0"), sem("moe_rows_1")]
        s_gt2 = sem("moe_transposed")
        s_gx = sem("moe_transpose_copied")
        s_up = sem("moe_up")
        s_ge = sem("moe_gelu")
        s_hi = sem("moe_hi")
        s_lo = sem("moe_lo")
        s_dn = sem("moe_down")
        s_ye = sem("moe_out_copied")
        s_yw = sem("moe_out_written")
        pXg = banks[:, 5, :].bitcast(F16).rearrange("p (s c n) -> p s c n", s=2, c=C)
        pY = banks[:, 4, :].rearrange("p (s d) -> p s d", s=2)
        ys_t = ys.rearrange("(i s p) d -> p i s d", s=2, p=P)

        def experts():
            with nc.Block() as block:
                @block.sync
                def _(sp):
                    sp.dma_start(b2_all, a["L0_ffn_b2"].rearrange("(a e) d -> a e d", a=1).to_broadcast([P, E, D])).then_inc(s_b2, 16)
                    with sp.Fori(0, NT) as i:
                        sp.wait_ge(s_ye, i + 1)
                        sp.dma_start(ys_t[:, bass.ds(i, 1), :, :].rearrange("p a s d -> p (a s) d"), ysb).then_inc(s_yw, 16)
                    sp.wait_ge(s_yw, 16 * NT)

                @block.gpsimd
                def _(pool):
                    def index(i, par):
                        nc.gpsimd.tensor_copy(idx_ring[:, par, :], slot_token[:, bass.ds(2 * i, 2)]).then_inc(s_gi, 1)

                    def step(i, par, h):
                        wait(pool, s_gt2, i)
                        pool.wait_ge(s_gi, i + 1)
                        index(i + 1, 1 - par)
                        for s in range(2):
                            nc.gpsimd.indirect_dma_start(xg[:, s, :], None, xs, bass.IndirectOffsetOnAxis(
                                ap=idx_ring[:, par, s:s + 1], axis=0)).then_inc(s_xg[s], 16)
                    index(0, 0)
                    pairs(pool, NT + 1, step)
                    for s in range(2):
                        pool.wait_ge(s_xg[s], 16 * (NT + 1))

                @block.tensor
                def _(pe):
                    def transposes(i):
                        wait(pe, s_gx, i)
                        for s in range(2):
                            pe.wait_ge(s_xg[s], 16 * (i + 1))
                            for part in range(2):
                                for c in range(C):
                                    last = nc.tensor.transpose(pXg[:, part, c, s * P:(s + 1) * P],
                                                               xg[:, s, part * D + c * P:part * D + (c + 1) * P], ident16[:])
                        last.then_inc(s_gt2, 1)

                    def up(i, e, b):
                        wait(pe, s_ge, 8 * (i - 1) + 2 * b + 2)
                        for f in (2 * b, 2 * b + 1):
                            n = 0
                            for pw, px in ((0, 0), (0, 1), (1, 0)):
                                for c in range(C):
                                    o = (2 * c + f // 4) * 2 * Q1 + pw * Q1 + f % 4 * P
                                    last = nc.tensor.matmul(
                                        banks[:, b, (f % 2) * TT:(f % 2) * TT + TT],
                                        wA[:, bass.ds(e, 1), o:o + P].rearrange("p a m -> p (a m)"),
                                        xgT[:, px, c, :], start=(n == 0), stop=(n == 3 * C - 1))
                                    n += 1
                        last.then_inc(s_up, 1)

                    def down(i, e, b):
                        pe.wait_ge(s_lo, 4 * i + b + 1)
                        if b == 0:
                            wait(pe, s_ye, i)
                        for s in range(2):
                            for ph, pw in ((0, 0), (1, 0), (0, 1)):
                                for k in range(2):
                                    o = (b // 2) * 2 * Q2 + pw * Q2 + (2 * b + k) % 4 * D
                                    last = nc.tensor.matmul(
                                        pY[:, s, :], hh[:, b, ph, k, s * P:(s + 1) * P],
                                        wB[:, bass.ds(e, 1), o:o + D].rearrange("p a m -> p (a m)"),
                                        start=(b == 0 and s == 0 and ph == 0 and pw == 0 and k == 0),
                                        stop=(b == 3 and s == 1 and pw == 1 and k == 1),
                                        skip_group_check=True)
                        last.then_inc(s_dn, 1)

                    def expert(i):
                        return pe.value_load(tile_expert[0:1, bass.ds(i, 1)], min_val=0, max_val=E - 1)

                    def tile(i, before=None):
                        e = expert(i)
                        if before is not None:
                            e_before = expert(before)
                            down(before, e_before, 2)
                        pe.wait_ge(s_gx, i + 1)
                        up(i, e, 0)
                        if before is not None:
                            down(before, e_before, 3)
                        up(i, e, 1)
                        up(i, e, 2)
                        down(i, e, 0)
                        up(i, e, 3)
                        transposes(i + 1)
                        down(i, e, 1)
                    transposes(0)
                    tile(0)
                    with pe.Fori(0, NT - 1) as i:
                        tile(i + 1, i)
                    e_last = expert(NT - 1)
                    down(NT - 1, e_last, 2)
                    down(NT - 1, e_last, 3)

                @block.scalar
                def _(act):
                    b1f = b1_cols[:].rearrange("p e f -> p (e f)")

                    def tile(i):
                        e = act.value_load(tile_expert[0:1, bass.ds(i, 1)], min_val=0, max_val=E - 1)
                        for b in range(4):
                            act.wait_ge(s_up, 4 * i + b + 1)
                            wait(act, s_lo, 4 * i + b - 1)
                            for k in range(2):
                                nc.scalar.activation(hf[:, b % 2, k * TT:(k + 1) * TT], banks[:, b, k * TT:(k + 1) * TT],
                                                     ACT.Gelu, bias=b1f[:, bass.ds(e * FC + (2 * b + k), 1)],
                                                     scale=1.0 / WS).then_inc(s_ge, 1)
                    tile(0)
                    with act.Fori(1, NT) as i:
                        tile(i)

                @block.vector
                def _(dve):
                    def rows(i):
                        dve.wait_ge(s_gt2, i + 1)
                        nc.vector.tensor_copy(xgT.rearrange("p s c n -> p (s c n)"),
                                              pXg.rearrange("p s c n -> p (s c n)")).then_inc(s_gx, 1)

                    def hidden(i, b):
                        dve.wait_ge(s_ge, 8 * i + 2 * b + 2)
                        wait(dve, s_dn, 4 * (i - 1) + b + 1)
                        h_hi, h_lo = (hh[:, b, s].rearrange("p k n -> p (k n)") for s in range(2))
                        nc.vector.tensor_copy(h_hi, hf[:, b % 2, :]).then_inc(s_hi, 1)
                        dve.wait_ge(s_hi, 4 * i + b + 1)
                        nc.vector.tensor_tensor(h_lo, hf[:, b % 2, :], h_hi, ALU.subtract).then_inc(s_lo, 1)

                    def y_out(i):
                        e = dve.value_load(tile_expert[0:1, bass.ds(i, 1)], min_val=0, max_val=E - 1)
                        dve.wait_ge(s_dn, 4 * i + 4)
                        wait(dve, s_yw, 16 * i)
                        nc.vector.scalar_tensor_tensor(
                            out=ysb, in0=pY, scalar=1.0 / WS,
                            in1=b2_all[:, bass.ds(e, 1), :].to_broadcast([P, 2, D]),
                            op0=ALU.mult, op1=ALU.add).then_inc(s_ye, 1)

                    def tile(i, before=None):
                        hidden(i, 0)
                        if before is not None:
                            y_out(before)
                        hidden(i, 1)
                        hidden(i, 2)
                        rows(i + 1)
                        hidden(i, 3)
                    dve.wait_ge(s_b2, 16)
                    rows(0)
                    tile(0)
                    with dve.Fori(0, NT - 1) as i:
                        tile(i + 1, i)
                    y_out(NT - 1)

        NP_ = INNER // P
        W1_ = 2 * SK
        G1 = view(region_a, 0, [2, B, C, HK], F16)
        kv1 = view(region_a, B * C * HK, [2, NP_, KB])
        ctxT1 = view(region_a, B * C * HK + 2 * NP_ * KB, [C, KB])
        w_out = view(region_b, 0, [NP_, D])
        wqT = view(region_b, NP_ * D, [NP_, D])
        ln_gamma = view(region_b, 2 * NP_ * D, [D])
        ln_beta = view(region_b, 2 * NP_ * D + D, [D])
        wkv1 = view(region_b, vw_word, [C, 2 * INNER])
        wq = view(region_b, vw_word + C * 2 * INNER, [C, INNER])
        ctx1 = view(region_b, vw_word + 3 * C * INNER, [B, D])
        VB1 = view(work, 2 * HKP, [P + NP_ * (W1_ + P)])
        kTB = view(work, 2 * HKP + P + NP_ * (W1_ + P), [NP_, W1_])
        yrows = view(work, 4 * HKP + 2 * D + 4 * C * P // 2, [2, D])
        assert 3 * C * INNER + B * D <= 2 * B * J * D // 2
        assert 2 * NP_ * D + 2 * D <= vw_word
        s_l1 = sem("l1_weights_loaded")
        s_l1c = sem("l1_consts")
        s_l1b = sem("l1_bias_scaled")
        s_ct1 = sem("l1_ctx_transposed")
        s_cc1 = sem("l1_ctx_copied")
        s_wt = sem("wq_transposed")
        s_wtc = sem("wq_copied")
        s_kv1 = sem("l1_kv")
        s_kvc = sem("l1_kv_copied")
        s_kb = sem("l1_k_spread")
        s_vb1 = sem("l1_v_spread")
        s_g1 = sem("l1_g")
        s_g1h = sem("l1_g_hi")
        s_g1l = sem("l1_g_lo")

        def fold_layer1():
            vw_base[0] = len(VGROUPS) * B
            with nc.Block() as block:
                @block.sync
                def _(sp):
                    sp.dma_start(ctx1[0:SK], a["ctx_1024"].rearrange("b k d -> k b d")).then_inc(s_l1, 16)
                    sp.dma_start(wq, a["L1_xattn_w_q"].rearrange("(c p) n -> p c n", p=P)).then_inc(s_l1, 16)
                    sp.dma_start(wkv1, a["L1_xattn_w_kv"].rearrange("(c p) n -> p c n", p=P)).then_inc(s_l1, 16)
                    sp.dma_start(w_out, a["L1_xattn_w_out"].rearrange("(c p) n -> p c n", p=P)).then_inc(s_l1, 16)
                    for dst, name in ((b_row[:], "L1_xattn_b_out"), (ln_gamma, "L1_xattn_ln_gamma"), (ln_beta, "L1_xattn_ln_beta")):
                        sp.dma_start(dst, a[name].rearrange("(a n) -> a n", a=1).to_broadcast([P, D])).then_inc(s_l1, 16)

                @block.gpsimd
                def _(pool):
                    nc.gpsimd.memset(VB1, 0.0).then_inc(s_l1c, 1)
                    nc.gpsimd.memset(kTB, 0.0).then_inc(s_l1c, 1)
                    nc.gpsimd.memset(S[:, :, HK:HKP], 0.0).then_inc(s_l1c, 1)
                    pool.wait_ge(s_l1c, 3)
                    pool.wait_ge(s_kvc, 2 * NP_)
                    for b in range(B):
                        wait(pool, s_vw, vw_base[0] + len(VGROUPS) * b)
                        for h in range(2):
                            rows = slice(64 * h, 64 * h + 64)
                            dst = VB1[rows, P:P + NP_ * (W1_ + P)].rearrange("p (n w) -> p n w", n=NP_)[:, :, h * SK:(h + 1) * SK]
                            nc.gpsimd.tensor_copy(dst, kv1[rows, 1, :, b * SK:(b + 1) * SK]).then_inc(s_vb1, 1)

                @block.scalar
                def _(act):
                    act.wait_ge(s_ct1, 1)
                    nc.scalar.copy(ctxT1, banks[:, 0:2, 0:KB]).then_inc(s_cc1, 1)
                    for n in range(NP_):
                        act.wait_ge(s_kv1, 2 * (n + 1))
                        o = 6 * (n % 2)
                        nc.scalar.copy(kv1[:, :, n, :], banks[:, o:o + 2, 0:KB]).then_inc(s_kvc, 2)
                    for b in range(B):
                        for c in range(C):
                            if c == 1:
                                vw_hi(act, b)
                            act.wait_ge(s_g1, 2 * b + c + 1)
                            nc.scalar.activation(G1[:, 0, b, c, 0:924].rearrange("p (a n) -> p a n", a=2), banks[:, 0:2, 0:462],
                                                 ACT.Copy, scale=AS).then_inc(s_g1h, 1)
                            nc.scalar.activation(G1[:, 0, b, c, 924:HK], banks[:, 2, 0:308],
                                                 ACT.Copy, scale=AS).then_inc(s_g1h, 1)

                @block.vector
                def _(dve):
                    dve.wait_ge(s_l1, 7 * 16)
                    nc.vector.tensor_scalar(b_row[:], b_row[:], gtanh[:, 1:2], gtanh[:, 4:5], ALU.mult, ALU.mult).then_inc(s_l1b, 1)
                    nc.vector.tensor_scalar(ln_gamma, ln_gamma, (1.0 + EPS) ** -0.5, None, ALU.mult).then_inc(s_l1b, 1)
                    dve.wait_ge(s_wt, 1)
                    nc.vector.tensor_copy(wqT.rearrange("p n d -> p (n d)"),
                                          banks[:, 2:6, :].rearrange("p a b -> p (a b)")).then_inc(s_wtc, 1)
                    dve.wait_ge(s_kvc, 2 * NP_)
                    dve.wait_ge(s_l1c, 3)
                    for b in range(B):
                        for c in range(C):
                            if c == 0:
                                wait(dve, s_g1, 2 * b)
                                for h in range(2):
                                    rows = slice(64 * h, 64 * h + 64)
                                    nc.vector.tensor_copy(kTB[rows, :, h * SK:(h + 1) * SK],
                                                          kv1[rows, 0, :, b * SK:(b + 1) * SK]).then_inc(s_kb, 1)
                            else:
                                vw_lo(dve, b)
                            dve.wait_ge(s_g1h, 2 * (2 * b + c + 1))
                            nc.vector.scalar_tensor_tensor(
                                out=G1[:, 1, b, c, 0:924].rearrange("p (a n) -> p a n", a=2), in0=banks[:, 0:2, 0:462],
                                scalar=AS, in1=G1[:, 0, b, c, 0:924].rearrange("p (a n) -> p a n", a=2),
                                op0=ALU.mult, op1=ALU.subtract).then_inc(s_g1l, 1)
                            nc.vector.scalar_tensor_tensor(
                                out=G1[:, 1, b, c, 924:HK], in0=banks[:, 2, 0:308], scalar=AS,
                                in1=G1[:, 0, b, c, 924:HK], op0=ALU.mult, op1=ALU.subtract).then_inc(s_g1l, 1)

                @block.tensor
                def _(pe):
                    pe.wait_ge(s_l1, 7 * 16)
                    for c in range(C):
                        for b in range(B):
                            last = nc.tensor.transpose(banks[:, c, b * SK:(b + 1) * SK],
                                                       ctx1[0:SK, b, c * P:(c + 1) * P], ident[0:SK, 0:SK])
                    last.then_inc(s_ct1, 1)
                    for n in range(NP_):
                        for c in range(C):
                            last = nc.tensor.transpose(banks[:, 2 + n // 2, (n % 2) * D + c * P:(n % 2) * D + (c + 1) * P],
                                                       wq[:, c, n * P:(n + 1) * P], ident[:])
                    last.then_inc(s_wt, 1)
                    pe.wait_ge(s_cc1, 1)
                    for n in range(NP_):
                        wait(pe, s_kvc, 2 * (n - 1))
                        for s in range(2):
                            for c in range(C):
                                o = s * INNER + n * P
                                last = nc.tensor.matmul(banks[:, 6 * (n % 2) + s, 0:KB], wkv1[:, c, o:o + P], ctxT1[:, c, :],
                                                        start=(c == 0), stop=(c == C - 1))
                            last.then_inc(s_kv1, 1)
                    pe.wait_ge(s_wtc, 1)
                    pe.wait_ge(s_kvc, 2 * NP_)
                    for b in range(B):
                        pe.wait_ge(s_kb, 2 * (b + 1))
                        for c in range(C):
                            if c == 1:
                                pe.wait_ge(s_vb1, 2 * (b + 1))
                                vw_product(pe, b, VB1, W1_, NP_, w_out, None)
                            wait(pe, s_g1l, 2 * (2 * b + c))
                            for n in range(NP_):
                                last = nc.tensor.matmul(banks[:, n // 3, (n % 3) * W1_:(n % 3) * W1_ + W1_],
                                                        wqT[:, n, c * P:(c + 1) * P], kTB[:, n, :], start=True, stop=True)
                            last.then_inc(s_g1, 1)

        GN = GT * P
        R2 = 2 * R
        f_o = B * C * HK
        U1r = view(region_a, f_o, [C, R2])
        V1r = view(region_a, f_o + 256, [F])
        U2r = view(region_a, f_o + 1280, [FC, R])
        V2r = view(region_a, f_o + 1792, [D])
        U1s = view(region_a, f_o + 2048, [2, C, R2], F16)
        V1s = view(region_a, f_o + 2304, [2, F], F16)
        U2s = view(region_a, f_o + 3328, [FC, R2], F16)
        V2s = view(region_a, f_o + 3840, [2, D], F16)
        fb1_rows = view(region_a, f_o + 4096, [P])
        fb1 = view(region_a, f_o + 4224, [FC])
        fbias = view(region_a, f_o + 4232, [D])
        fstats = view(region_a, f_o + 4600, [T, 6])
        fmv = view(region_a, f_o + 4800, [T, 2])
        frs = view(region_a, f_o + 4900, [2, T])
        fxn = view(region_b, 0, [GT, D])
        fct = view(region_b, GT * D, [GT, D])
        rank_s = view(region_b, 8192, [NG, GN], F16)
        fxT = view(region_b, 10240, [2, C, GN], F16)
        fq = view(region_b, 11264, [2, GN], F16)
        fhh = view(region_b, 11776, [FC, 2, GN], F16)
        fh = view(region_a, 0, [4, GN])
        V1_BANKS = (1, 3, 4, 6)
        LEAD = 3
        TX1_AT, U1_AT, TX0_AT, V2_AT = 1, 3, 7, (1, 3)
        s_fl = sem("ffn_loaded")
        s_fw = sem("ffn_weights_hi")
        s_fwl = sem("ffn_weights_lo")
        s_fbt = sem("ffn_bias_transposed")
        s_fb = sem("ffn_bias_columns")
        s_fbn = sem("ffn_bn")
        s_fag = sem("ffn_bn_aggr")
        s_frs = sem("ffn_rstd")
        s_fct = sem("ffn_centred")
        s_fxn = sem("ffn_xn")
        s_fba = sem("ffn_out_bias_added")
        s_ftx = sem("ffn_x_transposed")
        s_fxh = sem("ffn_x_hi")
        s_fxl = sem("ffn_x_lo")
        s_fu1 = sem("ffn_u1")
        s_fsh = sem("ffn_rank_hi")
        s_fsl = sem("ffn_rank_lo")
        s_fv1 = sem("ffn_v1")
        s_fge = sem("ffn_gelu")
        s_fhi = sem("ffn_h_hi")
        s_flo = sem("ffn_h_lo")
        s_fu2 = sem("ffn_u2")
        s_fqh = sem("ffn_q_hi")
        s_fql = sem("ffn_q_lo")
        s_fv2 = sem("ffn_v2")
        s_fep = sem("ffn_residual")
        s_out = sem("out_written")
        pFX = banks[:, 0, :].rearrange("p (c n) -> p c n", c=C)
        pFO = banks[:, 5, :].rearrange("p (a d) -> p a d", a=2)
        out_t = out.rearrange("b (t p) d -> p (b t) d", p=P)

        def group_loop(eng, body):
            body(0, False, True, True)
            with eng.Fori(1, NG - 2) as g:
                body(g, True, True, True)
            body(NG - 2, True, True, False)
            body(NG - 1, True, False, False)

        def xtile(g, j):
            return x_res[:, bass.ds(g * GT + j, 1), :].rearrange("p a b -> p (a b)")

        def two(g, pair):
            return x_res[:, bass.ds(g * GT + 2 * pair, 2), :]

        def transposed(g, f, nxt, nxt2, step):
            if nxt and f == TX1_AT:
                step(g + 1, 1)
            if nxt2 and f == TX0_AT:
                step(g + 2, 0)

        def ahead(g, f):
            return (g, f + LEAD) if f + LEAD < FC else (g + 1, f + LEAD - FC)

        def ffn_loads(sp):
            for k in range(2):
                rows = slice(k * R, (k + 1) * R)
                sp.dma_start(U1r[:, :, rows], a["L1_ffn_U1"].rearrange("(c p) r -> p c r", p=P)).then_inc(s_fl, 16)
                sp.dma_start(V1r[rows], a["L1_ffn_V1"]).then_inc(s_fl, 16)
                sp.dma_start(V2r[rows], a["L1_ffn_V2"]).then_inc(s_fl, 16)
            sp.dma_start(U2r, a["L1_ffn_U2"].rearrange("(f p) r -> p f r", p=P)).then_inc(s_fl, 16)
            sp.dma_start(fb1_rows[0:FC], a["L1_ffn_b1"].rearrange("(f p) -> f p", p=P)).then_inc(s_fl, 16)
            sp.dma_start(fbias, a["L1_ffn_b2"].rearrange("(a n) -> a n", a=1).to_broadcast([P, D])).then_inc(s_fl, 16)

        def low_rank_ffn():
            with nc.Block() as block:
                @block.sync
                def _(sp):
                    with sp.Fori(0, NG) as g:
                        sp.wait_ge(s_fep, 2 * (g + 1))
                        sp.dma_start(out_t[:, bass.ds(g * GT, GT), :], x_res[:, bass.ds(g * GT, GT), :]).then_inc(s_out, 16)
                    sp.wait_ge(s_out, 16 * NG)

                @block.gpsimd
                def _(pool):
                    def reciprocal_roots(k, tiles, n):
                        pool.wait_ge(s_fag, tiles.stop)
                        nc.gpsimd.tensor_tensor(frs[:, 1, tiles], fmv[:, tiles, 1], eps.to_broadcast([P, n]),
                                                ALU.add).then_inc(s_frs, 1)
                        pool.wait_ge(s_frs, 2 * k + 1)
                        nc.gpsimd.tensor_tensor(frs[:, 0, tiles], frs[:, 1, tiles], half.to_broadcast([P, n]),
                                                ALU.pow).then_inc(s_frs, 1)

                    def group(g, k):
                        four = bass.ds(g * GT, GT)
                        x4 = x_res[:, four, :]
                        wait(pool, s_fxn, g)
                        pool.wait_ge(s_fag, T if k == 2 else GT * (k + 1))
                        nc.gpsimd.tensor_tensor(fct, x4, fmv[:, four, 0:1].to_broadcast([P, GT, D]),
                                                ALU.subtract).then_inc(s_fct, 1)
                        pool.wait_ge(s_fct, g + 1)
                        wait(pool, s_ftx, 2 * g)
                        pool.wait_ge(s_frs, 2 * k + 2)
                        nc.gpsimd.tensor_tensor(fxn, fct, frs[:, 0, four].unsqueeze(2).to_broadcast([P, GT, D]),
                                                ALU.mult).then_inc(s_fxn, 1)
                        pool.wait_ge(s_fwl, 5)
                        nc.gpsimd.tensor_tensor(x4, x4, fbias.unsqueeze(1).to_broadcast([P, GT, D]),
                                                ALU.add).then_inc(s_fba, 1)
                    for g in range(2):
                        reciprocal_roots(g, slice(GT * g, GT * (g + 1)), GT)
                        group(g, g)
                    reciprocal_roots(2, slice(2 * GT, T), T - 2 * GT)
                    with pool.Fori(2, NG) as g:
                        group(g, 2)

                @block.scalar
                def _(act):
                    act.wait_ge(s_fl, 9 * 16)
                    nc.scalar.activation(U1s[:, 0], U1r, ACT.Copy, scale=AS).then_inc(s_fw, 1)
                    nc.scalar.activation(V1s[:, 0], V1r, ACT.Copy, scale=AS).then_inc(s_fw, 1)
                    nc.scalar.activation(V2s[:, 0], V2r, ACT.Copy, scale=AS).then_inc(s_fw, 1)
                    nc.scalar.activation(U2s[:, :, 0:R], U2r, ACT.Copy, scale=AS).then_inc(s_fw, 1)
                    act.wait_ge(s_fbt, 1)
                    nc.scalar.copy(fb1, banks[:, 2, 0:FC]).then_inc(s_fb, 1)
                    act.wait_ge(s_fb, 1)

                    def x_hi(g, pair):
                        act.wait_ge(s_ftx, 2 * g + pair + 1)
                        wait(act, s_fu1, g)
                        nc.scalar.copy(fxT[:, 0, :, pair * 2 * P:(pair + 1) * 2 * P], pFX).then_inc(s_fxh, 1)

                    def rank_hi(g):
                        act.wait_ge(s_fu1, g + 1)
                        nc.scalar.copy(rank_s[:, bass.ds(g, 1), :].rearrange("p a n -> p (a n)"), banks[:, 2, :]).then_inc(s_fsh, 1)

                    def gelu(g, f):
                        src = banks[:, V1_BANKS[f % 4], :]
                        act.wait_ge(s_fv1, FC * g + f + 1)
                        wait(act, s_fu2, FC * (g - 1) + f + 1)
                        nc.scalar.activation(fhh[:, f, 0, :], src, ACT.Gelu_apprx_tanh, bias=fb1[:, f:f + 1],
                                             scale=1.0 / (AS * AS)).then_inc(s_fhi, 1)
                        wait(act, s_flo, FC * g + f - 3)
                        nc.scalar.activation(fh[:, f % 4, :], src, ACT.Gelu_apprx_tanh, bias=fb1[:, f:f + 1],
                                             scale=1.0 / (AS * AS)).then_inc(s_fge, 1)

                    def body(g, prev, nxt, nxt2):
                        for f in range(FC):
                            if nxt or f + LEAD < FC:
                                gelu(*ahead(g, f))
                            transposed(g, f, nxt, nxt2, x_hi)
                            if nxt and f == U1_AT:
                                rank_hi(g + 1)
                    x_hi(0, 0)
                    x_hi(0, 1)
                    rank_hi(0)
                    for f in range(LEAD):
                        gelu(0, f)
                    x_hi(1, 0)
                    group_loop(act, body)

                @block.vector
                def _(dve):
                    def stats(g):
                        for t in range(GT * g, GT * (g + 1)):
                            nc.vector.bn_stats(fstats[:, t, :], x_res[:, t, :]).then_inc(s_fbn, 1)
                        dve.wait_ge(s_fbn, GT * (g + 1))
                        for t in range(GT * g, GT * (g + 1)):
                            nc.vector.bn_aggr(fmv[:, t, :], fstats[:, t, :]).then_inc(s_fag, 1)

                    def x_lo(g, pair):
                        cols = slice(pair * 2 * P, (pair + 1) * 2 * P)
                        dve.wait_ge(s_fxh, 2 * g + pair + 1)
                        nc.vector.tensor_tensor(fxT[:, 1, :, cols], pFX, fxT[:, 0, :, cols], ALU.subtract).then_inc(s_fxl, 1)

                    def rank_lo(g):
                        hi_rows = rank_s[R:R2, bass.ds(g, 1), :].rearrange("p a n -> p (a n)")
                        dve.wait_ge(s_fsh, g + 1)
                        nc.vector.tensor_tensor(hi_rows, banks[R:R2, 2, :], hi_rows, ALU.subtract).then_inc(s_fsl, 1)

                    def h_lo(g, f):
                        dve.wait_ge(s_fhi, FC * g + f + 1)
                        dve.wait_ge(s_fge, FC * g + f + 1)
                        nc.vector.tensor_tensor(fhh[:, f, 1, :], fh[:, f % 4, :], fhh[:, f, 0, :],
                                                ALU.subtract).then_inc(s_flo, 1)

                    def q_split(g):
                        dve.wait_ge(s_fu2, FC * (g + 1))
                        wait(dve, s_fv2, 2 * g)
                        nc.vector.tensor_copy(fq[:, 0, :], banks[:, 7, :]).then_inc(s_fqh, 1)
                        dve.wait_ge(s_fqh, g + 1)
                        nc.vector.tensor_tensor(fq[:, 1, :], banks[:, 7, :], fq[:, 0, :], ALU.subtract).then_inc(s_fql, 1)

                    def residual(g, pair):
                        dve.wait_ge(s_fv2, 2 * g + pair + 1)
                        dve.wait_ge(s_fba, g + 1)
                        nc.vector.scalar_tensor_tensor(out=two(g, pair), in0=pFO, scalar=gscale[:, 3:4], in1=two(g, pair),
                                                       op0=ALU.mult, op1=ALU.add).then_inc(s_fep, 1)

                    def body(g, prev, nxt, nxt2):
                        for f in range(FC):
                            if f == FC - 1:
                                q_split(g)
                            if nxt or f + LEAD < FC:
                                h_lo(*ahead(g, f))
                            transposed(g, f, nxt, nxt2, x_lo)
                            if nxt and f == U1_AT:
                                rank_lo(g + 1)
                            if prev and f in V2_AT:
                                residual(g - 1, V2_AT.index(f))
                            if not prev and f < NG - 4:
                                stats(4 + f)
                    stats(0)
                    dve.wait_ge(s_fw, 4)
                    for lo, r, hi in ((U1s[:, 1], U1r, U1s[:, 0]), (V1s[:, 1], V1r, V1s[:, 0]),
                                      (V2s[:, 1], V2r, V2s[:, 0]), (U2s[:, :, R:R2], U2r, U2s[:, :, 0:R])):
                        nc.vector.scalar_tensor_tensor(out=lo, in0=r, scalar=AS, in1=hi, op0=ALU.mult,
                                                       op1=ALU.subtract).then_inc(s_fwl, 1)
                    nc.vector.tensor_scalar(fbias, fbias, gtanh[:, 3:4], None, ALU.mult).then_inc(s_fwl, 1)
                    stats(1)
                    x_lo(0, 0)
                    x_lo(0, 1)
                    stats(2)
                    rank_lo(0)
                    stats(3)
                    for f in range(LEAD):
                        h_lo(0, f)
                    x_lo(1, 0)
                    group_loop(dve, body)
                    for pair in range(2):
                        residual(NG - 1, pair)

                @block.tensor
                def _(pe):
                    pe.wait_ge(s_fl, 9 * 16)
                    nc.tensor.transpose(banks[:, 2, 0:FC], fb1_rows[0:FC, :], ident[0:FC, 0:FC]).then_inc(s_fbt, 1)

                    def tx(g, pair):
                        pe.wait_ge(s_fxn, g + 1)
                        wait(pe, s_fxl, 2 * g + pair)
                        for j in range(2):
                            for c in range(C):
                                last = nc.tensor.transpose(pFX[:, c, j * P:(j + 1) * P],
                                                           fxn[:, 2 * pair + j, c * P:(c + 1) * P], ident[:])
                        last.then_inc(s_ftx, 1)

                    def u1(g):
                        pe.wait_ge(s_fxl, 2 * (g + 1))
                        wait(pe, s_fsl, g)
                        n = 0
                        for pw, px in ((0, 0), (0, 1), (1, 0)):
                            for c in range(C):
                                last = nc.tensor.matmul(banks[:, 2, :], U1s[:, pw, c, :], fxT[:, px, c, :],
                                                        start=(n == 0), stop=(n == 3 * C - 1))
                                n += 1
                        last.then_inc(s_fu1, 1)

                    def v1(g, f):
                        if f == 0:
                            pe.wait_ge(s_fsl, g + 1)
                        wait(pe, s_fge, FC * g + f - 3)
                        for part in range(2):
                            last = nc.tensor.matmul(banks[:, V1_BANKS[f % 4], :], V1s[:, part, f * P:(f + 1) * P],
                                                    rank_s[:, bass.ds(g, 1), :].rearrange("p a n -> p (a n)"),
                                                    start=(part == 0), stop=(part == 1))
                        last.then_inc(s_fv1, 1)

                    def u2(g, f):
                        pe.wait_ge(s_flo, FC * g + f + 1)
                        if f == 0:
                            wait(pe, s_fql, g)
                        for part in range(2):
                            last = nc.tensor.matmul(banks[:, 7, :], U2s[:, f, :], fhh[:, f, part, :],
                                                    start=(f == 0 and part == 0), stop=(f == FC - 1 and part == 1))
                        last.then_inc(s_fu2, 1)

                    def v2(g, pair):
                        pe.wait_ge(s_fql, g + 1)
                        wait(pe, s_fep, 2 * g + pair)
                        for j in range(2):
                            at = (2 * pair + j) * P
                            for n, (pq, pw) in enumerate(((0, 0), (1, 0), (0, 1))):
                                last = nc.tensor.matmul(pFO[:, j, :], fq[:, pq, at:at + P],
                                                        V2s[:, pw, :], start=(n == 0), stop=(n == 2))
                        last.then_inc(s_fv2, 1)

                    def body(g, prev, nxt, nxt2):
                        for f in range(FC):
                            if nxt or f + LEAD < FC:
                                v1(*ahead(g, f))
                            transposed(g, f, nxt, nxt2, tx)
                            if nxt and f == U1_AT:
                                u1(g + 1)
                            if prev and f in V2_AT:
                                v2(g - 1, V2_AT.index(f))
                            u2(g, f)
                    pe.wait_ge(s_fb, 1)
                    tx(0, 0)
                    tx(0, 1)
                    pe.wait_ge(s_fwl, 4)
                    u1(0)
                    for f in range(LEAD):
                        v1(0, f)
                    tx(1, 0)
                    group_loop(pe, body)
                    for pair in range(2):
                        v2(NG - 1, pair)

        if stop >= 1:
            attention("xattn0", pieces0, lambda part, b, c: G0[:, part, b, c, :], 0,
                      1.0 / (HD0 ** 0.5 * AS), eps, False, False)

        if stop >= 2:
            gating()
            experts()
            fold_layer1()
            pieces1 = [(bank, 0, n * SK, tuple(range(C)), h0 * SK) for bank, (h0, n) in enumerate(((0, 6), (6, 6), (12, 4)))]
            attention("xattn1", pieces1, lambda part, b, c: G1[:, part, b, c, :], 2,
                      1.0 / (HD1 ** 0.5 * AS), eps2, True, True)

        if stop >= 4:
            low_rank_ffn()
            return
        with nc.Block() as block:
            @block.sync
            def _(sp):
                sp.wait_ge(s_x, 64)
                for b in range(B):
                    sp.dma_start(out[b].rearrange("(t p) d -> p t d", p=P), x_res[:, b * TB:(b + 1) * TB, :]).then_inc(s_out, 16)
                sp.wait_ge(s_out, 16 * B)


_NAMES = ["x", "ctx_1024", "g_xattn", "g_ffn", "L0_xattn_W_kv", "L0_xattn_b_kv", "L0_xattn_W_o", "L0_xattn_b_o",
          "L0_ffn_Wg", "L0_ffn_bg", "L0_ffn_W1", "L0_ffn_b1", "L0_ffn_W2", "L0_ffn_b2", "L1_xattn_ln_gamma",
          "L1_xattn_ln_beta", "L1_xattn_w_q", "L1_xattn_w_kv", "L1_xattn_w_out", "L1_xattn_b_out", "L1_xattn_gate",
          "L1_ffn_U1", "L1_ffn_V1", "L1_ffn_b1", "L1_ffn_U2", "L1_ffn_V2", "L1_ffn_b2"]


def kernel(**inputs):
    import numpy as _np
    import concourse.bacc as _bacc
    from concourse import mybir as _mybir
    from concourse.bass_utils import run_bass_kernel_spmd as _run

    nc = _bacc.Bacc("TRN2", target_bir_lowering=False, num_devices=1)
    arrays, aps = {}, {}
    for name in _NAMES:
        v = _np.ascontiguousarray(inputs[name])
        arrays[f"in_{name}"] = v
        aps[name] = nc.dram_tensor(f"in_{name}", v.shape, _mybir.dt.from_np(v.dtype), kind="ExternalInput").ap()
    out = nc.dram_tensor("out", inputs["x"].shape, _mybir.dt.float32, kind="ExternalOutput").ap()
    flamingo_kernel(nc, aps, out)
    r = _run(nc, [arrays], core_ids=[0])
    return r.results[0]["out"]
```

```python
from contextlib import ExitStack

import concourse.bass as bass
from concourse import mybir

F32 = mybir.dt.float32
F16 = mybir.dt.float16
I32 = mybir.dt.int32
ALU = mybir.AluOpType
ACT = mybir.ActivationFunctionType
AX = mybir.AxisListType.X

P = 128
BANK = 512


def wait(eng, sem, value):
    if not (isinstance(value, int) and value <= 0):
        eng.wait_ge(sem, value)


def flamingo_kernel(nc, a, out):
    B, SQ, D = a["x"].shape
    _, SK, _ = a["ctx_1024"].shape
    C = D // P
    TB = SQ // P
    T = B * TB
    H = 16
    HD0 = D // H
    INNER = a["L1_xattn_w_q"].shape[1]
    HD1 = INNER // H
    E, _, F = a["L0_ffn_W1"].shape
    FC = F // P
    HK = H * SK
    J = -(-HK // P)
    HKP = J * P
    KB = B * SK
    R = a["L1_ffn_U1"].shape[1]
    EPS = 1e-5
    NCOL = T * E
    TT = 2 * P
    NT = 2 * B * SQ // TT + E - 1
    NH = 2 * (NT + 2)
    HEADS_OF_BANK = (6, 6, 4)
    HEADS_UP_TO = (0, 6, 12, 16)
    WS = 64.0
    AS = 16.0
    PS = 256.0

    ctx = ExitStack()
    with ctx:
        def sb(name, shape, dt=F32):
            return ctx.enter_context(nc.sbuf_tensor(name, shape, dt))

        def sem(name):
            return ctx.enter_context(nc.semaphore(name))

        def view(arena, word, shape, dt=F32):
            n = 1
            for s in shape:
                n *= s
            words = n if dt in (F32, I32) else n // 2
            v = arena[:, word:word + words]
            if dt != F32:
                v = v.bitcast(dt)
            if len(shape) == 2:
                v = v.rearrange("p (a b) -> p a b", a=shape[0])
            elif len(shape) == 3:
                v = v.rearrange("p (a b c) -> p a b c", a=shape[0], b=shape[1])
            elif len(shape) == 4:
                v = v.rearrange("p (a b c d) -> p a b c d", a=shape[0], b=shape[1], c=shape[2])
            return v

        x_res = sb("x_res", [P, T, D])
        region_a = sb("region_a", [P, 16384])
        region_b = sb("region_b", [P, 16384])
        work = sb("work", [P, 6900])
        ident = sb("ident", [P, P])
        ident16 = sb("ident16", [P, P], F16)
        b_row = sb("b_row", [P, D])
        gates = sb("gates", [P, 5])
        gtanh = sb("gtanh", [P, 5])
        gscale = sb("gscale", [P, 4])
        small = sb("small", [P, 48])
        mv = sb("mv", [P, 2, 2])
        bst = sb("bst", [P, 2, 6])
        rstd = sb("rstd", [P, 2, 2])
        smax = sb("smax", [P, 2, H])
        ssum = sb("ssum", [P, 2, H])
        srec = sb("srec", [P, 2, H])
        nmax = sb("nmax", [P, 2, H])
        slot_token = sb("slot_token", [P, NH], I32)
        tile_expert = sb("tile_expert", [1, NT], I32)
        pos = sb("pos", [P, 2, T], I32)
        topw = sb("topw", [P, 2, T])
        idx_now = sb("idx_now", [P, 2], I32)
        idx_ring = sb("idx_ring", [P, 2, 2], I32)
        b1_cols = sb("b1_cols", [P, E, FC])
        ctxT = sb("ctxT", [P, C, KB])
        KV_PARTS = 4
        KV_EARLY = KV_PARTS - 1
        wkv1_early = sb("wkv1_early", [P, KV_EARLY, C, 2, INNER // KV_PARTS])
        minus_half = small[:, 0:1]
        eps = small[:, 1:2]
        eps2 = small[:, 2:3]

        banks = ctx.enter_context(nc.psum_tensor("banks", [P, 8, BANK], F32))

        xs = nc.dram_tensor("xs", (B * SQ, 2 * D), F16, kind="Internal").ap()
        ys = nc.dram_tensor("ys", (NT * TT, D), F32, kind="Internal").ap()

        def table_for(func):
            nc.scalar.activation(small[:, 3:4], minus_half, func)

        G0 = view(region_b, 0, [2, B, C, (H // C) * SK], F16)
        vw_word = B * C * (H // C) * SK
        VW = view(region_b, vw_word, [2, B, J, D], F16)
        ctx_sb = view(region_a, 0, [B, D])
        wkv0 = view(region_a, 1024, [C, 2 * D])
        wo0 = view(region_a, 2048, [C, D])
        kT0 = view(region_a, 3200, [2, C, KB], F16)
        k_full = view(region_a, 3850, [C, KB])
        vT0 = view(region_a, 4500, [C, KB])
        W0 = (H // C) * SK
        VBW = P + C * (W0 + P)
        VB0 = view(region_a, 10000, [2, VBW])
        bkv = view(region_a, 7000, [2 * D])
        ones = view(region_a, 7600, [1])
        bias_cols = view(region_a, 7950, [2, C])
        wkv0s = view(region_a, 8100, [C, 2, D])
        bkvs = view(region_a, 9200, [2, D])
        mask = view(region_a, 8000, [H // C])
        mask16 = view(region_a, 8010, [H // C], F16)
        S = view(work, 0, [2, HKP])
        PT = view(work, 2 * HKP, [2, 2, J, P], F16)
        xnb = view(work, 4 * HKP, [2, D])
        xT = view(work, 4 * HKP + 2 * D, [2, 2, C, P], F16)

        s_c = sem("consts")
        s_x = sem("x_loaded")
        s_w = sem("setup_weights_loaded")
        s_ws = sem("kv_weights_sorted")
        s_ct = sem("ctx_transposed")
        s_ctc = sem("ctx_transpose_copied")
        s_kv = sem("kv_projected")
        s_kc = sem("kv_copied")
        s_kh = sem("k_hi")
        s_kl = sem("k_lo")
        s_vb = sem("v_spread")
        s_g0 = sem("k_spread_hi")
        s_g0l = sem("k_spread_lo")
        s_vw = sem("vw_done")
        s_vh = sem("vw_hi")
        s_vl = sem("vw_lo")
        s_gt = sem("gates_tanh")
        s_gs = sem("gates_scaled")
        VGROUPS = [(0, 4), (4, 8), (8, J)]

        def vw_chunks(width, n, j):
            return [(k, P + k * (width + P) + P * j - k * width) for k in range(n)
                    if P * j + P > k * width and P * j < (k + 1) * width]

        def vw_product(pe, b, vb, width, n, w_out, groups=range(3)):
            for g in groups:
                j0, j1 = VGROUPS[g]
                at = len(VGROUPS) * b + g
                wait(pe, s_vl, vw_base[0] + at - 1)
                wait(pe, s_vh, vw_base[0] + at - 1)
                for j in range(j0, j1):
                    parts = vw_chunks(width, n, j)
                    o = banks[:, 4 + 2 * (at % 2) + (j - j0) // 2, (j - j0) % 2 * D:(j - j0) % 2 * D + D]
                    for i, (k, start) in enumerate(parts):
                        last = nc.tensor.matmul(o, vb[:, start:start + P], w_out[:, k, :],
                                                start=(i == 0), stop=(i == len(parts) - 1))
                last.then_inc(s_vw, 1)

        def vw_hi(act, b, groups=range(3)):
            for g in groups:
                j0, j1 = VGROUPS[g]
                at = len(VGROUPS) * b + g
                act.wait_ge(s_vw, vw_base[0] + at + 1)
                src = banks[:, 4 + 2 * (at % 2):4 + 2 * (at % 2) + (j1 - j0) // 2, :]
                nc.scalar.activation(VW[:, 0, b, j0:j1, :].rearrange("p (a b) n -> p a (b n)", b=2), src,
                                     ACT.Copy, scale=AS).then_inc(s_vh, 1)

        def vw_lo(dve, b, groups=range(3)):
            for g in groups:
                j0, j1 = VGROUPS[g]
                at = len(VGROUPS) * b + g
                dve.wait_ge(s_vh, vw_base[0] + at + 1)
                src = banks[:, 4 + 2 * (at % 2):4 + 2 * (at % 2) + (j1 - j0) // 2, :]
                nc.vector.scalar_tensor_tensor(
                    out=VW[:, 1, b, j0:j1, :].rearrange("p (a b) n -> p a (b n)", b=2), in0=src, scalar=AS,
                    in1=VW[:, 0, b, j0:j1, :].rearrange("p (a b) n -> p a (b n)", b=2),
                    op0=ALU.mult, op1=ALU.subtract).then_inc(s_vl, 1)

        vw_base = [0]
        attention1 = {}

        def setup():
            def k_spread_lo(engine, b):
                for c in range(C):
                    engine.tensor_tensor(
                        G0[:, 1, b, c, :].rearrange("p (h k) -> p h k", k=SK),
                        kT0[:, 1, c, b * SK:(b + 1) * SK].unsqueeze(1).to_broadcast([P, H // C, SK]),
                        mask16.unsqueeze(2).to_broadcast([P, H // C, SK]), ALU.mult).then_inc(s_g0l, 1)

            def sync(sp):
                sp.dma_start(ctx_sb[0:SK], a["ctx_1024"].rearrange("b k d -> k b d")).then_inc(s_w, 16)
                sp.dma_start(wkv0, a["L0_xattn_W_kv"].rearrange("(c p) n -> p c n", p=P)).then_inc(s_w, 16)
                sp.dma_start(wo0, a["L0_xattn_W_o"].rearrange("(c p) n -> p c n", p=P)).then_inc(s_w, 16)
                sp.dma_start(bkv[0:1], a["L0_xattn_b_kv"].rearrange("(a n) -> a n", a=1)).then_inc(s_w, 16)
                sp.dma_start(b_row[:], a["L0_xattn_b_o"].rearrange("(a n) -> a n", a=1).to_broadcast([P, D])).then_inc(s_w, 16)
                for lo, name in ((0, "g_xattn"), (2, "g_ffn"), (4, "L1_xattn_gate")):
                    n = a[name].shape[0]
                    sp.dma_start(gates[:, lo:lo + n], a[name].rearrange("(a n) -> a n", a=1).to_broadcast([P, n])).then_inc(s_w, 16)
                for b in range(B):
                    sp.dma_start(x_res[:, b * TB:(b + 1) * TB, :],
                                 a["x"][b].rearrange("(t p) d -> p t d", p=P)).then_inc(s_x, 16)
                sp.wait_ge(s_vl, len(VGROUPS) * B)
                sp.wait_ge(s_g0, C * B)
                sp.wait_ge(s_g0l, C * B)

            def gpsimd(pool, early):
                nc.gpsimd.memset(ident[:], 0.0).then_inc(s_c, 1)
                nc.gpsimd.memset(mask, 1.0).then_inc(s_c, 1)
                nc.gpsimd.memset(ones, 1.0).then_inc(s_c, 1)
                nc.gpsimd.memset(VB0, 0.0).then_inc(s_c, 1)
                nc.gpsimd.memset(S[:, :, HK:HKP], 0.0).then_inc(s_c, 1)
                nc.gpsimd.memset(minus_half, -0.5).then_inc(s_c, 1)
                nc.gpsimd.memset(eps, EPS).then_inc(s_c, 1)
                nc.gpsimd.memset(eps2, EPS * EPS / (1.0 + EPS)).then_inc(s_c, 1)
                pool.wait_ge(s_c, 8)
                nc.gpsimd.affine_select(out=ident[:], in_=ident[:], compare_op=ALU.not_equal, fill=1.0, base=0,
                                        pattern=[[-1, P]], channel_multiplier=1).then_inc(s_c, 1)
                nc.gpsimd.affine_select(out=mask, in_=mask, compare_op=ALU.is_ge, fill=0.0, base=0,
                                        pattern=[[-HD0, H // C]], channel_multiplier=1).then_inc(s_c, 1)
                pool.wait_ge(s_c, 10)
                nc.gpsimd.affine_select(out=mask, in_=mask, compare_op=ALU.is_ge, fill=0.0, base=HD0 - 1,
                                        pattern=[[HD0, H // C]], channel_multiplier=-1).then_inc(s_c, 1)
                nc.gpsimd.tensor_copy(ident16[:], ident[:]).then_inc(s_c, 1)
                pool.wait_ge(s_c, 12)
                nc.gpsimd.tensor_copy(mask16, mask).then_inc(s_c, 1)
                pool.wait_ge(s_c, 13)
                pool.wait_ge(s_kh, 1)
                for b in range(B):
                    for c in range(C):
                        nc.gpsimd.tensor_tensor(
                            G0[:, 0, b, c, :].rearrange("p (h k) -> p h k", k=SK),
                            kT0[:, 0, c, b * SK:(b + 1) * SK].unsqueeze(1).to_broadcast([P, H // C, SK]),
                            mask16.unsqueeze(2).to_broadcast([P, H // C, SK]), ALU.mult).then_inc(s_g0, 1)
                nc.gpsimd.tensor_tensor(kT0[:, 1], k_full, kT0[:, 0], ALU.subtract).then_inc(s_kl, 1)
                early(0)
                pool.wait_ge(s_kl, 1)
                for b in range(B - 1):
                    k_spread_lo(nc.gpsimd, b)
                early(1)
                return 2

            def scalar(act):
                act.wait_ge(s_w, 8 * 16)
                nc.scalar.activation(gtanh[:], gates[:], ACT.Tanh).then_inc(s_gt, 1)
                act.wait_ge(s_ct, 1)
                nc.scalar.copy(ctxT[:], banks[:, 0:2, 0:KB]).then_inc(s_ctc, 1)
                act.wait_ge(s_kc, 1 + 2 * C)
                nc.scalar.copy(kT0[:, 0], k_full).then_inc(s_kh, 1)
                for b in range(B):
                    vw_hi(act, b)

            def tensor(pe):
                pe.wait_ge(s_w, 8 * 16)
                pe.wait_ge(s_c, 9)
                for c in range(C):
                    for b in range(B):
                        last = nc.tensor.transpose(banks[:, c, b * SK:(b + 1) * SK],
                                                   ctx_sb[0:SK, b, c * P:(c + 1) * P], ident[0:SK, 0:SK])
                last.then_inc(s_ct, 1)
                pe.wait_ge(s_ws, C + 1)
                for s in range(2):
                    for g in range(C):
                        last = nc.tensor.matmul(banks[:, 4, s * C + g:s * C + g + 1], bkvs[0:1, s, g * P:(g + 1) * P],
                                                ones[0:1, 0:1], start=True, stop=True)
                last.then_inc(s_kv, 1)
                pe.wait_ge(s_ctc, 1)
                for s in (1, 0):
                    for g in range(C):
                        for c in range(C):
                            last = nc.tensor.matmul(banks[:, 2 * s + g, 0:KB], wkv0s[:, c, s, g * P:(g + 1) * P],
                                                    ctxT[:, c, :], start=(c == 0), stop=(c == C - 1))
                    last.then_inc(s_kv, 1)
                for b in range(B):
                    pe.wait_ge(s_vb, C * (b + 1))
                    vw_product(pe, b, VB0[:, b % 2], W0, C, wo0)
                pe.wait_ge(s_g0, C * B)
                pe.wait_ge(s_g0l, C * B)

            def vector(dve, early):
                dve.wait_ge(s_w, 8 * 16)
                for c in range(C):
                    nc.vector.tensor_copy(wkv0s[:, c].rearrange("p s (h d) -> p s h d", d=HD0),
                                          wkv0[:, c].rearrange("p (h s d) -> p s h d", s=2, d=HD0)).then_inc(s_ws, 1)
                nc.vector.tensor_copy(bkvs[0:1].rearrange("p s (h d) -> p s h d", d=HD0),
                                      bkv[0:1].rearrange("p (h s d) -> p s h d", s=2, d=HD0)).then_inc(s_ws, 1)
                dve.wait_ge(s_gt, 1)
                nc.vector.tensor_scalar(gscale[:, 0:1], gtanh[:, 0:1], 1.0 / (AS * PS), None, ALU.mult).then_inc(s_gs, 1)
                nc.vector.tensor_copy(gscale[:, 1:2], gtanh[:, 2:3]).then_inc(s_gs, 1)
                nc.vector.tensor_scalar(gscale[:, 2:3], gtanh[:, 1:2], gtanh[:, 4:5], 1.0 / (AS * PS), ALU.mult, ALU.mult).then_inc(s_gs, 1)
                nc.vector.tensor_scalar(gscale[:, 3:4], gtanh[:, 3:4], 1.0 / (AS * AS), None, ALU.mult).then_inc(s_gs, 1)
                nc.vector.tensor_scalar(b_row[:], b_row[:], gtanh[:, 0:1], None, ALU.mult).then_inc(s_gs, 1)
                dve.wait_ge(s_kv, 1)
                nc.vector.tensor_copy(bias_cols.rearrange("p s c -> p (s c)"), banks[:, 4, 0:2 * C]).then_inc(s_kc, 1)
                dve.wait_ge(s_kc, 1)
                dve.wait_ge(s_kv, 2)
                for g in range(C):
                    nc.vector.tensor_scalar(vT0[:, g], banks[:, 2 + g, 0:KB], bias_cols[:, 1, g:g + 1], None,
                                            ALU.add).then_inc(s_kc, 1)
                dve.wait_ge(s_kc, 1 + C)
                dve.wait_ge(s_c, 13)

                def v_spread(b):
                    wait(dve, s_vw, len(VGROUPS) * (b - 1))
                    for c in range(C):
                        o = P + c * (W0 + P)
                        nc.vector.tensor_tensor(
                            VB0[:, b % 2, o:o + W0].rearrange("p (h k) -> p h k", k=SK),
                            vT0[:, c, b * SK:(b + 1) * SK].unsqueeze(1).to_broadcast([P, H // C, SK]),
                            mask.unsqueeze(2).to_broadcast([P, H // C, SK]), ALU.mult).then_inc(s_vb, 1)

                v_spread(0)
                v_spread(1)
                dve.wait_ge(s_kv, 3)
                for g in range(C):
                    nc.vector.tensor_scalar(k_full[:, g], banks[:, g, 0:KB], bias_cols[:, 0, g:g + 1], AS,
                                            ALU.add, ALU.mult).then_inc(s_kc, 1)
                for b in range(B):
                    vw_lo(dve, b)
                    if b + 2 < B:
                        v_spread(b + 2)
                    if b in (B - 3, B - 2):
                        early(b + 3 - B)
                    if b == B - 2:
                        dve.wait_ge(s_kl, 1)
                        k_spread_lo(nc.vector, B - 1)

            return sync, gpsimd, scalar, tensor, vector

        def attention(name, before, pieces, Gof, layer, softmax_scale, ln_eps, affine, combine,
                      after=None):
            stats_done = sem(name + "_stats")
            rstd_done = sem(name + "_rstd")
            xn_done = sem(name + "_xn")
            xin_done = sem(name + "_xn_ready")
            bias_done = sem(name + "_bias_added")
            tx_done = sem(name + "_x_transposed")
            xhi_done = sem(name + "_x_hi")
            xlo_done = sem(name + "_x_lo")
            sc_done = sem(name + "_scores")
            max_done = sem(name + "_max")
            nmax_done = sem(name + "_scaled_max")
            exp_done = sem(name + "_exp")
            sum_done = sem(name + "_sum")
            rec_done = sem(name + "_recip")
            nrm_done = sem(name + "_normalised")
            tp_done = sem(name + "_p_transposed")
            phi_done = sem(name + "_p_hi")
            plo_done = sem(name + "_p_lo")
            pv_done = sem(name + "_pv")
            epi_done = sem(name + "_residual")
            bn_done = sem(name + "_bn")
            eps_done = sem(name + "_eps")
            if combine:
                idx_done = sem(name + "_idx")
                got = [sem(name + "_rows_0"), sem(name + "_rows_1")]
                comb_a = sem(name + "_first_expert_added")
                comb_done = sem(name + "_experts_added")
            pX = banks[:, 0, 0:C * P].rearrange("p (c n) -> p c n", c=C)
            pS = banks[:, 1:4, :]
            pT = banks[:, 4:7, :].rearrange("p a b -> p (a b)")[:, 0:HKP]
            pO = banks[:, 7, 0:D]
            per = 2 if affine else 1
            sync_before, gpsimd_before, scalar_before, tensor_before, vector_before = before
            nothing = ({}, lambda: None)
            sync_after, gpsimd_after, scalar_after, tensor_after, vector_after = after or [lambda eng: nothing] * 5
            if after:
                attention1.update(xlo_done=xlo_done, exp_done=exp_done, plo_done=plo_done, epi_done=epi_done)

            def tile(t):
                return x_res[:, bass.ds(t, 1), :].rearrange("p a d -> p (a d)")

            FIRST, LAST = -5 if combine else -4, T + 2
            LO, HI = 4, T - 6 if combine else T - 4

            UNROLL = 4

            def ok(t):
                return not isinstance(t, int) or 0 <= t < T

            EARLY = 3 if combine else 2

            def drive(eng, step, first, tail):
                for s in range(first, LO):
                    step(s, s % 2, s // 2)
                with eng.Fori(0, (HI - LO) // UNROLL) as i:
                    for k in range(UNROLL):
                        step(UNROLL * i + (LO + k), k % 2, UNROLL // 2 * i + (LO + k) // 2)
                for s in range(HI - (HI - LO) % UNROLL, LAST + 1):
                    step(s, s % 2, s // 2)
                    if s in tail:
                        tail[s]()

            with nc.Block() as block:
                @block.sync
                def _(sp):
                    sync_before(sp)
                    if layer == 0:
                        w1_loads(sp)
                    else:
                        ffn_loads(sp)
                    sync_after(sp)

                @block.vector
                def _(dve):
                    def maximum(t, par, b):
                        h0, n = HEADS_UP_TO[b], HEADS_OF_BANK[b]
                        dve.wait_ge(sc_done, 3 * t + (b + 1))
                        nc.vector.tensor_reduce(smax[:, par, h0:h0 + n],
                                                pS[:, b, 0:n * SK].rearrange("p (h k) -> p h k", h=n),
                                                AX, ALU.max).then_inc(max_done, 1)

                    def scaled_maximum(t, par, b):
                        heads = slice(HEADS_UP_TO[b], HEADS_UP_TO[b + 1])
                        dve.wait_ge(max_done, 3 * t + (b + 1))
                        nc.vector.tensor_scalar(nmax[:, par, heads], smax[:, par, heads], -softmax_scale, None,
                                                ALU.mult).then_inc(nmax_done, 1)

                    def add_expert(t, k):
                        dve.wait_ge(got[k], 16 * (t + 1))
                        if k:
                            dve.wait_ge(comb_a, t + 1)
                        nc.vector.scalar_tensor_tensor(
                            out=tile(t), in0=yrows[:, k, :], scalar=topw[:, k, bass.ds(t, 1)],
                            in1=tile(t), op0=ALU.mult, op1=ALU.add).then_inc(comb_done if k else comb_a, 1)

                    def step(s, par, pair):
                        odd = 1 - par
                        if combine and ok(s + 4):
                            add_expert(s + 4, 0)
                        if ok(s + 3):
                            t = s + 3
                            dve.wait_ge(rstd_done, t + 1)
                            wait(dve, tx_done, t - 1)
                            nc.vector.tensor_scalar(xnb[:, odd, :], tile(t), mv[:, odd, 0:1], rstd[:, odd, 0:1],
                                                    ALU.subtract, ALU.mult).then_inc(xn_done, 1)
                        if combine and ok(s + 4):
                            add_expert(s + 4, 1)
                            dve.wait_ge(comb_done, s + 5)
                        if ok(s - 2):
                            t = s - 2
                            dve.wait_ge(phi_done, t + 1)
                            nc.vector.scalar_tensor_tensor(
                                out=PT[:, par, 1].rearrange("p j n -> p (j n)"), in0=pT, scalar=PS,
                                in1=PT[:, par, 0].rearrange("p j n -> p (j n)"),
                                op0=ALU.mult, op1=ALU.subtract).then_inc(plo_done, 1)
                        if ok(s + 4):
                            wait(dve, stats_done, s + 3)
                        if ok(s - 3):
                            t = s - 3
                            dve.wait_ge(pv_done, t + 1)
                            dve.wait_ge(bias_done, t + 1)
                            nc.vector.scalar_tensor_tensor(out=tile(t), in0=pO, scalar=gscale[:, layer:layer + 1],
                                                           in1=tile(t), op0=ALU.mult, op1=ALU.add).then_inc(epi_done, 1)
                        if ok(s + 4):
                            nc.vector.bn_stats(bst[:, par, :], tile(s + 4)).then_inc(bn_done, 1)
                        if ok(s + 1):
                            maximum(s + 1, odd, 0)
                        if ok(s + 4):
                            dve.wait_ge(bn_done, s + 5)
                        if ok(s + 1):
                            maximum(s + 1, odd, 1)
                        if ok(s + 4):
                            nc.vector.bn_aggr(mv[:, par, :], bst[:, par, :]).then_inc(stats_done, 1)
                        if ok(s + 1):
                            for b in range(2):
                                scaled_maximum(s + 1, odd, b)
                        if ok(s):
                            dve.wait_ge(exp_done, H * (s + 1))
                            nc.vector.tensor_reduce(ssum[:, par, :], S[:, par, 0:HK].rearrange("p (h k) -> p h k", k=SK),
                                                    AX, ALU.add).then_inc(sum_done, 1)
                        if ok(s + 1):
                            maximum(s + 1, odd, 2)
                        if ok(s):
                            dve.wait_ge(sum_done, s + 1)
                            wait(dve, nrm_done, s - 1)
                            nc.vector.reciprocal(srec[:, par, :], ssum[:, par, :]).then_inc(rec_done, 1)
                        if ok(s + 1):
                            scaled_maximum(s + 1, odd, 2)
                        if ok(s + 2):
                            t = s + 2
                            dve.wait_ge(xhi_done, t + 1)
                            nc.vector.tensor_tensor(xT[:, par, 1], pX, xT[:, par, 0], ALU.subtract).then_inc(xlo_done, 1)
                    def early(k):
                        if layer == 0 and k == 0:
                            dve.wait_ge(s_x, 16 * B)
                        step(FIRST + k, (FIRST + k) % 2, 0)
                    vector_before(dve, early)
                    tail, rest = vector_after(dve)
                    drive(dve, step, FIRST + EARLY, tail)
                    rest()

                @block.scalar
                def _(act):
                    def step(s, par, pair):
                        if ok(s):
                            wait(act, tp_done, s - 1)
                            for h in range(H):
                                b = sum(h >= end for end in HEADS_UP_TO[1:])
                                at = (h - HEADS_UP_TO[b]) * SK
                                if at == 0:
                                    act.wait_ge(nmax_done, 3 * s + (b + 1))
                                nc.scalar.activation(S[:, par, h * SK:(h + 1) * SK], pS[:, b, at:at + SK], ACT.Exp,
                                                     bias=nmax[:, par, h:h + 1], scale=softmax_scale).then_inc(exp_done, 1)
                            if layer == 0:
                                w1_hi(act, s, par, pair)
                        if ok(s - 1):
                            t, q = s - 1, 1 - par
                            act.wait_ge(tp_done, t + 1)
                            wait(act, pv_done, t - 1)
                            nc.scalar.activation(PT[:, q, 0].rearrange("p j n -> p (j n)"), pT, ACT.Copy,
                                                 scale=PS).then_inc(phi_done, 1)
                        if ok(s + 2):
                            t = s + 2
                            act.wait_ge(tx_done, t + 1)
                            wait(act, sc_done, 3 * (t - 1))
                            nc.scalar.copy(xT[:, par, 0], pX).then_inc(xhi_done, 1)
                    scalar_before(act)
                    tail, rest = scalar_after(act)
                    drive(act, step, FIRST, tail)
                    rest()

                @block.gpsimd
                def _(pool):
                    def index(t):
                        wait(pool, comb_done, t)
                        nc.gpsimd.tensor_copy(idx_now[:], pos[:, :, bass.ds(t, 1)].rearrange("p a b -> p (a b)")).then_inc(idx_done, 1)

                    def gather(t):
                        for k in range(2):
                            nc.gpsimd.indirect_dma_start(yrows[:, k, :], None, ys, bass.IndirectOffsetOnAxis(
                                ap=idx_now[:, k:k + 1], axis=0)).then_inc(got[k], 16)

                    def step(s, par, pair):
                        odd = 1 - par
                        if combine and ok(s + 5):
                            index(s + 5)
                            pool.wait_ge(idx_done, s + 6)
                        if ok(s + 3):
                            t = s + 3
                            pool.wait_ge(xn_done, t + 1)
                            if affine:
                                nc.gpsimd.tensor_tensor(xnb[:, odd, :], xnb[:, odd, :], ln_gamma, ALU.mult).then_inc(xin_done, 1)
                            nc.gpsimd.tensor_tensor(tile(t), tile(t), b_row[:], ALU.add).then_inc(bias_done, 1)
                        if combine and ok(s + 5):
                            gather(s + 5)
                        if affine and ok(s + 3):
                            pool.wait_ge(xin_done, 2 * (s + 3) + 1)
                            nc.gpsimd.tensor_tensor(xnb[:, odd, :], xnb[:, odd, :], ln_beta, ALU.add).then_inc(xin_done, 1)
                        if ok(s + 4):
                            t = s + 4
                            pool.wait_ge(stats_done, t + 1)
                            wait(pool, xn_done, t - 1)
                            nc.gpsimd.tensor_tensor(rstd[:, par, 1:2], mv[:, par, 1:2], ln_eps, ALU.add).then_inc(eps_done, 1)
                            pool.wait_ge(eps_done, t + 1)
                            nc.gpsimd.tensor_tensor(rstd[:, par, 0:1], rstd[:, par, 1:2], minus_half, ALU.pow).then_inc(rstd_done, 1)
                        if layer == 0 and ok(s):
                            w1_lo(pool, s)
                        if ok(s):
                            pool.wait_ge(rec_done, s + 1)
                            z = S[:, par, 0:HK].rearrange("p (h k) -> p h k", k=SK)
                            nc.gpsimd.tensor_tensor(z, z, srec[:, par, :].unsqueeze(2).to_broadcast([P, H, SK]),
                                                    ALU.mult).then_inc(nrm_done, 1)
                    def early(k):
                        step(FIRST + k, (FIRST + k) % 2, 0)
                    done = gpsimd_before(pool, early)
                    tail, rest = gpsimd_after(pool)
                    drive(pool, step, FIRST + done, tail)
                    rest()

                @block.tensor
                def _(pe):
                    def scores(t, par, b, batch):
                        wait(pe, exp_done, H * (t - 1) + HEADS_UP_TO[b + 1])
                        for bank, o0, o1, c, g0 in pieces:
                            if bank != b:
                                continue
                            cs = c if isinstance(c, tuple) else (c,)
                            n = 0
                            for cc in cs:
                                for px, pg in ((0, 0), (1, 0), (0, 1)):
                                    last = nc.tensor.matmul(
                                        banks[:, 1 + bank, o0:o1], xT[:, par, px, cc, :], Gof(pg, batch, cc)[:, g0:g0 + o1 - o0],
                                        start=(n == 0), stop=(n == 3 * len(cs) - 1))
                                    n += 1
                        last.then_inc(sc_done, 1)

                    def step(s, par, b1, b2):
                        odd = 1 - par
                        if ok(s + 1):
                            pe.wait_ge(xlo_done, s + 2)
                            scores(s + 1, odd, 0, b1)
                            scores(s + 1, odd, 1, b1)
                        if ok(s - 1):
                            t = s - 1
                            pe.wait_ge(nrm_done, t + 1)
                            wait(pe, plo_done, t)
                            for j in range(J):
                                last = nc.tensor.transpose(pT[:, j * P:(j + 1) * P], S[:, odd, j * P:(j + 1) * P], ident[:])
                            last.then_inc(tp_done, 1)
                        if ok(s + 1):
                            scores(s + 1, odd, 2, b1)
                        if ok(s + 2):
                            t = s + 2
                            pe.wait_ge(xin_done if affine else xn_done, per * (t + 1))
                            wait(pe, xlo_done, t)
                            for c in range(C):
                                last = nc.tensor.transpose(pX[:, c, :], xnb[:, par, c * P:(c + 1) * P], ident[:])
                            last.then_inc(tx_done, 1)
                        if ok(s - 2):
                            t = s - 2
                            pe.wait_ge(plo_done, t + 1)
                            wait(pe, epi_done, t)
                            n = 0
                            for pp, pv in ((0, 0), (1, 0), (0, 1)):
                                for j in range(J):
                                    last = nc.tensor.matmul(pO, PT[:, par, pp, j, :], VW[:, pv, b2, j, :],
                                                            start=(n == 0), stop=(n == 3 * J - 1))
                                    n += 1
                            last.then_inc(pv_done, 1)

                    def batches(s):
                        return min(max(s + 1, 0), T - 1) // TB, min(max(s - 2, 0), T - 1) // TB

                    tensor_before(pe)
                    tail, rest = tensor_after(pe)
                    s = FIRST
                    while s <= LAST:
                        n = 0
                        while LO <= s and s + n + 1 <= T - 3 and batches(s) == batches(s + n + 1):
                            n += 1
                        if n >= 3:
                            n = (n + 1) // 2
                            with pe.Fori(0, n) as i:
                                for k in range(2):
                                    step(2 * i + (s + k), (s + k) % 2, *batches(s))
                            s += 2 * n
                        else:
                            step(s, s % 2, *batches(s))
                            if s in tail:
                                tail[s]()
                            s += 1
                    rest()

        pieces0 = []
        for bank, (h0, n) in enumerate(zip(HEADS_UP_TO, HEADS_OF_BANK)):
            for c in range(C):
                lo, hi = max(h0, c * H // C), min(h0 + n, (c + 1) * H // C)
                if lo < hi:
                    pieces0.append((bank, (lo - h0) * SK, (hi - h0) * SK, c, (lo - c * H // C) * SK))
        TE = [P, T, E]
        WW = C * F
        Q1, Q2 = F // 2, WW // 2
        N1, N2 = E * WW // Q1, E * WW // Q2
        wA = view(region_a, 0, [E, 2 * WW], F16)
        wB = view(region_b, 0, [E, 2 * WW], F16)
        piece_a32, piece_a16 = view(region_a, 0, [N1, Q1]), view(region_a, 0, [N1, 2, Q1], F16)
        piece_b32, piece_b16 = view(region_b, 0, [N2, Q2]), view(region_b, 0, [N2, 2, Q2], F16)
        raw_last1 = view(work, 4 * HKP + 2 * D + 2 * C * P, [Q1])
        raw_last2 = view(work, 0, [2, Q2])
        GT = 4
        NG = T // GT
        g_o = 5 * WW
        xn_g = view(region_b, g_o, [2, GT, D])
        xs_g = view(region_b, g_o + 2 * GT * D, [2, GT, 2, D], F16)
        xT_g = view(region_b, g_o + 4 * GT * D, [2, 2, C, 2 * P])
        logits_T = wkv1_early[0:E, 0].rearrange("p a b n -> p a (b n)")
        w_o = WW
        stats = view(work, w_o, [T, 6])
        mv_all = view(work, w_o + 192, [T, 2])
        rs_all = view(work, w_o + 256, [2, T])
        r_o = w_o + 320
        wg = view(work, r_o, [C, E])
        bg = view(work, r_o + 16, [E])
        iota_e = view(work, r_o + 24, [E])
        b1_rows = view(work, r_o + 32, [P])
        tri = view(work, r_o + 160, [P], F16)
        ones16 = view(work, r_o + 224, [P], F16)
        logits = view(work, r_o + 288, [T, E])
        q_o = r_o + 288 + NCOL
        oh = [view(work, q_o, [T, E]), view(work, q_o + NCOL, [T, E])]
        tmp = view(work, q_o + 2 * NCOL, [T, E])
        sel16 = view(work, q_o + 3 * NCOL, [T, E], F16)
        i_o = q_o + 3 * NCOL + NCOL // 2
        incl = view(work, i_o, [E, T])
        top_v = view(work, i_o + NCOL, [6, T])
        c_o = i_o + NCOL + 6 * T
        iota_lo = view(work, c_o, [P], F16)
        iota_hi = view(work, c_o + 64, [NH], F16)
        token = view(work, c_o + 64 + NH // 2, [T], F16)
        h_o = c_o + 64 + NH // 2 + T // 2
        oh_lo = view(work, h_o, [2, 2, GT, P], F16)
        oh_hi = view(work, h_o + 2 * GT * P, [2, 2, GT, NH], F16)
        p_o = h_o + 2 * GT * (P + NH)
        pos_f = view(work, p_o, [2, T])
        lohi_i = view(work, p_o + 2 * T, [2, 2 * T], I32)
        lohi = view(work, p_o + 6 * T, [2, 2, T], F16)
        t_o = p_o + 8 * T
        tiles_i = view(work, t_o, [2, E], I32)
        tiles_f = view(work, t_o + 2 * E, [3, E])
        iota_tile = view(work, t_o + 5 * E, [NT])
        tile_cmp = view(work, t_o + 5 * E + NT, [NT, E])
        ones_t = view(work, t_o + 5 * E + NT * (E + 1), [T])
        te_f = view(work, t_o + 5 * E + NT * (E + 1) + T, [NT])
        slot_f = view(work, t_o + 5 * E + NT * (E + 2) + T, [NH])
        assert T * P <= 4096 and NH % 2 == 0
        assert t_o + 5 * E + NT * (E + 2) + T + NH <= 6900

        s_w1 = [sem("w1_pieces_loaded_0"), sem("w1_pieces_loaded_1")]
        s_w2 = [sem("w2_first_loaded"), sem("w2_rest_loaded")]
        s_w1h = sem("w1_hi")
        s_w1l = sem("w1_lo")
        s_whi = sem("w2_hi")
        s_wlo = sem("w2_lo")
        s_gl = sem("gate_inputs_loaded")
        s_gc = sem("gate_consts")
        s_b1t = sem("b1_transposed")
        s_b1 = sem("b1_columns")
        s_bn = sem("gate_bn")
        s_ag = sem("gate_bn_aggr")
        s_rs = sem("gate_rstd")
        s_xn = sem("gate_xn")
        s_xh = sem("gate_x_hi")
        s_xl = sem("gate_x_lo")
        s_tx = sem("gate_x_transposed")
        s_tc = sem("gate_x_transpose_copied")
        s_lt = sem("gate_logits_by_expert")
        s_lc = sem("gate_logits_copied")
        s_lg = sem("gate_logits")
        s_st = [sem("xs_written_0"), sem("xs_written_1")]
        s_r = sem("routing_step")
        s_se = sem("selected")
        s_ex = sem("gate_exp")
        s_pf = sem("prefix_counts")
        s_hot = sem("one_hots")
        s_heq = sem("one_hot_slots_unweighted")
        s_hm = sem("one_hots_used")
        s_slot = sem("slot_table")

        def w1_loads(sp):
            rows = a["L0_ffn_W1"].rearrange("e (c p) (h n) -> p (e c) h n", p=P, h=2)

            def load(i, par, dst):
                wait(sp, s_w1[par], 16 * i)
                sp.dma_start(dst, rows[:, bass.ds(i, 1), par, :].rearrange("p a n -> p (a n)")).then_inc(s_w1[par], 16)

            def place(i, par):
                return piece_a32[:, bass.ds(2 * i + (par + 1), 1), :].rearrange("p a n -> p (a n)")
            for par in range(2):
                load(0, par, place(0, par))
            with sp.Fori(1, N1 // 2 - 1) as i:
                for par in range(2):
                    load(i, par, place(i, par))
            load(N1 // 2 - 1, 0, place(N1 // 2 - 1, 0))
            load(N1 // 2 - 1, 1, raw_last1)

        def w1_piece(q):
            raw = (raw_last1 if isinstance(q, int) and q == N1 - 1 else
                   piece_a32[:, bass.ds(q + 1, 1), :].rearrange("p a n -> p (a n)"))
            return [raw] + [piece_a16[:, bass.ds(q, 1), part, :].rearrange("p a n -> p (a n)") for part in range(2)]

        def w1_hi(act, q, par, pair):
            raw, hi, _ = w1_piece(q)
            act.wait_ge(s_w1[par], 16 * pair + 16)
            wait(act, s_w1l, q)
            nc.scalar.activation(hi, raw, ACT.Copy, scale=WS).then_inc(s_w1h, 1)
            nc.scalar.activation(raw, raw, ACT.Copy, scale=WS).then_inc(s_w1h, 1)

        def w1_lo(pool, q):
            raw, hi, lo = w1_piece(q)
            pool.wait_ge(s_w1h, 2 * q + 2)
            nc.gpsimd.tensor_tensor(lo, raw, hi, ALU.subtract).then_inc(s_w1l, 1)

        def w2_loads(sp, experts, last, s_loaded):
            for e in experts:
                sp.dma_start(piece_b32[:, 2 * e + 2:2 * e + 4, :].rearrange("p a (f n) -> p (a f) n", n=D),
                             a["L0_ffn_W2"][e].rearrange("(f p) n -> p f n", p=P)).then_inc(s_loaded, 16)
            if last:
                sp.dma_start(raw_last2.rearrange("p a (f n) -> p (a f) n", n=D),
                             a["L0_ffn_W2"][E - 1].rearrange("(f p) n -> p f n", p=P)).then_inc(s_loaded, 16)

        def w2_raw(q):
            return piece_b32[:, q + 2, :] if q + 2 < N2 else raw_last2[:, q + 2 - N2, :]

        def w2_hi(act, q):
            act.wait_ge(s_w2[0], 16 * 5)
            if q >= 8:
                act.wait_ge(s_w2[1], 16 * 3)
            wait(act, s_wlo, q - 1)
            nc.scalar.activation(piece_b16[:, q, 0, :], w2_raw(q), ACT.Copy, scale=WS).then_inc(s_whi, 1)
            nc.scalar.activation(w2_raw(q), w2_raw(q), ACT.Copy, scale=WS).then_inc(s_whi, 1)

        def w2_lo(pool, q):
            pool.wait_ge(s_whi, 2 * q + 2)
            nc.gpsimd.tensor_tensor(piece_b16[:, q, 1, :], w2_raw(q), piece_b16[:, q, 0, :],
                                    ALU.subtract).then_inc(s_wlo, 1)

        pGX = banks[:, 0:2, :].rearrange("p a (c n) -> p a c n", c=C)
        pG = banks[:, 2, 0:NCOL]
        pPre = banks[:, 3, 0:NCOL].rearrange("p (t e) -> p t e", e=E)
        pTot = banks[:, 4, 0:NCOL].rearrange("p (t e) -> p t e", e=E)
        pB1 = banks[:, 5, 0:E * FC]
        pSlot = banks[:, 6, 0:NH]
        xs_t = xs.rearrange("(t p) d -> p t d", p=P)

        def pairs(eng, n, step):
            for t in range(2):
                step(t, t, 0)
            with eng.Fori(1, n // 2) as i:
                for k in range(2):
                    step(2 * i + k, k, i)

        def gating():
            with nc.Block() as block:
                @block.sync
                def _(sp):
                    sp.dma_start(wg, a["L0_ffn_Wg"].rearrange("(c p) e -> p c e", p=P)).then_inc(s_gl, 16)
                    sp.dma_start(bg, a["L0_ffn_bg"].rearrange("(a e) -> a e", a=1).to_broadcast([P, E])).then_inc(s_gl, 16)
                    sp.dma_start(b1_rows[0:E * FC], a["L0_ffn_b1"].rearrange("e (f p) -> (e f) p", p=P)).then_inc(s_gl, 16)
                    w2_loads(sp, range(1), False, s_w2[0])
                    for g in range(NG):
                        sp.wait_ge(s_xl, g + 1)
                        sp.wait_ge(s_xh, g + 1)
                        sp.dma_start(xs_t[:, GT * g:GT * (g + 1), :], xs_g[:, g % 2].rearrange("p t s d -> p t (s d)")).then_inc(s_st[g % 2], 16)
                        if g < 4:
                            w2_loads(sp, range(g + 1, min(g + 2, 4)), g == 3, s_w2[0])
                    for par in range(2):
                        sp.wait_ge(s_st[par], 16 * NG // 2)
                    sp.wait_ge(s_lg, NG)
                    w2_loads(sp, range(4, E - 1), False, s_w2[1])

                @block.gpsimd
                def _(pool):
                    nc.gpsimd.iota(iota_e, pattern=[[1, E]], base=-E, channel_multiplier=0,
                                   allow_small_or_imprecise_dtypes=True).then_inc(s_gc, 1)
                    nc.gpsimd.memset(tri, 1.0).then_inc(s_gc, 1)
                    nc.gpsimd.memset(ones16, 1.0).then_inc(s_gc, 1)
                    pool.wait_ge(s_gc, 3)
                    nc.gpsimd.affine_select(out=tri, in_=tri, compare_op=ALU.is_gt, fill=0.0, base=0,
                                            pattern=[[1, P]], channel_multiplier=-1).then_inc(s_gc, 1)
                    nc.gpsimd.iota(iota_lo, pattern=[[1, P]], base=0, channel_multiplier=0,
                                   allow_small_or_imprecise_dtypes=True).then_inc(s_gc, 1)
                    nc.gpsimd.iota(iota_hi, pattern=[[1, NH]], base=0, channel_multiplier=0,
                                   allow_small_or_imprecise_dtypes=True).then_inc(s_gc, 1)
                    nc.gpsimd.iota(token, pattern=[[P, T]], base=-T * P // 2, channel_multiplier=1,
                                   allow_small_or_imprecise_dtypes=True).then_inc(s_gc, 1)
                    nc.gpsimd.iota(iota_tile, pattern=[[1, NT]], base=0, channel_multiplier=0,
                                   allow_small_or_imprecise_dtypes=True).then_inc(s_gc, 1)
                    nc.gpsimd.memset(ones_t, 1.0).then_inc(s_gc, 1)

                    def reciprocal_roots(k, g0, g1):
                        cols = slice(GT * g0, GT * g1)
                        n = GT * (g1 - g0)
                        pool.wait_ge(s_ag, GT * g1)
                        nc.gpsimd.tensor_tensor(rs_all[:, 1, cols], mv_all[:, cols, 1], eps.to_broadcast([P, n]), ALU.add).then_inc(s_rs, 1)
                        pool.wait_ge(s_rs, 2 * k + 1)
                        nc.gpsimd.tensor_tensor(rs_all[:, 0, cols], rs_all[:, 1, cols], minus_half.to_broadcast([P, n]), ALU.pow).then_inc(s_rs, 1)

                    def x_lo(g):
                        pool.wait_ge(s_xh, g + 1)
                        wait(pool, s_st[g % 2], 16 * (g // 2))
                        nc.gpsimd.tensor_tensor(xs_g[:, g % 2, :, 1, :], xn_g[:, g % 2], xs_g[:, g % 2, :, 0, :],
                                                ALU.subtract).then_inc(s_xl, 1)
                    reciprocal_roots(0, 0, 1)
                    for g in range(NG):
                        if g + 1 < NG:
                            reciprocal_roots(g + 1, g + 1, g + 2)
                        x_lo(g)
                    for q in range(N2):
                        w2_lo(pool, q)

                @block.scalar
                def _(act):
                    act.wait_ge(s_b1t, 1)
                    nc.scalar.copy(b1_cols[:].rearrange("p e f -> p (e f)"), pB1).then_inc(s_b1, 1)

                    def logits_copy(g, par):
                        act.wait_ge(s_lt, g + 1)
                        nc.scalar.copy(logits_T[:, par], banks[0:E, 3 + par, :]).then_inc(s_lc, 1)

                    def step(g, par, h):
                        act.wait_ge(s_xn, GT * g + GT)
                        wait(act, s_st[par], 16 * h)
                        nc.scalar.copy(xs_g[:, par, :, 0, :], xn_g[:, par]).then_inc(s_xh, 1)
                        for pair in range(2):
                            act.wait_ge(s_tx, 2 * g + (pair + 1))
                            wait(act, s_lt, g - 1)
                            nc.scalar.copy(xT_g[:, par, pair], pGX[:, pair]).then_inc(s_tc, 1)
                        if not isinstance(g, int) or g > 0:
                            logits_copy(g - 1, 1 - par)
                    pairs(act, NG, step)
                    logits_copy(NG - 1, 1)
                    for q in range(N2):
                        w2_hi(act, q)
                        if q == N2 // 2:
                            act.wait_ge(s_se, 1)
                            nc.scalar.activation(top_v[:, 3, :], top_v[:, 3, :], ACT.Exp).then_inc(s_ex, 1)

                @block.tensor
                def _(pe):
                    pe.wait_ge(s_gl, 48)
                    nc.tensor.transpose(pB1, b1_rows[0:E * FC, :], ident[0:E * FC, 0:E * FC]).then_inc(s_b1t, 1)

                    def step(g, par, h):
                        pe.wait_ge(s_xn, GT * g + GT)
                        for pair in range(2):
                            wait(pe, s_tc, 2 * g + (pair - 1))
                            for j in range(2):
                                for c in range(C):
                                    last = nc.tensor.transpose(pGX[:, pair, c, j * P:(j + 1) * P],
                                                               xn_g[:, par, 2 * pair + j, c * P:(c + 1) * P], ident[:])
                            last.then_inc(s_tx, 1)
                        if not isinstance(g, int) or g > 0:
                            product(g - 1, 1 - par)
                        if not isinstance(g, int):
                            back(g - 2, par)

                    def product(g, par):
                        for pair in range(2):
                            pe.wait_ge(s_tc, 2 * g + (pair + 1))
                            for c in range(C):
                                last = nc.tensor.matmul(banks[0:E, 3 + par, pair * 2 * P:(pair + 1) * 2 * P], wg[:, c, :],
                                                        xT_g[:, par, pair, c, :], start=(c == 0), stop=(c == C - 1))
                        last.then_inc(s_lt, 1)

                    def back(g, par):
                        pe.wait_ge(s_lc, g + 1)
                        for j in range(GT):
                            last = nc.tensor.matmul(banks[:, 2, bass.ds(g * (GT * E) + j * E, E)],
                                                    logits_T[:, par, j * P:(j + 1) * P], ident[0:E, 0:E],
                                                    start=True, stop=True)
                        last.then_inc(s_lg, 1)
                    pairs(pe, NG, step)
                    product(NG - 1, 1)
                    back(NG - 2, 0)
                    back(NG - 1, 1)
                    pe.wait_ge(s_se, 2)
                    pe.wait_ge(s_gc, 4)
                    sel = sel16.rearrange("p t e -> p (t e)")
                    nc.tensor.matmul(banks[:, 3, 0:NCOL], tri, sel, start=True, stop=True).then_inc(s_pf, 1)
                    nc.tensor.matmul(banks[:, 4, 0:NCOL], ones16, sel, start=True, stop=True).then_inc(s_pf, 1)

                    def hot(g, par, first=False, last_one=False):
                        pe.wait_ge(s_hot, 2 * g + 2)
                        for k in range(2):
                            for j in range(GT):
                                last = nc.tensor.matmul(pSlot, oh_lo[:, par, k, j, :], oh_hi[:, par, k, j, :],
                                                        start=first and k == 0 and j == 0,
                                                        stop=last_one and k == 1 and j == GT - 1)
                        last.then_inc(s_hm, 1)
                    hot(0, 0, first=True)
                    hot(1, 1)
                    with pe.Fori(1, NG // 2 - 1) as i:
                        for par in range(2):
                            hot(2 * i + par, par)
                    hot(NG - 2, 0)
                    hot(NG - 1, 1, last_one=True)

                @block.vector
                def _(dve):
                    def group_stats(g):
                        for t in range(GT * g, GT * (g + 1)):
                            nc.vector.bn_stats(stats[:, t, :], x_res[:, t, :]).then_inc(s_bn, 1)
                        dve.wait_ge(s_bn, GT * (g + 1))
                        for t in range(GT * g, GT * (g + 1)):
                            nc.vector.bn_aggr(mv_all[:, t, :], stats[:, t, :]).then_inc(s_ag, 1)

                    def group_xn(g):
                        wait(dve, s_xl, g - 1)
                        wait(dve, s_tx, 2 * (g - 1))
                        wait(dve, s_xh, g - 1)
                        dve.wait_ge(s_rs, 2 * g + 2)
                        for j in range(GT):
                            t = GT * g + j
                            nc.vector.tensor_scalar(xn_g[:, g % 2, j, :], x_res[:, t, :], mv_all[:, t, 0:1],
                                                    rs_all[:, 0, t:t + 1], ALU.subtract, ALU.mult).then_inc(s_xn, 1)
                    group_stats(0)
                    group_stats(1)
                    for g in range(NG):
                        group_xn(g)
                        if g + 2 < NG:
                            group_stats(g + 2)

                    count = [0]

                    def link(instruction):
                        count[0] += 1
                        instruction.then_inc(s_r, 1)
                        dve.wait_ge(s_r, count[0])

                    def bt(v):
                        return v.unsqueeze(2).to_broadcast(TE)

                    def be(v):
                        return v.unsqueeze(1).to_broadcast(TE)

                    dve.wait_ge(s_lg, NG)
                    dve.wait_ge(s_gc, 4)
                    link(nc.vector.tensor_tensor(logits, pG.rearrange("p (t e) -> p t e", e=E), be(bg), ALU.add))
                    src = logits
                    for k in range(2):
                        link(nc.vector.tensor_reduce(top_v[:, k, :], src, AX, ALU.max))
                        link(nc.vector.tensor_tensor(tmp, src, bt(top_v[:, k, :]), ALU.is_equal))
                        link(nc.vector.tensor_tensor(tmp, tmp, be(iota_e), ALU.mult))
                        link(nc.vector.tensor_reduce(top_v[:, 2, :], tmp, AX, ALU.min))
                        link(nc.vector.tensor_tensor(oh[k], be(iota_e), bt(top_v[:, 2, :]), ALU.is_equal))
                        if k == 0:
                            link(nc.vector.scalar_tensor_tensor(out=logits, in0=oh[0], scalar=-1e30, in1=logits,
                                                                op0=ALU.mult, op1=ALU.add))
                    nc.vector.tensor_tensor(top_v[:, 3, :], top_v[:, 1, :], top_v[:, 0, :], ALU.subtract).then_inc(s_se, 1)
                    nc.vector.tensor_tensor(sel16, oh[0], oh[1], ALU.add).then_inc(s_se, 1)
                    dve.wait_ge(s_pf, 2)
                    dve.wait_ge(s_gc, 9)
                    for e in range(E):
                        link(nc.vector.tensor_tensor_scan(incl[:, e, :], ones_t, pTot[:, :, e], 0.0, ALU.mult, ALU.add))
                    link(nc.vector.tensor_scalar(tiles_i[:, 0, :], incl[:, :, T - 1], float(TT - 1), None, ALU.add))
                    link(nc.vector.tensor_scalar(tiles_i[:, 1, :], tiles_i[:, 0, :], TT.bit_length() - 1, None, ALU.arith_shift_right))
                    link(nc.vector.tensor_copy(tiles_f[:, 0, :], tiles_i[:, 1, :]))
                    link(nc.vector.tensor_tensor_scan(tiles_f[:, 1, :], ones_t[:, 0:E], tiles_f[:, 0, :], 0.0, ALU.mult, ALU.add))
                    link(nc.vector.tensor_tensor(tiles_f[:, 2, :], tiles_f[:, 1, :], tiles_f[:, 0, :], ALU.subtract))
                    link(nc.vector.tensor_scalar(tiles_f[:, 2, :], tiles_f[:, 2, :], float(TT), None, ALU.mult))
                    link(nc.vector.tensor_tensor(tmp, incl.rearrange("p e t -> p t e"), pTot, ALU.subtract))
                    link(nc.vector.tensor_tensor(tmp, tmp, pPre, ALU.add))
                    link(nc.vector.tensor_tensor(tmp, tmp, be(tiles_f[:, 2, :]), ALU.add))
                    for k in range(2):
                        link(nc.vector.tensor_tensor(oh[k], oh[k], tmp, ALU.mult))
                        link(nc.vector.tensor_reduce(pos_f[:, k, :], oh[k], AX, ALU.add))
                    link(nc.vector.tensor_copy(pos[:], pos_f))
                    flat = pos[:].rearrange("p a b -> p (a b)")
                    link(nc.vector.tensor_scalar(lohi_i[:, 0, :], flat, P - 1, None, ALU.bitwise_and))
                    link(nc.vector.tensor_scalar(lohi_i[:, 1, :], flat, P.bit_length() - 1, None, ALU.arith_shift_right))
                    link(nc.vector.tensor_copy(lohi.rearrange("p a k t -> p a (k t)"), lohi_i))

                    def hot(g, par, h):
                        four = bass.ds(GT * g, GT)
                        wait(dve, s_hm, g - 1)
                        nc.vector.tensor_tensor(oh_hi[:, par], iota_hi.unsqueeze(1).unsqueeze(1).to_broadcast([P, 2, GT, NH]),
                                                lohi[:, 1, :, four].unsqueeze(3).to_broadcast([P, 2, GT, NH]),
                                                ALU.is_equal).then_inc(s_heq, 1)
                        nc.vector.tensor_tensor(oh_lo[:, par], iota_lo.unsqueeze(1).unsqueeze(1).to_broadcast([P, 2, GT, P]),
                                                lohi[:, 0, :, four].unsqueeze(3).to_broadcast([P, 2, GT, P]),
                                                ALU.is_equal).then_inc(s_hot, 1)
                        dve.wait_ge(s_heq, g + 1)
                        nc.vector.tensor_tensor(oh_hi[:, par], oh_hi[:, par],
                                                token[:, four].unsqueeze(1).unsqueeze(3).to_broadcast([P, 2, GT, NH]),
                                                ALU.mult).then_inc(s_hot, 1)
                    pairs(dve, NG, hot)
                    row = [1, NT, E]
                    link(nc.vector.tensor_tensor(tile_cmp[0:1], iota_tile[0:1].unsqueeze(2).to_broadcast(row),
                                                 tiles_f[0:1, 1, :].unsqueeze(1).to_broadcast(row), ALU.is_ge))
                    link(nc.vector.tensor_reduce(te_f[0:1], tile_cmp[0:1], AX, ALU.add))
                    link(nc.vector.tensor_scalar(te_f[0:1], te_f[0:1], float(E - 1), None, ALU.min))
                    link(nc.vector.tensor_copy(tile_expert[:], te_f[0:1]))
                    dve.wait_ge(s_hm, NG)
                    link(nc.vector.tensor_scalar(slot_f, pSlot, float(T * P // 2), None, ALU.add))
                    nc.vector.tensor_copy(slot_token[:], slot_f).then_inc(s_slot, 1)
                    dve.wait_ge(s_ex, 1)
                    link(nc.vector.tensor_scalar(top_v[:, 4, :], top_v[:, 3, :], 1.0, None, ALU.add))
                    link(nc.vector.reciprocal(top_v[:, 5, :], top_v[:, 4, :]))
                    link(nc.vector.tensor_scalar(topw[:, 0, :], top_v[:, 5, :], gscale[:, 1:2], None, ALU.mult))
                    link(nc.vector.tensor_tensor(topw[:, 1, :], topw[:, 0, :], top_v[:, 3, :], ALU.mult))

        b2_all = view(work, 0, [E, D])
        m_o = E * D
        xg = view(work, m_o, [2, 2 * D], F16)
        xgT = view(work, m_o + 512, [2, C, TT], F16)
        hf = view(work, m_o + 1024, [2, 2 * TT])
        hh = view(work, m_o + 2048, [4, 2, 2, TT], F16)
        ysb = view(work, m_o + 4096, [2, D])
        s_b2 = sem("b2_loaded")
        s_gi = sem("moe_index")
        s_xg = [sem("moe_rows_0"), sem("moe_rows_1")]
        s_gt2 = sem("moe_transposed")
        s_gx = sem("moe_transpose_copied")
        s_up = sem("moe_up")
        s_ge = sem("moe_gelu")
        s_hi = sem("moe_hi")
        s_lo = sem("moe_lo")
        s_dn = sem("moe_down")
        s_ye = sem("moe_out_copied")
        s_yw = sem("moe_out_written")
        pXg = banks[:, 5, :].bitcast(F16).rearrange("p (s c n) -> p s c n", s=2, c=C)
        pY = banks[:, 4, :].rearrange("p (s d) -> p s d", s=2)
        ys_t = ys.rearrange("(i s p) d -> p i s d", s=2, p=P)

        def experts():
            with nc.Block() as block:
                @block.sync
                def _(sp):
                    sp.dma_start(b2_all, a["L0_ffn_b2"].rearrange("(a e) d -> a e d", a=1).to_broadcast([P, E, D])).then_inc(s_b2, 16)

                    def write(i):
                        sp.wait_ge(s_ye, i + 1)
                        sp.dma_start(ys_t[:, bass.ds(i, 1), :, :].rearrange("p a s d -> p (a s) d"), ysb).then_inc(s_yw, 16)
                    for i in range(KV_EARLY):
                        write(i)
                        wkv1_load(sp, i)
                    with sp.Fori(KV_EARLY, NT) as i:
                        write(i)

                @block.gpsimd
                def _(pool):
                    def index(i, par):
                        nc.gpsimd.tensor_copy(idx_ring[:, par, :], slot_token[:, bass.ds(2 * i, 2)]).then_inc(s_gi, 1)

                    def step(i, par, h):
                        wait(pool, s_gt2, i)
                        pool.wait_ge(s_gi, i + 1)
                        index(i + 1, 1 - par)
                        for s in range(2):
                            nc.gpsimd.indirect_dma_start(xg[:, s, :], None, xs, bass.IndirectOffsetOnAxis(
                                ap=idx_ring[:, par, s:s + 1], axis=0)).then_inc(s_xg[s], 16)
                    index(0, 0)
                    pairs(pool, NT + 1, step)
                    for s in range(2):
                        pool.wait_ge(s_xg[s], 16 * (NT + 1))

                @block.tensor
                def _(pe):
                    def transposes(i):
                        wait(pe, s_gx, i)
                        for s in range(2):
                            pe.wait_ge(s_xg[s], 16 * (i + 1))
                            for part in range(2):
                                for c in range(C):
                                    last = nc.tensor.transpose(pXg[:, part, c, s * P:(s + 1) * P],
                                                               xg[:, s, part * D + c * P:part * D + (c + 1) * P], ident16[:])
                        last.then_inc(s_gt2, 1)

                    def up(i, e, b):
                        wait(pe, s_ge, 8 * (i - 1) + 2 * b + 2)
                        for f in (2 * b, 2 * b + 1):
                            n = 0
                            for pw, px in ((0, 0), (0, 1), (1, 0)):
                                for c in range(C):
                                    o = (2 * c + f // 4) * 2 * Q1 + pw * Q1 + f % 4 * P
                                    last = nc.tensor.matmul(
                                        banks[:, b, (f % 2) * TT:(f % 2) * TT + TT],
                                        wA[:, bass.ds(e, 1), o:o + P].rearrange("p a m -> p (a m)"),
                                        xgT[:, px, c, :], start=(n == 0), stop=(n == 3 * C - 1))
                                    n += 1
                        last.then_inc(s_up, 1)

                    def down(i, e, b):
                        pe.wait_ge(s_lo, 4 * i + b + 1)
                        if b == 0:
                            wait(pe, s_ye, i)
                        for s in range(2):
                            for ph, pw in ((0, 0), (1, 0), (0, 1)):
                                for k in range(2):
                                    o = (b // 2) * 2 * Q2 + pw * Q2 + (2 * b + k) % 4 * D
                                    last = nc.tensor.matmul(
                                        pY[:, s, :], hh[:, b, ph, k, s * P:(s + 1) * P],
                                        wB[:, bass.ds(e, 1), o:o + D].rearrange("p a m -> p (a m)"),
                                        start=(b == 0 and s == 0 and ph == 0 and pw == 0 and k == 0),
                                        stop=(b == 3 and s == 1 and pw == 1 and k == 1),
                                        skip_group_check=True)
                        last.then_inc(s_dn, 1)

                    def expert(i):
                        return pe.value_load(tile_expert[0:1, bass.ds(i, 1)], min_val=0, max_val=E - 1)

                    def tile(i, before=None, e_before=None):
                        if before is not None:
                            down(before, e_before, 2)
                        e = expert(i)
                        pe.wait_ge(s_gx, i + 1)
                        up(i, e, 0)
                        if before is not None:
                            down(before, e_before, 3)
                        up(i, e, 1)
                        up(i, e, 2)
                        down(i, e, 0)
                        up(i, e, 3)
                        transposes(i + 1)
                        down(i, e, 1)
                        return e
                    transposes(0)
                    tile(0)
                    with pe.Fori(0, (NT - 1) // 2) as i:
                        e = tile(2 * i + 1, 2 * i, expert(2 * i))
                        tile(2 * i + 2, 2 * i + 1, e)
                    e_last = expert(NT - 1)
                    down(NT - 1, e_last, 2)
                    down(NT - 1, e_last, 3)

                @block.scalar
                def _(act):
                    b1f = b1_cols[:].rearrange("p e f -> p (e f)")
                    table_for(ACT.Gelu)

                    def tile(i):
                        e = act.value_load(tile_expert[0:1, bass.ds(i, 1)], min_val=0, max_val=E - 1)
                        for b in range(4):
                            act.wait_ge(s_up, 4 * i + b + 1)
                            wait(act, s_lo, 4 * i + b - 1)
                            for k in range(2):
                                nc.scalar.activation(hf[:, b % 2, k * TT:(k + 1) * TT], banks[:, b, k * TT:(k + 1) * TT],
                                                     ACT.Gelu, bias=b1f[:, bass.ds(e * FC + (2 * b + k), 1)],
                                                     scale=1.0 / WS).then_inc(s_ge, 1)
                    tile(0)
                    with act.Fori(1, NT) as i:
                        tile(i)

                @block.vector
                def _(dve):
                    def rows(i):
                        dve.wait_ge(s_gt2, i + 1)
                        nc.vector.tensor_copy(xgT.rearrange("p s c n -> p (s c n)"),
                                              pXg.rearrange("p s c n -> p (s c n)")).then_inc(s_gx, 1)

                    def hidden(i, b):
                        dve.wait_ge(s_ge, 8 * i + 2 * b + 2)
                        wait(dve, s_dn, 4 * (i - 1) + b + 1)
                        h_hi, h_lo = (hh[:, b, s].rearrange("p k n -> p (k n)") for s in range(2))
                        nc.vector.tensor_copy(h_hi, hf[:, b % 2, :]).then_inc(s_hi, 1)
                        dve.wait_ge(s_hi, 4 * i + b + 1)
                        nc.vector.tensor_tensor(h_lo, hf[:, b % 2, :], h_hi, ALU.subtract).then_inc(s_lo, 1)

                    def y_out(i):
                        e = dve.value_load(tile_expert[0:1, bass.ds(i, 1)], min_val=0, max_val=E - 1)
                        dve.wait_ge(s_dn, 4 * i + 4)
                        wait(dve, s_yw, 16 * i)
                        nc.vector.scalar_tensor_tensor(
                            out=ysb, in0=pY, scalar=1.0 / WS,
                            in1=b2_all[:, bass.ds(e, 1), :].to_broadcast([P, 2, D]),
                            op0=ALU.mult, op1=ALU.add).then_inc(s_ye, 1)

                    def tile(i, before=None):
                        hidden(i, 0)
                        if before is not None:
                            y_out(before)
                        hidden(i, 1)
                        hidden(i, 2)
                        rows(i + 1)
                        hidden(i, 3)
                    dve.wait_ge(s_b2, 16)
                    rows(0)
                    tile(0)
                    tile(1, 0)
                    with dve.Fori(1, NT - 1) as i:
                        tile(i + 1, i)
                    y_out(NT - 1)

        NP_ = INNER // P
        W1_ = 2 * SK
        GB = 3 * W1_
        G1 = view(region_a, 0, [2, B, C, HK], F16)
        kv1 = view(region_a, B * C * HK, [2, NP_, KB])
        w_out = view(region_b, 0, [NP_, D])
        wqT = view(region_b, NP_ * D, [NP_, D])
        ln_gamma = view(region_b, 2 * NP_ * D, [D])
        ln_beta = view(region_b, 2 * NP_ * D + D, [D])
        wkv1_last = view(region_b, vw_word, [C, 2, INNER // KV_PARTS])
        wq = view(region_b, vw_word + C * 2 * INNER, [C, INNER])
        VB1 = view(work, 2 * HKP, [P + NP_ * (W1_ + P)])
        kTB = view(work, 0, [2, NP_, W1_])
        yrows = view(work, 4 * HKP + 2 * D + 4 * C * P // 2, [2, D])
        assert 3 * C * INNER <= 2 * B * J * D // 2
        assert 2 * NP_ * D + 2 * D <= vw_word
        s_wkv1 = [sem("l1_kv_early_loaded"), sem("l1_kv_last_loaded")]
        s_wq = sem("l1_wq_loaded")
        s_l1 = sem("l1_rest_loaded")
        s_l1c = sem("l1_consts")
        s_l1b = sem("l1_bias_scaled")
        s_wt = sem("wq_transposed")
        s_wtc = sem("wq_copied")
        s_kv1 = sem("l1_kv")
        s_kvc = sem("l1_kv_copied")
        s_kb = sem("l1_k_spread")
        s_vb1 = sem("l1_v_spread_even")
        s_vb1a = sem("l1_v_spread_odd")
        s_g1 = sem("l1_g")
        s_g1h = sem("l1_g_hi")
        s_g1l = sem("l1_g_lo")

        def wkv1_part(i):
            return wkv1_early[:, i] if i < KV_EARLY else wkv1_last

        def wkv1_load(sp, i):
            src = a["L1_xattn_w_kv"].rearrange("(c p) (s i n) -> p c s i n", p=P, s=2, i=KV_PARTS)
            for s in range(2):
                sp.dma_start(wkv1_part(i)[:, :, s, :], src[:, :, s, i, :]).then_inc(s_wkv1[i // KV_EARLY], 16)

        def fold_layer1():
            vw_base[0] = len(VGROUPS) * B

            def k_spread(dve, b, pairs=slice(0, NP_)):
                wait(dve, s_g1, C * (b - 1))
                for h in range(2):
                    rows = slice(64 * h, 64 * h + 64)
                    nc.vector.tensor_copy(kTB[rows, b % 2, pairs, h * SK:(h + 1) * SK],
                                          kv1[rows, 0, pairs, b * SK:(b + 1) * SK]).then_inc(s_kb, 1)

            def v_spread(b, h):
                rows = slice(64 * h, 64 * h + 64)
                return (VB1[rows, P:P + NP_ * (W1_ + P)].rearrange("p (n w) -> p n w", n=NP_)[:, :, h * SK:(h + 1) * SK],
                        kv1[rows, 1, :, b * SK:(b + 1) * SK])

            def sync(sp):
                wkv1_load(sp, KV_EARLY)
                sp.dma_start(wq, a["L1_xattn_w_q"].rearrange("(c p) n -> p c n", p=P)).then_inc(s_wq, 16)
                sp.dma_start(w_out, a["L1_xattn_w_out"].rearrange("(c p) n -> p c n", p=P)).then_inc(s_l1, 16)
                for dst, name in ((b_row[:], "L1_xattn_b_out"), (ln_gamma, "L1_xattn_ln_gamma"), (ln_beta, "L1_xattn_ln_beta")):
                    sp.dma_start(dst, a[name].rearrange("(a n) -> a n", a=1).to_broadcast([P, D])).then_inc(s_l1, 16)
                sp.wait_ge(s_kb, 2 * (B + 1))
                sp.wait_ge(s_vb1, B)
                sp.wait_ge(s_vb1a, B)

            def gpsimd(pool, early):
                nc.gpsimd.memset(VB1, 0.0).then_inc(s_l1c, 1)
                nc.gpsimd.memset(kTB, 0.0).then_inc(s_l1c, 1)
                pool.wait_ge(s_yw, 16 * NT)
                pool.wait_ge(s_l1c, 2)
                pool.wait_ge(s_kvc, 2 * NP_)
                for b in range(B):
                    wait(pool, s_vw, vw_base[0] + len(VGROUPS) * b)
                    nc.gpsimd.tensor_copy(*v_spread(b, 0)).then_inc(s_vb1, 1)
                    if b == B - 2:
                        early(0)
                        early(1)
                return 2

            def scalar(act):
                for n in range(NP_):
                    act.wait_ge(s_kv1, 2 * (n + 1))
                    o = 6 * (n % 2)
                    nc.scalar.copy(kv1[:, :, n, :], banks[:, o:o + 2, 0:KB]).then_inc(s_kvc, 2)
                act.wait_ge(s_kvc, 2 * NP_)
                act.wait_ge(s_l1c, 2)

                def g_hi(b, c):
                    act.wait_ge(s_g1, C * b + c + 1)
                    nc.scalar.activation(G1[:, 0, b, c, 0:2 * GB].rearrange("p (a n) -> p a n", a=2), banks[:, 0:2, 0:GB],
                                         ACT.Copy, scale=AS).then_inc(s_g1h, 1)
                    nc.scalar.activation(G1[:, 0, b, c, 2 * GB:HK], banks[:, 2, 0:HK - 2 * GB],
                                         ACT.Copy, scale=AS).then_inc(s_g1h, 1)
                for b in range(B):
                    wait(act, s_vw, vw_base[0] + len(VGROUPS) * b)
                    nc.scalar.copy(*v_spread(b, 1)).then_inc(s_vb1a, 1)
                    g_hi(b, 0)
                    vw_hi(act, b, (0,))
                    g_hi(b, 1)
                    vw_hi(act, b, (1, 2))
                table_for(ACT.Exp)

            def vector(dve, early):
                dve.wait_ge(s_wt, 1)
                nc.vector.tensor_copy(wqT.rearrange("p n d -> p (n d)"),
                                      banks[:, 2:6, :].rearrange("p a b -> p (a b)")).then_inc(s_wtc, 1)
                dve.wait_ge(s_l1c, 2)
                dve.wait_ge(s_kvc, 2 * (NP_ - 1))
                k_spread(dve, 0, slice(0, NP_ - 1))
                dve.wait_ge(s_kvc, 2 * NP_)

                def g_lo(b, c):
                    dve.wait_ge(s_g1h, 2 * (C * b + c + 1))
                    nc.vector.scalar_tensor_tensor(
                        out=G1[:, 1, b, c, 0:2 * GB].rearrange("p (a n) -> p a n", a=2), in0=banks[:, 0:2, 0:GB],
                        scalar=AS, in1=G1[:, 0, b, c, 0:2 * GB].rearrange("p (a n) -> p a n", a=2),
                        op0=ALU.mult, op1=ALU.subtract).then_inc(s_g1l, 1)
                    nc.vector.scalar_tensor_tensor(
                        out=G1[:, 1, b, c, 2 * GB:HK], in0=banks[:, 2, 0:HK - 2 * GB], scalar=AS,
                        in1=G1[:, 0, b, c, 2 * GB:HK], op0=ALU.mult, op1=ALU.subtract).then_inc(s_g1l, 1)
                k_spread(dve, 0, slice(NP_ - 1, NP_))
                for b in range(B):
                    g_lo(b, 0)
                    if b + 1 < B:
                        k_spread(dve, b + 1)
                    if b == B - 2:
                        early(0)
                        early(1)
                    vw_lo(dve, b, (0,))
                    g_lo(b, 1)
                    vw_lo(dve, b, (1, 2))
                    if b == B - 2:
                        early(2)
                    if b == 0:
                        dve.wait_ge(s_l1, 64)
                        nc.vector.tensor_scalar(b_row[:], b_row[:], gtanh[:, 1:2], gtanh[:, 4:5], ALU.mult, ALU.mult).then_inc(s_l1b, 1)
                        nc.vector.tensor_scalar(ln_gamma, ln_gamma, (1.0 + EPS) ** -0.5, None, ALU.mult).then_inc(s_l1b, 1)
                nc.vector.memset(S[:, :, HK:HKP], 0.0).then_inc(s_l1b, 1)

            def tensor(pe):
                for n in range(NP_):
                    if n == 0:
                        pe.wait_ge(s_wkv1[0], 32 * KV_EARLY)
                    if n == KV_EARLY * NP_ // KV_PARTS:
                        pe.wait_ge(s_wkv1[1], 32)
                    if n == NP_ - 2:
                        pe.wait_ge(s_wq, 16)
                        for m in range(NP_):
                            for c in range(C):
                                last = nc.tensor.transpose(banks[:, 2 + m // 2, (m % 2) * D + c * P:(m % 2) * D + (c + 1) * P],
                                                           wq[:, c, m * P:(m + 1) * P], ident[:])
                        last.then_inc(s_wt, 1)
                    wait(pe, s_kvc, 2 * (n - 1))
                    for s in range(2):
                        for c in range(C):
                            o = n % (NP_ // KV_PARTS) * P
                            last = nc.tensor.matmul(banks[:, 6 * (n % 2) + s, 0:KB],
                                                    wkv1_part(n * KV_PARTS // NP_)[:, c, s, o:o + P], ctxT[:, c, :],
                                                    start=(c == 0), stop=(c == C - 1))
                        last.then_inc(s_kv1, 1)
                pe.wait_ge(s_wtc, 1)
                pe.wait_ge(s_kvc, 2 * NP_)
                pe.wait_ge(s_l1, 64)

                def g_product(b, c):
                    wait(pe, s_g1l, 2 * (C * b + c))
                    for n in range(NP_):
                        last = nc.tensor.matmul(banks[:, n // 3, (n % 3) * W1_:(n % 3) * W1_ + W1_],
                                                wqT[:, n, c * P:(c + 1) * P], kTB[:, b % 2, n, :], start=True, stop=True)
                    last.then_inc(s_g1, 1)
                for b in range(B):
                    pe.wait_ge(s_kb, 2 * (b + 2))
                    g_product(b, 0)
                    pe.wait_ge(s_vb1, b + 1)
                    pe.wait_ge(s_vb1a, b + 1)
                    vw_product(pe, b, VB1, W1_, NP_, w_out, (0,))
                    g_product(b, 1)
                    vw_product(pe, b, VB1, W1_, NP_, w_out, (1, 2))
                pe.wait_ge(s_g1l, 2 * C * B)

            return sync, gpsimd, scalar, tensor, vector

        GN = GT * P
        R2 = 2 * R
        f_o = B * C * HK
        U1r = view(region_a, f_o, [C, R2])
        V1r = view(region_a, f_o + 256, [F])
        U2r = view(region_a, f_o + 1280, [FC, R])
        V2r = view(region_a, f_o + 1792, [D])
        U1s = view(region_a, f_o + 2048, [2, C, R2], F16)
        V1s = view(region_a, f_o + 2304, [2, F], F16)
        U2s = view(region_a, f_o + 3328, [FC, R2], F16)
        V2s = view(region_a, f_o + 3840, [2, D], F16)
        fb1_rows = view(region_a, f_o + 4096, [P])
        fb1 = view(region_a, f_o + 4224, [FC])
        fbias = view(region_a, f_o + 4232, [D])
        fstats = view(region_a, f_o + 4488, [T, 6])
        fmv = view(region_a, f_o + 4680, [T, 2])
        frs = view(region_a, f_o + 4744, [2, T])
        fxT = view(region_a, f_o + 4808, [2, C, GN], F16)
        fq = view(region_a, f_o + 5832, [2, GN], F16)
        fh = view(region_a, 0, [4, GN])
        fhh = view(region_a, 4 * GN, [FC, 2, GN], F16)
        assert f_o + 6344 <= 16384 and 2 * GT * D + NG * GN // 2 <= vw_word
        fxn = view(region_b, 0, [GT, D])
        fct = view(region_b, GT * D, [GT, D])
        rank_s = view(region_b, 2 * GT * D, [NG, GN], F16)
        V1_BANKS = (1, 3, 4, 6)
        HI_ON_VECTOR = (3, 7)
        LEAD = 3
        TX1_AT, U1_AT, TX0_AT, Q_AT, V2_AT = 1, 3, 7, 2, (3, 5)
        s_fl = sem("ffn_loaded")
        s_fw = sem("ffn_weights_hi")
        s_fwl = sem("ffn_weights_lo")
        s_fbt = sem("ffn_bias_transposed")
        s_fb = sem("ffn_bias_columns")
        s_fbn = sem("ffn_bn")
        s_fag = sem("ffn_bn_aggr")
        s_frs = sem("ffn_rstd")
        s_fct = sem("ffn_centred")
        s_fxn = sem("ffn_xn")
        s_fba = sem("ffn_out_bias_added")
        s_ftx = sem("ffn_x_transposed")
        s_fxh = sem("ffn_x_hi")
        s_fxl = sem("ffn_x_lo")
        s_fu1 = sem("ffn_u1")
        s_fsh = sem("ffn_rank_hi")
        s_fsl = sem("ffn_rank_lo")
        s_fv1 = sem("ffn_v1")
        s_fge = sem("ffn_gelu")
        s_fhi = sem("ffn_h_hi")
        s_fhv = sem("ffn_h_hi_by_vector")
        s_flo = sem("ffn_h_lo")
        s_fu2 = sem("ffn_u2")
        s_fqh = sem("ffn_q_hi")
        s_fql = sem("ffn_q_lo")
        s_fv2 = sem("ffn_v2")
        s_fep = sem("ffn_residual")
        s_out = sem("out_written")
        pFX = banks[:, 0, :].rearrange("p (c n) -> p c n", c=C)

        def two_outputs(g, pair):
            bank = 2 if isinstance(g, int) and g == NG - 1 and pair == 1 else 0
            return banks[:, bank, :].rearrange("p (a d) -> p a d", a=2)
        Q_BANKS = (7, 5)
        out_t = out.rearrange("b (t p) d -> p (b t) d", p=P)

        def group_loop(eng, body):
            body(0, 0, False, True, True)
            body(1, 1, True, True, True)
            with eng.Fori(1, NG // 2 - 1) as i:
                for par in range(2):
                    body(2 * i + par, par, True, True, True)
            body(NG - 2, 0, True, True, False)
            body(NG - 1, 1, True, False, False)

        def two(g, pair):
            return x_res[:, bass.ds(g * GT + 2 * pair, 2), :]

        def transposed(g, f, nxt, nxt2, step):
            if nxt and f == TX1_AT:
                step(g + 1, 1)
            if nxt2 and f == TX0_AT:
                step(g + 2, 0)

        def ahead(g, f):
            return (g, f + LEAD) if f + LEAD < FC else (g + 1, f + LEAD - FC)

        def ffn_loads(sp):
            for k in range(2):
                rows = slice(k * R, (k + 1) * R)
                sp.dma_start(U1r[:, :, rows], a["L1_ffn_U1"].rearrange("(c p) r -> p c r", p=P)).then_inc(s_fl, 16)
                sp.dma_start(V1r[rows], a["L1_ffn_V1"]).then_inc(s_fl, 16)
                sp.dma_start(V2r[rows], a["L1_ffn_V2"]).then_inc(s_fl, 16)
            sp.dma_start(U2r, a["L1_ffn_U2"].rearrange("(f p) r -> p f r", p=P)).then_inc(s_fl, 16)
            sp.dma_start(fb1_rows[0:FC], a["L1_ffn_b1"].rearrange("(f p) -> f p", p=P)).then_inc(s_fl, 16)
            sp.dma_start(fbias, a["L1_ffn_b2"].rearrange("(a n) -> a n", a=1).to_broadcast([P, D])).then_inc(s_fl, 16)

        def low_rank_ffn():
            def sync(sp):
                with sp.Fori(0, NG) as g:
                    sp.wait_ge(s_fep, 2 * (g + 1))
                    sp.dma_start(out_t[:, bass.ds(g * GT, GT), :], x_res[:, bass.ds(g * GT, GT), :]).then_inc(s_out, 16)
                sp.wait_ge(s_out, 16 * NG)

            def gpsimd(pool):
                def reciprocal_roots(k, tiles, n):
                    pool.wait_ge(s_fag, tiles.stop)
                    nc.gpsimd.tensor_tensor(frs[:, 1, tiles], fmv[:, tiles, 1], eps.to_broadcast([P, n]),
                                            ALU.add).then_inc(s_frs, 1)
                    pool.wait_ge(s_frs, 2 * k + 1)
                    nc.gpsimd.tensor_tensor(frs[:, 0, tiles], frs[:, 1, tiles], minus_half.to_broadcast([P, n]),
                                            ALU.pow).then_inc(s_frs, 1)

                def group(g, k):
                    four = bass.ds(g * GT, GT)
                    x4 = x_res[:, four, :]
                    wait(pool, s_fxn, g)
                    pool.wait_ge(s_fag, T if k == 3 else GT * (k + 1))
                    nc.gpsimd.tensor_tensor(fct, x4, fmv[:, four, 0:1].to_broadcast([P, GT, D]),
                                            ALU.subtract).then_inc(s_fct, 1)
                    pool.wait_ge(s_fct, g + 1)
                    wait(pool, s_ftx, 2 * g)
                    pool.wait_ge(s_frs, 2 * k + 2)
                    nc.gpsimd.tensor_tensor(fxn, fct, frs[:, 0, four].unsqueeze(2).to_broadcast([P, GT, D]),
                                            ALU.mult).then_inc(s_fxn, 1)
                    pool.wait_ge(s_fwl, 5)
                    nc.gpsimd.tensor_tensor(x4, x4, fbias.unsqueeze(1).to_broadcast([P, GT, D]),
                                            ALU.add).then_inc(s_fba, 1)
                def start(g):
                    reciprocal_roots(g, slice(GT * g, GT * (g + 1)), GT)
                    group(g, g)

                def rest():
                    start(2)
                    reciprocal_roots(3, slice(3 * GT, T), T - 3 * GT)
                    with pool.Fori(3, NG) as g:
                        group(g, 3)
                return {T - 3: lambda: start(0), T - 1: lambda: start(1)}, rest

            def scalar(act):
                def weights():
                    act.wait_ge(s_fl, 9 * 16)
                    nc.scalar.activation(U1s[:, 0], U1r, ACT.Copy, scale=AS).then_inc(s_fw, 1)
                    nc.scalar.activation(V1s[:, 0], V1r, ACT.Copy, scale=AS).then_inc(s_fw, 1)
                    nc.scalar.activation(V2s[:, 0], V2r, ACT.Copy, scale=AS).then_inc(s_fw, 1)
                    nc.scalar.activation(U2s[:, :, 0:R], U2r, ACT.Copy, scale=AS).then_inc(s_fw, 1)

                def first_x():
                    act.wait_ge(s_fbt, 1)
                    nc.scalar.copy(fb1, banks[:, 0, 0:FC]).then_inc(s_fb, 1)
                    x_hi(0, 0)
                    x_hi(0, 1)

                def x_hi(g, pair):
                    act.wait_ge(s_ftx, 2 * g + pair + 1)
                    wait(act, s_fu1, g)
                    nc.scalar.copy(fxT[:, 0, :, pair * 2 * P:(pair + 1) * 2 * P], pFX).then_inc(s_fxh, 1)

                def rank_hi(g):
                    act.wait_ge(s_fu1, g + 1)
                    nc.scalar.copy(rank_s[:, bass.ds(g, 1), :].rearrange("p a n -> p (a n)"), banks[:, 2, :]).then_inc(s_fsh, 1)

                def gelu(g, f):
                    src = banks[:, V1_BANKS[f % 4], :]
                    act.wait_ge(s_fv1, FC * g + f + 1)
                    if f not in HI_ON_VECTOR:
                        wait(act, s_fu2, FC * (g - 1) + f + 1)
                        nc.scalar.activation(fhh[:, f, 0, :], src, ACT.Gelu_apprx_tanh, bias=fb1[:, f:f + 1],
                                             scale=1.0 / (AS * AS)).then_inc(s_fhi, 1)
                    wait(act, s_flo, FC * g + f - 3)
                    nc.scalar.activation(fh[:, f % 4, :], src, ACT.Gelu_apprx_tanh, bias=fb1[:, f:f + 1],
                                         scale=1.0 / (AS * AS)).then_inc(s_fge, 1)

                def body(g, par, prev, nxt, nxt2):
                    for f in range(FC):
                        if nxt or f + LEAD < FC:
                            gelu(*ahead(g, f))
                        transposed(g, f, nxt, nxt2, x_hi)
                        if nxt and f == U1_AT:
                            rank_hi(g + 1)

                def rest():
                    table_for(ACT.Gelu_apprx_tanh)
                    act.wait_ge(s_fb, 1)
                    for f in range(LEAD):
                        gelu(0, f)
                    x_hi(1, 0)
                    group_loop(act, body)
                return {T - 3: weights, T - 2: first_x, T: lambda: rank_hi(0)}, rest

            def vector(dve):
                def stats(g):
                    for t in range(GT * g, GT * (g + 1)):
                        nc.vector.bn_stats(fstats[:, t, :], x_res[:, t, :]).then_inc(s_fbn, 1)
                    dve.wait_ge(s_fbn, GT * (g + 1))
                    for t in range(GT * g, GT * (g + 1)):
                        nc.vector.bn_aggr(fmv[:, t, :], fstats[:, t, :]).then_inc(s_fag, 1)

                def x_lo(g, pair):
                    cols = slice(pair * 2 * P, (pair + 1) * 2 * P)
                    dve.wait_ge(s_fxh, 2 * g + pair + 1)
                    nc.vector.tensor_tensor(fxT[:, 1, :, cols], pFX, fxT[:, 0, :, cols], ALU.subtract).then_inc(s_fxl, 1)

                def rank_lo(g):
                    hi_rows = rank_s[R:R2, bass.ds(g, 1), :].rearrange("p a n -> p (a n)")
                    dve.wait_ge(s_fsh, g + 1)
                    nc.vector.tensor_tensor(hi_rows, banks[R:R2, 2, :], hi_rows, ALU.subtract).then_inc(s_fsl, 1)

                def h_lo(g, f):
                    dve.wait_ge(s_fge, FC * g + f + 1)
                    if f in HI_ON_VECTOR:
                        n = HI_ON_VECTOR.index(f)
                        wait(dve, s_fu2, FC * (g - 1) + f + 1)
                        nc.vector.tensor_copy(fhh[:, f, 0, :], fh[:, f % 4, :]).then_inc(s_fhv, 1)
                        dve.wait_ge(s_fhv, len(HI_ON_VECTOR) * g + (n + 1))
                    else:
                        n = len([c for c in range(f + 1) if c not in HI_ON_VECTOR])
                        dve.wait_ge(s_fhi, (FC - len(HI_ON_VECTOR)) * g + n)
                    nc.vector.tensor_tensor(fhh[:, f, 1, :], fh[:, f % 4, :], fhh[:, f, 0, :],
                                            ALU.subtract).then_inc(s_flo, 1)

                def q_split(g, par):
                    dve.wait_ge(s_fu2, FC * (g + 1))
                    wait(dve, s_fv2, 2 * g)
                    nc.vector.tensor_copy(fq[:, 0, :], banks[:, Q_BANKS[par], :]).then_inc(s_fqh, 1)
                    dve.wait_ge(s_fqh, g + 1)
                    nc.vector.tensor_tensor(fq[:, 1, :], banks[:, Q_BANKS[par], :], fq[:, 0, :], ALU.subtract).then_inc(s_fql, 1)

                def residual(g, pair):
                    dve.wait_ge(s_fv2, 2 * g + pair + 1)
                    dve.wait_ge(s_fba, g + 1)
                    nc.vector.scalar_tensor_tensor(out=two(g, pair), in0=two_outputs(g, pair), scalar=gscale[:, 3:4], in1=two(g, pair),
                                                   op0=ALU.mult, op1=ALU.add).then_inc(s_fep, 1)

                def body(g, par, prev, nxt, nxt2):
                    for f in range(FC):
                        if prev and f == Q_AT:
                            q_split(g - 1, 1 - par)
                        if nxt or f + LEAD < FC:
                            h_lo(*ahead(g, f))
                        transposed(g, f, nxt, nxt2, x_lo)
                        if nxt and f == U1_AT:
                            rank_lo(g + 1)
                        if prev and f in V2_AT:
                            residual(g - 1, V2_AT.index(f))
                        if not prev and f % 2 == 0:
                            stats(4 + f // 2)
                def weights():
                    dve.wait_ge(s_fw, 4)
                    for lo, r, hi in ((U1s[:, 1], U1r, U1s[:, 0]), (V1s[:, 1], V1r, V1s[:, 0]),
                                      (V2s[:, 1], V2r, V2s[:, 0]), (U2s[:, :, R:R2], U2r, U2s[:, :, 0:R])):
                        nc.vector.scalar_tensor_tensor(out=lo, in0=r, scalar=AS, in1=hi, op0=ALU.mult,
                                                       op1=ALU.subtract).then_inc(s_fwl, 1)
                    nc.vector.tensor_scalar(fbias, fbias, gtanh[:, 3:4], None, ALU.mult).then_inc(s_fwl, 1)

                def first_x():
                    stats(1)
                    x_lo(0, 0)
                    x_lo(0, 1)

                def first_rank():
                    stats(2)
                    rank_lo(0)

                def rest():
                    stats(3)
                    for f in range(LEAD):
                        h_lo(0, f)
                    x_lo(1, 0)
                    group_loop(dve, body)
                    q_split(NG - 1, 1)
                    for pair in range(2):
                        residual(NG - 1, pair)
                return {T - 4: lambda: stats(0), T - 3: weights, T - 2: first_x, T: first_rank}, rest

            def tensor(pe):
                def tx(g, pair):
                    pe.wait_ge(s_fxn, g + 1)
                    wait(pe, s_fxl, 2 * g + pair)
                    wait(pe, s_fep, 2 * (g - 2))
                    for j in range(2):
                        for c in range(C):
                            last = nc.tensor.transpose(pFX[:, c, j * P:(j + 1) * P],
                                                       fxn[:, 2 * pair + j, c * P:(c + 1) * P], ident[:])
                    last.then_inc(s_ftx, 1)

                def u1(g):
                    pe.wait_ge(s_fxl, 2 * (g + 1))
                    wait(pe, s_fsl, g)
                    n = 0
                    for pw, px in ((0, 0), (0, 1), (1, 0)):
                        for c in range(C):
                            last = nc.tensor.matmul(banks[:, 2, :], U1s[:, pw, c, :], fxT[:, px, c, :],
                                                    start=(n == 0), stop=(n == 3 * C - 1))
                            n += 1
                    last.then_inc(s_fu1, 1)

                def v1(g, f):
                    if f == 0:
                        pe.wait_ge(s_fsl, g + 1)
                    wait(pe, s_fge, FC * g + f - 3)
                    for part in range(2):
                        last = nc.tensor.matmul(banks[:, V1_BANKS[f % 4], :], V1s[:, part, f * P:(f + 1) * P],
                                                rank_s[:, bass.ds(g, 1), :].rearrange("p a n -> p (a n)"),
                                                start=(part == 0), stop=(part == 1))
                    last.then_inc(s_fv1, 1)

                def u2(g, par, f):
                    pe.wait_ge(s_flo, FC * g + f + 1)
                    if f == 0:
                        wait(pe, s_fql, g - 1)
                    for part in range(2):
                        last = nc.tensor.matmul(banks[:, Q_BANKS[par], :], U2s[:, f, :], fhh[:, f, part, :],
                                                start=(f == 0 and part == 0), stop=(f == FC - 1 and part == 1))
                    last.then_inc(s_fu2, 1)

                def v2(g, pair, transposed_pairs=2 * NG):
                    pe.wait_ge(s_fql, g + 1)
                    if isinstance(g, int) and g == NG - 1 and pair == 1:
                        pe.wait_ge(s_fsl, NG)
                    else:
                        wait(pe, s_fep, 2 * g + pair)
                        wait(pe, s_fxl, transposed_pairs)
                    for j in range(2):
                        at = (2 * pair + j) * P
                        for n, (pq, pw) in enumerate(((0, 0), (1, 0), (0, 1))):
                            last = nc.tensor.matmul(two_outputs(g, pair)[:, j, :], fq[:, pq, at:at + P],
                                                    V2s[:, pw, :], start=(n == 0), stop=(n == 2))
                    last.then_inc(s_fv2, 1)

                def body(g, par, prev, nxt, nxt2):
                    for f in range(FC):
                        if nxt or f + LEAD < FC:
                            v1(*ahead(g, f))
                        transposed(g, f, nxt, nxt2, tx)
                        if nxt and f == U1_AT:
                            u1(g + 1)
                        if prev and f in V2_AT:
                            v2(g - 1, V2_AT.index(f), 2 * (g + 2) if nxt else 2 * NG)
                        u2(g, par, f)
                def first_x():
                    pe.wait_ge(s_fl, 9 * 16)
                    pe.wait_ge(attention1["xlo_done"], T)
                    nc.tensor.transpose(banks[:, 0, 0:FC], fb1_rows[0:FC, :], ident[0:FC, 0:FC]).then_inc(s_fbt, 1)
                    pe.wait_ge(s_fb, 1)
                    tx(0, 0)
                    tx(0, 1)

                def first_rank():
                    pe.wait_ge(s_fwl, 4)
                    pe.wait_ge(attention1["exp_done"], H * T)
                    u1(0)

                def rest():
                    pe.wait_ge(attention1["plo_done"], T)
                    pe.wait_ge(attention1["epi_done"], T)
                    for f in range(LEAD):
                        v1(0, f)
                    tx(1, 0)
                    group_loop(pe, body)
                    for pair in range(2):
                        v2(NG - 1, pair)
                return {T - 2: first_x, T - 1: first_rank}, rest

            return sync, gpsimd, scalar, tensor, vector

        attention("xattn0", setup(), pieces0, lambda part, b, c: G0[:, part, b, c, :], 0,
                  1.0 / (HD0 ** 0.5 * AS), eps, False, False)
        gating()
        experts()
        pieces1 = [(bank, 0, n * SK, tuple(range(C)), h0 * SK) 
                   for bank, (h0, n) in enumerate(zip(HEADS_UP_TO, HEADS_OF_BANK))]
        attention("xattn1", fold_layer1(), pieces1, lambda part, b, c: G1[:, part, b, c, :], 2,
                  1.0 / (HD1 ** 0.5 * AS), eps2, True, True, low_rank_ffn())


_NAMES = ["x", "ctx_1024", "g_xattn", "g_ffn", "L0_xattn_W_kv", "L0_xattn_b_kv", "L0_xattn_W_o", "L0_xattn_b_o",
          "L0_ffn_Wg", "L0_ffn_bg", "L0_ffn_W1", "L0_ffn_b1", "L0_ffn_W2", "L0_ffn_b2", "L1_xattn_ln_gamma",
          "L1_xattn_ln_beta", "L1_xattn_w_q", "L1_xattn_w_kv", "L1_xattn_w_out", "L1_xattn_b_out", "L1_xattn_gate",
          "L1_ffn_U1", "L1_ffn_V1", "L1_ffn_b1", "L1_ffn_U2", "L1_ffn_V2", "L1_ffn_b2"]


def kernel(**inputs):
    import numpy as _np
    import concourse.bacc as _bacc
    from concourse import mybir as _mybir
    from concourse.bass_utils import run_bass_kernel_spmd as _run

    nc = _bacc.Bacc("TRN2", target_bir_lowering=False, num_devices=1)
    arrays, aps = {}, {}
    for name in _NAMES:
        v = _np.ascontiguousarray(inputs[name])
        arrays[f"in_{name}"] = v
        aps[name] = nc.dram_tensor(f"in_{name}", v.shape, _mybir.dt.from_np(v.dtype), kind="ExternalInput").ap()
    out = nc.dram_tensor("out", inputs["x"].shape, _mybir.dt.float32, kind="ExternalOutput").ap()
    flamingo_kernel(nc, aps, out)
    r = _run(nc, [arrays], core_ids=[0])
    return r.results[0]["out"]
```
